# Optimizing a Trainium2 kernel written in Bass

```python
import numpy as np
import jax
import jax.numpy as jnp

def _softmax(x, axis=-1):
    return jax.nn.softmax(x, axis=axis)

def _gelu(x):
    return jax.nn.gelu(x, approximate=True)

def _silu(x):
    return jax.nn.silu(x)

def _sigmoid(x):
    return jax.nn.sigmoid(x)

def _layernorm(x, axis=-1, eps=1e-05):
    m = jnp.mean(x, axis=axis, keepdims=True)
    v = jnp.var(x, axis=axis, keepdims=True)
    return (x - m) / jnp.sqrt(v + eps)

def _scatter_add(tgt, idx, src, axis=0):
    return tgt.at[idx].add(src)

def _segment_sum(src, seg, n):
    return jax.ops.segment_sum(src, seg, n)
kernel_name = 'mk_macaron_d1_jaxref_r8_4f28b4'

def setup_inputs(seed: int=0):
    np.random.seed(seed)
    _w = jnp.asarray

    def _L0_attn_setup():
        import jax, jax.numpy as jnp
        import numpy as np
        D_MODEL = 512
        N_HEADS = 32
        HEAD_DIM = D_MODEL // N_HEADS
        CLIP_QKV = 8.0
        ALIBI_BIAS_MAX = 8.0
        LN_EPS = 1e-05

        def _alibi_slopes(n_heads: int, bias_max: float) -> jnp.ndarray:
            next_pow2 = 2 ** int(np.ceil(np.log2(n_heads)))
            m = np.arange(1, next_pow2 + 1, dtype=np.float32) * (bias_max / next_pow2)
            slopes = 1.0 / np.power(2.0, m)
            if next_pow2 != n_heads:
                slopes = np.concatenate([slopes[1::2], slopes[::2]])[:n_heads]
            return jnp.asarray(slopes)

        def _layer_norm(x, w, b):
            mu = jnp.mean(x, axis=-1, keepdims=True)
            var = jnp.mean(jnp.square(x - mu), axis=-1, keepdims=True)
            return (x - mu) * jax.lax.rsqrt(var + LN_EPS) * w + b
        key = jax.random.key(seed)
        ks = jax.random.split(key, 3)
        B, S = (1, 256)
        hidden_states = jax.random.normal(ks[0], (B, S, D_MODEL), dtype=jnp.float32)
        Wqkv = jax.random.normal(ks[1], (3 * D_MODEL, D_MODEL), dtype=jnp.float32) * 0.02
        Wout = jax.random.normal(ks[2], (D_MODEL, D_MODEL), dtype=jnp.float32) * 0.02
        return {'hidden_states': hidden_states, 'Wqkv': Wqkv, 'q_ln_w': jnp.ones((D_MODEL,), jnp.float32), 'q_ln_b': jnp.zeros((D_MODEL,), jnp.float32), 'k_ln_w': jnp.ones((D_MODEL,), jnp.float32), 'k_ln_b': jnp.zeros((D_MODEL,), jnp.float32), 'Wout': Wout}
    _L0_attn_in = _L0_attn_setup()

    def _L0_ffn_setup():
        import jax, jax.numpy as jnp
        import numpy as np
        TOP_K = 2
        key = jax.random.key(seed)
        k0, k1, k2 = jax.random.split(key, 3)
        B, S, D, H, E = (4, 256, 512, 512, 8)
        sc = 1.0 / np.sqrt(D).astype(np.float32)
        x = jax.random.normal(k0, (B, S, D), dtype=jnp.float32)
        W_gate = jax.random.normal(k1, (D, E), dtype=jnp.float32) * sc
        b_gate = jnp.zeros((E,), dtype=jnp.float32)
        W_e = jax.random.normal(k2, (E, D, H), dtype=jnp.float32) * sc
        b_e = jnp.zeros((E, H), dtype=jnp.float32)
        return {'x': x, 'W_gate': W_gate, 'b_gate': b_gate, 'W_e': W_e, 'b_e': b_e}
    _L0_ffn_in = _L0_ffn_setup()
    _d = {'L0_attn_hidden_states': _L0_attn_in['hidden_states'], 'L0_attn_Wqkv': _L0_attn_in['Wqkv'], 'L0_attn_q_ln_w': _L0_attn_in['q_ln_w'], 'L0_attn_q_ln_b': _L0_attn_in['q_ln_b'], 'L0_attn_k_ln_w': _L0_attn_in['k_ln_w'], 'L0_attn_k_ln_b': _L0_attn_in['k_ln_b'], 'L0_attn_Wout': _L0_attn_in['Wout'], 'L0_ffn_W_gate': _L0_ffn_in['W_gate'], 'L0_ffn_b_gate': _L0_ffn_in['b_gate'], 'L0_ffn_W_e': _L0_ffn_in['W_e'], 'L0_ffn_b_e': _L0_ffn_in['b_e']}
    _x0 = _d['L0_attn_hidden_states']
    _d['L0_attn_hidden_states'] = jax.random.normal(jax.random.fold_in(jax.random.key(seed), 1), (4, 512, 512), dtype=_x0.dtype)
    del _x0
    return _d

def reference(L0_attn_hidden_states, L0_attn_Wqkv, L0_attn_q_ln_w, L0_attn_q_ln_b, L0_attn_k_ln_w, L0_attn_k_ln_b, L0_attn_Wout, L0_ffn_W_gate, L0_ffn_b_gate, L0_ffn_W_e, L0_ffn_b_e):

    def _L0_attn_ref(hidden_states, Wqkv, q_ln_w, q_ln_b, k_ln_w, k_ln_b, Wout):
        import jax, jax.numpy as jnp
        import numpy as np
        D_MODEL = 512
        N_HEADS = 32
        HEAD_DIM = D_MODEL // N_HEADS
        CLIP_QKV = 8.0
        ALIBI_BIAS_MAX = 8.0
        LN_EPS = 1e-05

        def _alibi_slopes(n_heads: int, bias_max: float) -> jnp.ndarray:
            next_pow2 = 2 ** int(np.ceil(np.log2(n_heads)))
            m = np.arange(1, next_pow2 + 1, dtype=np.float32) * (bias_max / next_pow2)
            slopes = 1.0 / np.power(2.0, m)
            if next_pow2 != n_heads:
                slopes = np.concatenate([slopes[1::2], slopes[::2]])[:n_heads]
            return jnp.asarray(slopes)

        def _layer_norm(x, w, b):
            mu = jnp.mean(x, axis=-1, keepdims=True)
            var = jnp.mean(jnp.square(x - mu), axis=-1, keepdims=True)
            return (x - mu) * jax.lax.rsqrt(var + LN_EPS) * w + b
        B, S, _ = hidden_states.shape
        qkv = jnp.einsum('bsd,ed->bse', hidden_states, Wqkv)
        qkv = jnp.clip(qkv, -CLIP_QKV, CLIP_QKV)
        q, k, v = jnp.split(qkv, [D_MODEL, 2 * D_MODEL], axis=-1)
        q = _layer_norm(q, q_ln_w, q_ln_b)
        k = _layer_norm(k, k_ln_w, k_ln_b)
        q = q.reshape(B, S, N_HEADS, HEAD_DIM)
        k = k.reshape(B, S, N_HEADS, HEAD_DIM)
        v = v.reshape(B, S, N_HEADS, HEAD_DIM)
        scale = HEAD_DIM ** (-0.5)
        scores = jnp.einsum('bqhd,bkhd->bhqk', q, k) * scale
        slopes = _alibi_slopes(N_HEADS, ALIBI_BIAS_MAX)
        pos = jnp.arange(S)
        rel = (pos[None, :] - pos[:, None]).astype(jnp.float32)
        scores = scores + slopes[None, :, None, None] * rel[None, None]
        causal = pos[None, :] <= pos[:, None]
        scores = jnp.where(causal[None, None], scores, jnp.float32(-1e+30))
        probs = jax.nn.softmax(scores, axis=-1)
        out = jnp.einsum('bhqk,bkhd->bqhd', probs, v).reshape(B, S, D_MODEL)
        return jnp.einsum('bsd,ed->bse', out, Wout)

    def _L0_ffn_ref(x, W_gate, b_gate, W_e, b_e):
        import jax, jax.numpy as jnp
        import numpy as np
        TOP_K = 2
        logits = x @ W_gate + b_gate
        _, top_idx = jax.lax.top_k(logits, TOP_K)
        y_all = jax.nn.relu(jnp.einsum('bsd,edh->bseh', x, W_e) + b_e)
        y = jnp.take_along_axis(y_all, top_idx[..., None], axis=2)
        return y.mean(axis=2)
    x = L0_attn_hidden_states
    x = x + 0.5 * _L0_ffn_ref(_layernorm(x, axis=-1), L0_ffn_W_gate, L0_ffn_b_gate, L0_ffn_W_e, L0_ffn_b_e)
    x = x + _L0_attn_ref(_layernorm(x, axis=-1), L0_attn_Wqkv, L0_attn_q_ln_w, L0_attn_q_ln_b, L0_attn_k_ln_w, L0_attn_k_ln_b, L0_attn_Wout)
    x = x + 0.5 * _L0_ffn_ref(_layernorm(x, axis=-1), L0_ffn_W_gate, L0_ffn_b_gate, L0_ffn_W_e, L0_ffn_b_e)
    return x

_drawn_inputs = setup_inputs


def setup_inputs(seed=0):
    import zlib

    import numpy as np

    out = dict(_drawn_inputs(seed))
    spreads = {'L0_attn_q_ln_w': (1.0, 0.596),
     'L0_attn_q_ln_b': (0.0, 0.396),
     'L0_attn_k_ln_w': (1.0, 0.553),
     'L0_attn_k_ln_b': (0.0, 0.8),
     'L0_ffn_b_gate': (0.0, 0.1),
     'L0_ffn_b_e': (0.0, 0.1)}
    factors = {}
    for name, (base, spread) in spreads.items():
        noise = np.random.default_rng([zlib.crc32(name.encode()), seed]).standard_normal(out[name].shape)
        drawn = base * np.exp(spread * noise) if base else spread * noise
        out[name] = jnp.asarray(drawn.astype(out[name].dtype))
    for name, factor in factors.items():
        out[name] = (out[name] * factor).astype(out[name].dtype)
    return out
```

```python
import concourse.bass as bass
from concourse import mybir
from contextlib import ExitStack

F32 = mybir.dt.float32
F32R = mybir.dt.float32r
BF16 = mybir.dt.bfloat16
I32 = mybir.dt.int32
U32 = mybir.dt.uint32
ALU = mybir.AluOpType
ACT = mybir.ActivationFunctionType
X_AXIS = mybir.AxisListType.X

P = 128
D = 512
B, SEQ = 4, 512
TOKENS = B * SEQ
TILES = TOKENS // P
QT = SEQ // P
C = D // P
E = 8
H = 32
HD = D // H
HG = 4
NG = B * H // HG
VW = 32
CLIP = 8.0
EPS = 1e-5
NEG = -1e30
STACK = 4 * HD
BIAS_ROWS = 4
MAX_ROWS = 2


def at_least(engine, sem, value):
    if isinstance(value, int) and value <= 0:
        return
    engine.wait_ge(sem, value)


class Chain:

    def __init__(self, engine, sem, base=0, passed=None):
        self.engine, self.sem, self.base, self.n, self.passed = engine, sem, base, 0, passed

    def __call__(self, instruction, apart=False):
        self.n += 1
        instruction.then_inc(self.sem, 1)
        self.engine.wait_ge(self.sem, self.base + self.n)
        if apart and not isinstance(self.base, int):
            self.engine.sem_inc(self.passed, 1)


def tile_loop(engine, step, first=2, last=TILES - 2):
    for t in range(first):
        step(t, t % 2)
    with engine.Fori(first // 2, last // 2) as i:
        for par in range(2):
            step(2 * i + par, par)
    for t in range(last, TILES):
        step(t, t % 2)


def rsqrt_steps(nc, chain, var, y, tmp):
    chain(nc.vector.tensor_scalar(tmp[1], var, EPS, None, ALU.add))
    chain(nc.vector.tensor_scalar(y.bitcast(I32), tmp[1].bitcast(I32), -0.5, 1597463007.0, ALU.mult, ALU.add))
    for _ in range(3):
        chain(nc.vector.tensor_tensor(tmp[0], y, y, ALU.mult))
        chain(nc.vector.scalar_tensor_tensor(tmp[0], tmp[0], -0.5, tmp[1], ALU.mult, ALU.mult))
        chain(nc.vector.scalar_tensor_tensor(y, tmp[0], 1.5, y, ALU.add, ALU.mult))


RSQRT_LINKS = 11


def layernorm_steps(nc, chain, x, out, ln):
    chain(nc.vector.bn_stats(ln["stats"], x), apart=True)
    chain(nc.vector.bn_aggr(ln["mv"], ln["stats"]))
    rsqrt_steps(nc, chain, ln["mv"][:, 1:2], ln["rstd"], (ln["t0"], ln["t1"]))
    return nc.vector.tensor_scalar(out, x, ln["mv"][:, 0:1], ln["rstd"], ALU.subtract, ALU.mult)


LN_LINKS = 2 + RSQRT_LINKS


class Memory:

    def __init__(self, nc, ctx, prefix):
        self.nc, self.ctx, self.prefix = nc, ctx, prefix

    def sb(self, name, shape, dt=F32):
        return self.ctx.enter_context(self.nc.sbuf_tensor(f"{self.prefix}_{name}", shape, dt))

    def ps(self, name, width=512):
        return self.ctx.enter_context(self.nc.psum_tensor(f"{self.prefix}_{name}", [P, width], F32))

    def sem(self, name):
        return self.ctx.enter_context(self.nc.semaphore(f"{self.prefix}_{name}"))

    def ln(self):
        return {"stats": self.sb("ln_stats", [P, 6])[:, :], "mv": self.sb("ln_mv", [P, 2])[:, :],
                "rstd": self.sb("ln_rstd", [P, 1])[:, :], "t0": self.sb("ln_t0", [P, 1])[:, :],
                "t1": self.sb("ln_t1", [P, 1])[:, :]}


def rows(dram, t, n=P):
    return dram[bass.ds(t * n, n), :]


def ffn_block(nc, prefix, x_in, x_out, w_gate, b_gate, w_e, b_e):
    with ExitStack() as ctx:
        m = Memory(nc, ctx, prefix)
        w_hi = m.sb("w_hi", [P, E * C, D], F32R)
        w_lo = m.sb("w_lo", [P, E * C, D], F32R)
        w_stage = [m.sb(f"w_stage{i}", [P, C, D]) for i in range(2)]
        g_raw = m.sb("g_raw", [P, C, E])
        g_hi = m.sb("g_hi", [P, C, E], F32R)
        g_lo = m.sb("g_lo", [P, C, E], F32R)
        be_bc = m.sb("be_bc", [P, E * D])
        bg_bc = m.sb("bg_bc", [P, E])
        iota = m.sb("iota", [P, E])
        ident = m.sb("ident", [P, P])
        x = [m.sb(f"x{i}", [P, D]) for i in range(2)]
        xn = [m.sb(f"xn{i}", [P, D]) for i in range(2)]
        xT_hi = [m.sb(f"xT_hi{i}", [P, C * P], F32R) for i in range(2)]
        xT_lo = [m.sb(f"xT_lo{i}", [P, C * P], F32R) for i in range(2)]
        acc = [m.sb(f"acc{i}", [P, D]) for i in range(2)]
        z = [m.sb(f"z{i}", [P, D]) for i in range(2)]
        r = [m.sb(f"r{i}", [P, D]) for i in range(2)]
        logits = m.sb("logits", [P, E])
        top = m.sb("top", [P, 8])
        top_idx = m.sb("top_idx", [P, 8], U32)
        top_idf = m.sb("top_idf", [P, 8])
        pick = m.sb("pick", [P, E])
        coef = [m.sb(f"coef{i}", [P, E]) for i in range(2)]
        ln = m.ln()
        z_ps = [m.ps(f"z_ps{i}") for i in range(4)]
        t_ps = [m.ps(f"t_ps{i}") for i in range(2)]
        g_ps = m.ps("g_ps")

        w_loaded = [m.sem(f"w_loaded{i}") for i in range(2)]
        g_loaded, bias_loaded = m.sem("g_loaded"), m.sem("bias_loaded")
        w_hi_done, w_lo_done, g_done = m.sem("w_hi_done"), m.sem("w_lo_done"), m.sem("g_done")
        ident_done, iota_done = m.sem("ident_done"), m.sem("iota_done")
        x_loaded = [m.sem(f"x_loaded{i}") for i in range(2)]
        stored = [m.sem(f"stored{i}") for i in range(2)]
        xn_done, tr_done = m.sem("xn_done"), m.sem("tr_done")
        hi_done, lo_done = m.sem("hi_done"), m.sem("lo_done")
        gate_done, coef_done = m.sem("gate_done"), m.sem("coef_done")
        z_done, zb_done = m.sem("z_done"), m.sem("zb_done")
        r_done, acc_done = m.sem("r_done"), m.sem("acc_done")
        ln_chain, gate_chain, passed = m.sem("ln_chain"), m.sem("gate_chain"), m.sem("passed")

        block = ctx.enter_context(nc.Block())

        @block.sync
        def _(sp):
            sp.dma_start(x[0][:, :], rows(x_in, 0)).then_inc(x_loaded[0], 16)
            sp.dma_start(g_raw[:, :, :], w_gate.rearrange("(c p) e -> p c e", p=P)).then_inc(g_loaded, 16)
            sp.dma_start(bg_bc[:, :], b_gate.rearrange("(a e) -> a e", a=1).to_broadcast([P, E])).then_inc(bias_loaded, 16)
            sp.dma_start(be_bc[:, :], b_e.rearrange("(a e) h -> a (e h)", a=1).to_broadcast([P, E * D])).then_inc(bias_loaded, 16)
            for e in range(E):
                if e >= 2:
                    sp.wait_ge(w_lo_done, e - 1)
                sp.dma_start(w_stage[e % 2][:, :, :], w_e[e].rearrange("(c p) h -> p c h", p=P)).then_inc(w_loaded[e % 2], 16)
                if e == 0:
                    sp.dma_start(x[1][:, :], rows(x_in, 1)).then_inc(x_loaded[1], 16)

            def step(t, par):
                if not (isinstance(t, int) and t + 2 >= TILES):
                    sp.wait_ge(acc_done, E * t + 1)
                    sp.dma_start(x[par][:, :], rows(x_in, t + 2)).then_inc(x_loaded[par], 16)
                sp.wait_ge(acc_done, E * (t + 1))
                sp.dma_start(rows(x_out, t), acc[par][:, :]).then_inc(stored[par], 16)
            tile_loop(sp, step)
            for par in range(2):
                sp.wait_ge(stored[par], 16 * (TILES // 2))

        @block.gpsimd
        def _(pool):
            nc.gpsimd.memset(ident[:, :], 0.0).then_inc(iota_done, 1)
            nc.gpsimd.iota(iota[:, :], [[1, E]], base=0, channel_multiplier=0,
                           allow_small_or_imprecise_dtypes=True).then_inc(iota_done, 1)
            pool.wait_ge(iota_done, 2)
            nc.gpsimd.affine_select(out=ident[:, :], in_=ident[:, :], compare_op=ALU.not_equal, fill=1.0, base=0,
                                    pattern=[[-1, P]], channel_multiplier=1).then_inc(ident_done, 1)

            def step(t, par):
                for e in range(E):
                    n = E * t + e
                    pool.wait_ge(r_done, n + 1)
                    if e == 0:
                        at_least(pool, stored[par], 16 * (t // 2))
                        at_least(pool, x_loaded[par], 16 * (t // 2 + 1))
                    else:
                        pool.wait_ge(acc_done, n)
                    nc.gpsimd.tensor_tensor(acc[par][:, :], (x if e == 0 else acc)[par][:, :], r[e % 2][:, :],
                                            ALU.add).then_inc(acc_done, 1)
            tile_loop(pool, step)

        def front(t):
            return not (isinstance(t, int) and t + 1 >= TILES)

        @block.tensor
        def _(pe):
            def transpose(t, par):
                pe.wait_ge(xn_done, t + 1)
                at_least(pe, lo_done, t - 1)
                for c in range(C):
                    last = nc.tensor.transpose(t_ps[par][:, c * P:(c + 1) * P], xn[par][:, c * P:(c + 1) * P], ident[:, :])
                last.then_inc(tr_done, 1)

            def gate(t, par):
                pe.wait_ge(lo_done, t + 1)
                at_least(pe, coef_done, t)
                last = split_matmuls(nc, g_ps[:, 0:E], xT_hi[par], xT_lo[par], lambda c: g_hi[:, c, :],
                                     lambda c: g_lo[:, c, :])
                last.then_inc(gate_done, 1)

            def expert(t, par, e):
                at_least(pe, zb_done, E * t + e - 3)
                if isinstance(t, int) and t == 0:
                    pe.wait_ge(w_lo_done, e + 1)
                last = split_matmuls(nc, z_ps[e % 4][:, :], xT_hi[par], xT_lo[par], lambda c: w_hi[:, e * C + c, :],
                                     lambda c: w_lo[:, e * C + c, :])
                last.then_inc(z_done, 1)

            pe.wait_ge(ident_done, 1)
            transpose(0, 0)
            pe.wait_ge(g_done, 2)
            gate(0, 0)

            def step(t, par):
                for e in range(E):
                    if e == 2 and front(t):
                        transpose(t + 1, 1 - par)
                    if e == 6 and front(t):
                        gate(t + 1, 1 - par)
                    expert(t, par, e)
            tile_loop(pe, step)

        @block.scalar
        def _(act):
            act.wait_ge(g_loaded, 16)
            nc.scalar.activation(g_hi[:, :, :], g_raw[:, :, :], ACT.Copy).then_inc(g_done, 1)

            def hi(t, par):
                act.wait_ge(tr_done, t + 1)
                at_least(act, z_done, E * (t - 1))
                nc.scalar.activation(xT_hi[par][:, :], t_ps[par][:, :], ACT.Copy).then_inc(hi_done, 1)

            hi(0, 0)
            for e in range(E):
                act.wait_ge(w_loaded[e % 2], 16 * (e // 2 + 1))
                nc.scalar.activation(w_hi[:, e * C:(e + 1) * C, :], w_stage[e % 2][:, :, :], ACT.Copy).then_inc(w_hi_done, 1)

            def step(t, par):
                for e in range(E):
                    if e == 2 and front(t):
                        hi(t + 1, 1 - par)
                    n = E * t + e
                    act.wait_ge(zb_done, n + 1)
                    if e == 0:
                        act.wait_ge(coef_done, t + 1)
                    at_least(act, acc_done, n - 1)
                    nc.scalar.activation(r[e % 2][:, :], z[e % 2][:, :], ACT.Relu,
                                         scale=coef[par][:, e:e + 1]).then_inc(r_done, 1)
            tile_loop(act, step)

        GATE_LINKS = 7

        @block.vector
        def _(dve):
            def norm(t, par):
                dve.wait_ge(x_loaded[par], 16 * (t // 2 + 1))
                at_least(dve, tr_done, t - 1)
                chain = Chain(dve, ln_chain, LN_LINKS * t, passed)
                layernorm_steps(nc, chain, x[par][:, :], xn[par][:, :], ln).then_inc(xn_done, 1)
                assert chain.n == LN_LINKS

            def lo(t, par):
                dve.wait_ge(hi_done, t + 1)
                nc.vector.tensor_tensor(xT_lo[par][:, :], t_ps[par][:, :], xT_hi[par][:, :].bitcast(F32),
                                        ALU.subtract).then_inc(lo_done, 1)

            def choose(t, par):
                dve.wait_ge(gate_done, t + 1)
                chain = Chain(dve, gate_chain, GATE_LINKS * t, passed)
                chain(nc.vector.tensor_tensor(logits[:, :], g_ps[:, 0:E], bg_bc[:, :], ALU.add), apart=True)
                chain(nc.vector.max(top[:, :], logits[:, :]), apart=True)
                chain(nc.vector.max_index(top_idx[:, :], top[:, :], logits[:, :]))
                chain(nc.vector.tensor_copy(top_idf[:, :], top_idx[:, :]))
                chain(nc.vector.tensor_scalar(pick[:, :], iota[:, :], top_idf[:, 0:1], None, ALU.is_equal))
                chain(nc.vector.scalar_tensor_tensor(pick[:, :], iota[:, :], top_idf[:, 1:2], pick[:, :],
                                                     ALU.is_equal, ALU.add))
                at_least(dve, r_done, E * (t - 1))
                chain(nc.vector.tensor_scalar(coef[par][:, :], pick[:, :], 0.25, None, ALU.mult))
                nc.vector.tensor_copy(logits[:, 0:1], coef[par][:, 0:1]).then_inc(coef_done, 1)
                assert chain.n == GATE_LINKS

            norm(0, 0)
            dve.wait_ge(g_done, 1)
            nc.vector.tensor_tensor(g_lo[:, :, :], g_raw[:, :, :], g_hi[:, :, :].bitcast(F32), ALU.subtract).then_inc(g_done, 1)
            lo(0, 0)
            dve.wait_ge(bias_loaded, 32)
            dve.wait_ge(iota_done, 2)
            choose(0, 0)
            for e in range(E):
                dve.wait_ge(w_hi_done, e + 1)
                nc.vector.tensor_tensor(w_lo[:, e * C:(e + 1) * C, :], w_stage[e % 2][:, :, :],
                                        w_hi[:, e * C:(e + 1) * C, :].bitcast(F32), ALU.subtract).then_inc(w_lo_done, 1)

            def step(t, par):
                if front(t):
                    norm(t + 1, 1 - par)
                for e in range(E):
                    if e == 2 and front(t):
                        lo(t + 1, 1 - par)
                    if e == 6 and front(t):
                        choose(t + 1, 1 - par)
                    n = E * t + e
                    dve.wait_ge(z_done, n + 1)
                    at_least(dve, r_done, n - 1)
                    nc.vector.tensor_tensor(z[e % 2][:, :], z_ps[e % 4][:, :], be_bc[:, e * D:(e + 1) * D],
                                            ALU.add).then_inc(zb_done, 1)
            tile_loop(dve, step)


def split_matmuls(nc, out, x_hi, x_lo, w_hi, w_lo):
    for c in range(C):
        s = slice(c * P, (c + 1) * P)
        nc.tensor.matmul(out, x_hi[:, s], w_hi(c), start=(c == 0), stop=False)
        nc.tensor.matmul(out, x_hi[:, s], w_lo(c), start=False, stop=False)
        last = nc.tensor.matmul(out, x_lo[:, s], w_hi(c), start=False, stop=(c == C - 1))
    return last


def load_transposed_weight(nc, m, w, n_tiles, w_hi, w_lo, ident, ident_done, t_ps):
    stage = [m.sb(f"wst{i}", [P, D]) for i in range(2)]
    loaded = [m.sem(f"wst_loaded{i}") for i in range(2)]
    tr, hi, lo = m.sem("w_tr"), m.sem("w_hi_done"), m.sem("w_lo_done")

    def cols(w_t, t):
        return w_t[:, :, bass.ds(t * P, P)]

    def pairs(engine, step):
        for t in range(2):
            step(t, t)
        if n_tiles > 2:
            with engine.Fori(1, n_tiles // 2) as i:
                for par in range(2):
                    step(2 * i + par, par)

    def sync(sp):
        def step(t, par):
            at_least(sp, tr, t - 1)
            sp.dma_start(stage[par][:, :], rows(w, t)).then_inc(loaded[par], 16)
        pairs(sp, step)

    def tensor(pe):
        pe.wait_ge(ident_done, 1)

        def step(t, par):
            pe.wait_ge(loaded[par], 16 * (t // 2 + 1))
            at_least(pe, lo, t - 1)
            for c in range(C):
                last = nc.tensor.transpose(t_ps[par][:, c * P:(c + 1) * P], stage[par][:, c * P:(c + 1) * P], ident[:, :])
            last.then_inc(tr, 1)
        pairs(pe, step)

    def bank(par):
        return t_ps[par][:, :].rearrange("p (c n) -> p c n", c=C)

    def scalar(act):
        def step(t, par):
            act.wait_ge(tr, t + 1)
            nc.scalar.activation(cols(w_hi, t), bank(par), ACT.Copy).then_inc(hi, 1)
        pairs(act, step)

    def vector(dve):
        def step(t, par):
            dve.wait_ge(hi, t + 1)
            nc.vector.tensor_tensor(cols(w_lo, t), bank(par), cols(w_hi, t).bitcast(F32), ALU.subtract).then_inc(lo, 1)
        pairs(dve, step)

    return {"sync": sync, "tensor": tensor, "scalar": scalar, "vector": vector, "done": (lo, n_tiles)}


def make_identity(nc, pool, ident, zeroed, done):
    nc.gpsimd.memset(ident[:, :], 0.0).then_inc(zeroed, 1)
    pool.wait_ge(zeroed, 1)
    nc.gpsimd.affine_select(out=ident[:, :], in_=ident[:, :], compare_op=ALU.not_equal, fill=1.0, base=0,
                            pattern=[[-1, P]], channel_multiplier=1).then_inc(done, 1)


def qkv_block(nc, x1, w_qkv, ln_params, bias_const, q_dram, k_dram, v_dram, bias_dram):
    with ExitStack() as ctx:
        m = Memory(nc, ctx, "qkv")
        w_hi = m.sb("w_hi", [P, C, 3 * D], F32R)
        w_lo = m.sb("w_lo", [P, C, 3 * D], F32R)
        ident = m.sb("ident", [P, P])
        lnp = [m.sb(f"lnp{i}", [P, D]) for i in range(4)]
        x = [m.sb(f"x{i}", [P, D]) for i in range(2)]
        xn = [m.sb(f"xn{i}", [P, D]) for i in range(2)]
        xT_hi = [m.sb(f"xT_hi{i}", [P, C * P], F32R) for i in range(2)]
        xT_lo = [m.sb(f"xT_lo{i}", [P, C * P], F32R) for i in range(2)]
        clipped = [[m.sb(f"clip{s}{i}", [P, D]) for i in range(2)] for s in "qk"]
        normed = [[m.sb(f"norm{s}{i}", [P, D]) for i in range(2)] for s in "qk"]
        parts = [[m.sb(f"parts{s}{i}", [P, H, 2, HD], F32R) for i in range(2)] for s in "qk"]
        turned = [[m.sb(f"turned{s}{i}", [P, 8, P], F32R) for i in range(2)] for s in "qk"]
        vals = [m.sb(f"vals{i}", [P, H, VW]) for i in range(2)]
        ln = m.ln()
        qk_stats = m.sb("qk_stats", [P, 2, 6])
        qk_mv = m.sb("qk_mv", [P, 2, 2])
        qk_rstd, qk_t0, qk_t1, qk_var = (m.sb(n, [P, 2]) for n in ("qk_rstd", "qk_t0", "qk_t1", "qk_var"))
        o_ps = [m.ps(f"o_ps{i}") for i in range(3)]
        t_ps = [m.ps(f"t_ps{i}") for i in range(2)]
        s_ps = [m.ps(f"s_ps{i}") for i in range(2)]

        x_loaded = [m.sem(f"x_loaded{i}") for i in range(2)]
        lnp_loaded, bias_copied = m.sem("lnp_loaded"), m.sem("bias_copied")
        zeroed, ident_done, vals_set = m.sem("zeroed"), m.sem("ident_done"), m.sem("vals_set")
        scaled = m.sem("scaled")
        xn_done, tr_done = m.sem("xn_done"), m.sem("tr_done")
        hi_done, lo_done = m.sem("hi_done"), m.sem("lo_done")
        proj_done = [m.sem(f"proj_done{s}") for s in "qkv"]
        clip_done = [m.sem(f"clip_done{s}") for s in "qkv"]
        unit_done = m.sem("unit_done")
        affine_chain, affine_done = m.sem("affine_chain"), m.sem("affine_done")
        part_hi, part_lo = m.sem("part_hi"), m.sem("part_lo")
        turn_done, turn_out = m.sem("turn_done"), m.sem("turn_out")
        qk_stored = [m.sem(f"qk_stored{i}") for i in range(2)]
        v_stored = [m.sem(f"v_stored{i}") for i in range(2)]
        ln_chain, qk_chain, passed = m.sem("ln_chain"), m.sem("qk_chain"), m.sem("passed")

        wprep = load_transposed_weight(nc, m, w_qkv, 3 * D // P, w_hi, w_lo, ident, ident_done, t_ps)
        block = ctx.enter_context(nc.Block())

        def front(t):
            return not (isinstance(t, int) and t + 1 >= TILES)

        @block.sync
        def _(sp):
            for par in range(2):
                sp.dma_start(x[par][:, :], rows(x1, par)).then_inc(x_loaded[par], 16)
            for i, p in enumerate(ln_params):
                sp.dma_start(lnp[i][:, :], p.rearrange("(a e) -> a e", a=1).to_broadcast([P, D])).then_inc(lnp_loaded, 16)
            sp.dma_start(bias_dram, bias_const).then_inc(bias_copied, 16)
            wprep["sync"](sp)

            def store(t, par):
                b, j = t // QT, t % QT
                sp.wait_ge(clip_done[2], t + 1)
                sp.dma_start(rows(v_dram, t), vals[par][:, :, :].rearrange("p h w -> p (h w)")).then_inc(v_stored[par], 16)
                for s, dram in enumerate((q_dram, k_dram)):
                    sp.wait_ge(turn_out, 4 * t + 2 * s + 2)
                    out = dram[bass.ds(b * (8 * P), 8 * P), bass.ds(j * P, P)].rearrange("(g p) n -> p g n", p=P)
                    sp.dma_start(out, turned[s][par][:, :, :].bitcast(F32)).then_inc(qk_stored[par], 16)

            def step(t, par):
                if not (isinstance(t, int) and t + 2 >= TILES):
                    sp.wait_ge(xn_done, t + 1)
                    sp.dma_start(x[par][:, :], rows(x1, t + 2)).then_inc(x_loaded[par], 16)
                store(t, par)
            tile_loop(sp, step)
            sp.wait_ge(bias_copied, 16)
            for par in range(2):
                sp.wait_ge(v_stored[par], 16 * (TILES // 2))
                sp.wait_ge(qk_stored[par], 32 * (TILES // 2))

        @block.gpsimd
        def _(pool):
            make_identity(nc, pool, ident, zeroed, ident_done)
            for par in range(2):
                nc.gpsimd.memset(vals[par][:, :, HD:VW], 0.0).then_inc(zeroed, 1)
            pool.wait_ge(zeroed, 3)
            for par in range(2):
                nc.gpsimd.memset(vals[par][:, :, HD:HD + 1], 1.0).then_inc(vals_set, 1)
            pool.wait_ge(scaled, 2)

            def step(t, par):
                chain = Chain(pool, affine_chain, 2 * t)
                for s in range(2):
                    pool.wait_ge(unit_done, 2 * t + s + 1)
                    chain(nc.gpsimd.tensor_tensor(normed[s][par][:, :], normed[s][par][:, :], lnp[2 * s][:, :], ALU.mult))
                    nc.gpsimd.tensor_tensor(normed[s][par][:, :], normed[s][par][:, :], lnp[2 * s + 1][:, :],
                                            ALU.add).then_inc(affine_done, 1)
            tile_loop(pool, step)

        @block.tensor
        def _(pe):
            wprep["tensor"](pe)
            sem, count = wprep["done"]
            pe.wait_ge(sem, count)

            def transpose(t, par):
                pe.wait_ge(xn_done, t + 1)
                at_least(pe, lo_done, t - 1)
                for c in range(C):
                    last = nc.tensor.transpose(t_ps[par][:, c * P:(c + 1) * P], xn[par][:, c * P:(c + 1) * P], ident[:, :])
                last.then_inc(tr_done, 1)

            def project(t, par, s):
                at_least(pe, clip_done[s], t)
                cols = slice(s * D, (s + 1) * D)
                split_matmuls(nc, o_ps[s][:, :], xT_hi[par], xT_lo[par], lambda c: w_hi[:, c, cols],
                              lambda c: w_lo[:, c, cols]).then_inc(proj_done[s], 1)

            def turn(t, par, s):
                pe.wait_ge(part_lo, 2 * t + s + 1)
                flat = parts[s][par][:, :, :, :].rearrange("p h k d -> p (h k d)").bitcast(F32)
                for half in range(2):
                    at_least(pe, turn_out, 4 * t + 2 * s + half - 1)
                    for g in range(4):
                        col = (4 * half + g) * P
                        last = nc.tensor.transpose(s_ps[half][:, g * P:(g + 1) * P], flat[:, col:col + P], ident[:, :])
                    last.then_inc(turn_done, 1)

            transpose(0, 0)

            def step(t, par):
                pe.wait_ge(lo_done, t + 1)
                project(t, par, 0)
                if front(t):
                    transpose(t + 1, 1 - par)
                project(t, par, 1)
                if not (isinstance(t, int) and t == 0):
                    turn(t - 1, 1 - par, 0)
                project(t, par, 2)
                if not (isinstance(t, int) and t == 0):
                    turn(t - 1, 1 - par, 1)
            tile_loop(pe, step)
            turn(TILES - 1, 1, 0)
            turn(TILES - 1, 1, 1)

        @block.scalar
        def _(act):
            wprep["scalar"](act)

            def hi(t, par):
                act.wait_ge(tr_done, t + 1)
                at_least(act, proj_done[2], t - 1)
                nc.scalar.activation(xT_hi[par][:, :], t_ps[par][:, :], ACT.Copy).then_inc(hi_done, 1)

            def split_hi(t, par, s):
                act.wait_ge(affine_done, 2 * t + s + 1)
                at_least(act, turn_done, 4 * (t - 2) + 2 * s + 2)
                nc.scalar.activation(parts[s][par][:, :, 0, :], normed[s][par][:, :].rearrange("p (h d) -> p h d", d=HD),
                                     ACT.Copy).then_inc(part_hi, 1)

            def turned_out(t, par, s, half):
                act.wait_ge(turn_done, 4 * t + 2 * s + half + 1)
                if half == 0 and s == 0:
                    at_least(act, qk_stored[par], 32 * (t // 2))
                nc.scalar.activation(turned[s][par][:, 4 * half:4 * half + 4, :],
                                     s_ps[half][:, :].rearrange("p (g n) -> p g n", g=4), ACT.Copy).then_inc(turn_out, 1)

            hi(0, 0)

            def step(t, par):
                if front(t):
                    hi(t + 1, 1 - par)
                if not (isinstance(t, int) and t == 0):
                    for s in range(2):
                        for half in range(2):
                            turned_out(t - 1, 1 - par, s, half)
                for s in range(2):
                    split_hi(t, par, s)
            tile_loop(act, step)
            for s in range(2):
                for half in range(2):
                    turned_out(TILES - 1, 1, s, half)

        @block.vector
        def _(dve):
            dve.wait_ge(lnp_loaded, 64)
            for i in range(2):
                nc.vector.tensor_scalar(lnp[i][:, :], lnp[i][:, :], HD ** -0.5, None, ALU.mult).then_inc(scaled, 1)
            wprep["vector"](dve)

            def norm(t, par):
                dve.wait_ge(x_loaded[par], 16 * (t // 2 + 1))
                at_least(dve, tr_done, t - 1)
                chain = Chain(dve, ln_chain, LN_LINKS * t, passed)
                layernorm_steps(nc, chain, x[par][:, :], xn[par][:, :], ln).then_inc(xn_done, 1)

            def lo(t, par):
                dve.wait_ge(hi_done, t + 1)
                nc.vector.tensor_tensor(xT_lo[par][:, :], t_ps[par][:, :], xT_hi[par][:, :].bitcast(F32),
                                        ALU.subtract).then_inc(lo_done, 1)

            def clip(t, par, s):
                dve.wait_ge(proj_done[s], t + 1)
                if s == 2:
                    at_least(dve, v_stored[par], 16 * (t // 2))
                    nc.vector.tensor_scalar(vals[par][:, :, 0:HD], o_ps[2][:, :].rearrange("p (h d) -> p h d", d=HD),
                                            CLIP, -CLIP, ALU.min, ALU.max).then_inc(clip_done[2], 1)
                else:
                    at_least(dve, unit_done, 2 * (t - 1))
                    nc.vector.tensor_scalar(clipped[s][par][:, :], o_ps[s][:, :], CLIP, -CLIP, ALU.min,
                                            ALU.max).then_inc(clip_done[s], 1)

            def unit(t, par):
                chain = Chain(dve, qk_chain, QK_LINKS * t, passed)
                for s in range(2):
                    dve.wait_ge(clip_done[s], t + 1)
                    chain(nc.vector.bn_stats(qk_stats[:, s, :], clipped[s][par][:, :]), apart=True)
                for s in range(2):
                    chain(nc.vector.bn_aggr(qk_mv[:, s, :], qk_stats[:, s, :]), apart=True)
                chain(nc.vector.tensor_copy(qk_var[:, :], qk_mv[:, :, 1]))
                rsqrt_steps(nc, chain, qk_var[:, :], qk_rstd[:, :], (qk_t0[:, :], qk_t1[:, :]))
                assert chain.n == QK_LINKS
                at_least(dve, part_lo, 2 * (t - 1))
                for s in range(2):
                    nc.vector.tensor_scalar(normed[s][par][:, :], clipped[s][par][:, :], qk_mv[:, s, 0:1],
                                            qk_rstd[:, s:s + 1], ALU.subtract, ALU.mult).then_inc(unit_done, 1)

            def split_lo(t, par, s):
                dve.wait_ge(part_hi, 2 * t + s + 1)
                nc.vector.tensor_tensor(parts[s][par][:, :, 1, :], normed[s][par][:, :].rearrange("p (h d) -> p h d", d=HD),
                                        parts[s][par][:, :, 0, :].bitcast(F32), ALU.subtract).then_inc(part_lo, 1)

            norm(0, 0)
            lo(0, 0)
            norm(1, 1)
            dve.wait_ge(vals_set, 2)

            def step(t, par):
                if front(t):
                    lo(t + 1, 1 - par)
                clip(t, par, 0)
                clip(t, par, 1)
                unit(t, par)
                clip(t, par, 2)
                if not (isinstance(t, int) and t + 2 >= TILES):
                    norm(t + 2, par)
                for s in range(2):
                    split_lo(t, par, s)
            tile_loop(dve, step)


QK_LINKS = 5 + RSQRT_LINKS


def stack_unit(u):
    if u == 0:
        return 0, (0, 1, 2, 3), P
    if u < 3:
        return 1, (2 * u - 2, 2 * u - 1), 2 * P
    i = 2 if u < 7 else 3
    return i, ((u - 3) % 4,), (i + 1) * P


S_UNITS = 11
T_UNITS = 5
PCOLS = HG * 10 * P


def prob_cols(h, j):
    return {0: h * 1024, 1: h * 1024 + 512, 3: h * 1024 + 896, 2: HG * 1024 + h * 256}[j]


def attention_block(nc, q_dram, k_dram, v_dram, bias_dram, o_dram):
    with ExitStack() as ctx:
        m = Memory(nc, ctx, "att")
        RING = 4
        q_st = [m.sb(f"q_st{i}", [P, HG, SEQ], F32R) for i in range(RING)]
        k_st = [m.sb(f"k_st{i}", [P, HG, SEQ], F32R) for i in range(RING)]
        v_sb = [m.sb(f"v_sb{i}", [P, QT, HG * VW]) for i in range(RING)]
        prob = [m.sb(f"prob{i}", [P, PCOLS]) for i in range(2)]
        nmax = [m.sb(f"nmax{i}", [P, QT, HG]) for i in range(2)]
        m_hi = [m.sb(f"m_hi{i}", [HG, SEQ], F32R) for i in range(2)]
        m_lo = [m.sb(f"m_lo{i}", [HG, SEQ], F32R) for i in range(2)]
        oT = [m.sb(f"oT{i}", [P, SEQ]) for i in range(2)]
        rden = m.sb("rden", [P, QT, HG, 1])
        o_sb = [m.sb(f"o_sb{i}", [P, QT, 2 * HG * HD]) for i in range(2)]
        ident = m.sb("ident", [P, P])
        ident_bf = m.sb("ident_bf", [P, P], BF16)
        mask = m.sb("mask", [P, HG, P], BF16)
        mask_t = m.sb("mask_t", [P, 2, P], BF16)
        s_ps = [m.ps(f"s_ps{i}") for i in range(2)]
        st_ps = [m.ps(f"st_ps{i}", 1024) for i in range(2)]
        pv_ps = m.ps("pv_ps")
        x_ps = m.ps("x_ps")

        stack_loaded = [m.sem(f"stack_loaded{i}") for i in range(RING)]
        zeroed, const_done = m.sem("zeroed"), m.sem("const_done")
        s_done, max_done = m.sem("s_done"), m.sem("max_done")
        mT_done, m_hi_done, m_lo_done = m.sem("mT_done"), m.sem("m_hi_done"), m.sem("m_lo_done")
        m_loaded = [m.sem(f"m_loaded{i}") for i in range(2)]
        st_done, exp_done = m.sem("st_done"), m.sem("exp_done")
        pv_done, oT_done, turn_done = m.sem("pv_done"), m.sem("oT_done"), m.sem("turn_done")
        rden_done, o_done = m.sem("rden_done"), m.sem("o_done")
        o_stored = [m.sem(f"o_stored{i}") for i in range(2)]
        LOADS = 8
        SCORE_ROWS = STACK + BIAS_ROWS
        FULL_ROWS = SCORE_ROWS + MAX_ROWS
        block = ctx.enter_context(nc.Block())

        def group_loop(engine, step):
            step(0, 0)
            with engine.Fori(0, (NG - 4) // 4) as i:
                for k in range(1, 5):
                    step(4 * i + k, k % 4)
            for n in range(NG - 3, NG):
                step(n, n % 4)

        def is_last(n, ahead=1):
            return isinstance(n, int) and n + ahead >= NG

        def is_first(n):
            return isinstance(n, int) and n == 0

        @block.sync
        def _(sp):
            def load(n, r):
                at_least(sp, st_done, T_UNITS * (n - 3))
                at_least(sp, pv_done, n - 3)
                src_q = q_dram[bass.ds(n * P, P), :].rearrange("(h r) n -> r h n", h=HG)
                src_k = k_dram[bass.ds(n * P, P), :].rearrange("(h r) n -> r h n", h=HG)
                q, k, done = q_st[r], k_st[r], stack_loaded[r]
                g8 = n % 8

                def put(dst, src):
                    sp.dma_start(dst.bitcast(F32), src).then_inc(done, 16)
                put(q[0:2 * HD, :, :], src_q)
                put(q[2 * HD:4 * HD, :, :], src_q)
                put(k[0:2 * HD, :, :], src_k)
                put(k[2 * HD:3 * HD, :, :], src_k[HD:2 * HD])
                put(k[3 * HD:4 * HD, :, :], src_k[0:HD])
                put(q[STACK:STACK + BIAS_ROWS, :, :], bias_dram[0, 0:BIAS_ROWS, bass.ds(g8 * HG, HG), :])
                put(k[STACK:FULL_ROWS, :, :], bias_dram[1, :, bass.ds(g8 * HG, HG), :])
                b = n // 8
                src_v = v_dram[bass.ds(b * SEQ, SEQ), bass.ds(g8 * (HG * VW), HG * VW)].rearrange("(j p) w -> p j w", p=P)
                sp.dma_start(v_sb[r][:, :, :], src_v).then_inc(done, 16)

            def max_rows(n, r):
                sp.wait_ge(m_lo_done, n + 1)
                at = q_st[r]
                for i, src in enumerate((m_hi, m_lo)):
                    row = SCORE_ROWS + i
                    sp.dma_start(at[row:row + 1, :, :].bitcast(F32), src[r % 2][:, :].bitcast(F32)).then_inc(m_loaded[r % 2], 16)

            def store(n, r):
                sp.wait_ge(o_done, n + 1)
                out = o_dram[bass.ds((n // 8) * SEQ, SEQ), bass.ds(((n % 8) // 2) * P, P)].rearrange("(i p) w -> p i w", p=P)
                sp.dma_start(out, o_sb[(r // 2) % 2][:, :, :]).then_inc(o_stored[(r // 2) % 2], 16)

            for n in range(3):
                load(n, n)
            max_rows(0, 0)

            def step(n, r):
                if not is_last(n, 3):
                    load(n + 3, (r + 3) % 4)
                if not is_last(n):
                    max_rows(n + 1, (r + 1) % 4)
                if not is_first(n) and r % 2 == 0:
                    store(n - 1, (r - 1) % 4)
            group_loop(sp, step)
            store(NG - 1, 3)
            for i in range(2):
                sp.wait_ge(o_stored[i], 16 * (NG // 4))

        @block.gpsimd
        def _(pool):
            nc.gpsimd.memset(ident[:, :], 0.0).then_inc(zeroed, 1)
            nc.gpsimd.memset(ident_bf[:, :], 0.0).then_inc(zeroed, 1)
            nc.gpsimd.memset(mask[:, :, :], 0.0).then_inc(zeroed, 1)
            nc.gpsimd.memset(mask_t[:, :, :], 0.0).then_inc(zeroed, 1)
            pool.wait_ge(zeroed, 4)
            for a in (ident, ident_bf):
                nc.gpsimd.affine_select(out=a[:, :], in_=a[:, :], compare_op=ALU.not_equal, fill=1.0, base=0,
                                        pattern=[[-1, P]], channel_multiplier=1).then_inc(const_done, 1)
            nc.gpsimd.affine_select(out=mask[:, :, :], in_=mask[:, :, :], compare_op=ALU.is_ge, fill=NEG, base=0,
                                    pattern=[[0, HG], [-1, P]], channel_multiplier=1).then_inc(const_done, 1)
            nc.gpsimd.affine_select(out=mask_t[:, :, :], in_=mask_t[:, :, :], compare_op=ALU.is_ge, fill=NEG, base=0,
                                    pattern=[[0, 2], [1, P]], channel_multiplier=-1).then_inc(const_done, 1)

        @block.tensor
        def _(pe):
            pe.wait_ge(const_done, 4)

            def scores(n, r, u):
                i, heads, w = stack_unit(u)
                bank = s_ps[(S_UNITS * r + u) % 2]
                if u == 0:
                    pe.wait_ge(stack_loaded[r], 16 * LOADS * (n // 4 + 1))
                at_least(pe, max_done, S_UNITS * n + u - 1)
                k = len(heads)
                diag = bank[:, 0:k * w].rearrange("p (h w) -> p h w", h=k)[:, :, i * P:(i + 1) * P]
                nc.tensor.matmul(diag, ident_bf[:, :], mask[:, 0:k, :], start=True, stop=False, skip_group_check=True)
                for a, h in enumerate(heads):
                    last = nc.tensor.matmul(bank[:, a * w:(a + 1) * w], q_st[r][0:SCORE_ROWS, h, i * P:(i + 1) * P],
                                            k_st[r][0:SCORE_ROWS, h, 0:w], start=False, stop=(a == k - 1),
                                            skip_group_check=True)
                last.then_inc(s_done, 1)

            def turn_max(n, r):
                pe.wait_ge(max_done, S_UNITS * (n + 1))
                at_least(pe, o_done, n - 1)
                if isinstance(n, int) and n == 1:
                    pe.wait_ge(m_lo_done, 1)
                for i in range(QT):
                    last = nc.tensor.transpose(x_ps[0:HG, i * P:(i + 1) * P], nmax[r % 2][:, i, :], ident[:, :])
                last.then_inc(mT_done, 1)

            def scores_by_key(n, r, u):
                bank = st_ps[(T_UNITS * r + u) % 2]
                if u == 0:
                    pe.wait_ge(m_loaded[r % 2], 32 * (n // 2 + 1))
                at_least(pe, exp_done, T_UNITS * n + u - 1)
                todo = [(u, 0, 0), (u, 1, 512), (u, 3, 896)] if u < 4 else [(h, 2, 256 * h) for h in range(HG)]
                if u < 4:
                    diags = [bank[:, 0:P], bank[:, 512:1024].rearrange("p (a w) -> p a w", a=4)[:, 0:4:3, :]]
                else:
                    diags = [bank[:, 512 * a:512 * (a + 1)].rearrange("p (h w) -> p h w", h=2)[:, :, 0:P] for a in range(2)]
                for d in diags:
                    rhs = mask_t[:, 0, :] if len(d.shape) == 2 else mask_t[:, :, :]
                    nc.tensor.matmul(d, ident_bf[:, :], rhs, start=True, stop=False, skip_group_check=True)
                for h, j, col in todo:
                    w = SEQ - j * P
                    last = nc.tensor.matmul(bank[:, col:col + w], k_st[r][0:FULL_ROWS, h, j * P:(j + 1) * P],
                                            q_st[r][0:FULL_ROWS, h, j * P:SEQ], start=False, stop=True,
                                            skip_group_check=True)
                last.then_inc(st_done, 1)

            def values(n, r):
                pe.wait_ge(exp_done, T_UNITS * (n + 1))
                at_least(pe, oT_done, n)
                for j in range(QT):
                    for h in range(HG):
                        w = SEQ - j * P
                        col = prob_cols(h, j)
                        last = nc.tensor.matmul(pv_ps[VW * h:VW * (h + 1), j * P:SEQ], v_sb[r][:, j, VW * h:VW * (h + 1)],
                                                prob[r % 2][:, col:col + w], start=(j == 0), stop=(j == QT - 1))
                last.then_inc(pv_done, 1)

            def turn_out(n, r):
                pe.wait_ge(oT_done, n + 1)
                if isinstance(n, int) and n + 1 >= NG:
                    pe.wait_ge(o_done, n)
                else:
                    pe.wait_ge(m_lo_done, n + 2)
                for i in range(QT):
                    last = nc.tensor.transpose(x_ps[:, i * P:(i + 1) * P], oT[r % 2][:, i * P:(i + 1) * P], ident[:, :])
                last.then_inc(turn_done, 1)

            for u in range(S_UNITS):
                scores(0, 0, u)
            turn_max(0, 0)

            def step(n, r):
                rn, rp = (r + 1) % 4, (r - 1) % 4
                more = not is_last(n)
                for item in ("S0 S1 S2 PV S3 T0 S4 T1 S5 OT T2 S6 T3 S7 T4 S8 S9 S10 MT").split():
                    kind, u = item[0], item[1:]
                    if kind == "S" and more:
                        scores(n + 1, rn, int(u))
                    elif kind == "T":
                        scores_by_key(n, r, int(u))
                    elif kind == "P" and not is_first(n):
                        values(n - 1, rp)
                    elif kind == "O" and not is_first(n):
                        turn_out(n - 1, rp)
                    elif kind == "M" and more:
                        turn_max(n + 1, rn)
            group_loop(pe, step)
            values(NG - 1, 3)
            turn_out(NG - 1, 3)

        @block.scalar
        def _(act):
            def max_hi(n, r):
                act.wait_ge(mT_done, n + 1)
                at_least(act, m_loaded[r % 2], 32 * (n // 2))
                nc.scalar.activation(m_hi[r % 2][:, :], x_ps[0:HG, :], ACT.Copy).then_inc(m_hi_done, 1)

            def exps(n, r, u):
                act.wait_ge(st_done, T_UNITS * n + u + 1)
                if u == 0:
                    at_least(act, pv_done, n - 1)
                nc.scalar.activation(prob[r % 2][:, 1024 * u:1024 * (u + 1)], st_ps[(T_UNITS * r + u) % 2][:, :],
                                     ACT.Exp).then_inc(exp_done, 1)

            def out_copy(n, r):
                act.wait_ge(pv_done, n + 1)
                at_least(act, turn_done, n)
                nc.scalar.activation(oT[r % 2][:, :], pv_ps[:, :], ACT.Copy).then_inc(oT_done, 1)

            max_hi(0, 0)

            def step(n, r):
                if not is_first(n):
                    out_copy(n - 1, (r - 1) % 4)
                for u in range(T_UNITS):
                    exps(n, r, u)
                if not is_last(n):
                    max_hi(n + 1, (r + 1) % 4)
            group_loop(act, step)
            out_copy(NG - 1, 3)

        @block.vector
        def _(dve):
            def reduce(n, r, u):
                i, heads, w = stack_unit(u)
                k = len(heads)
                dve.wait_ge(s_done, S_UNITS * n + u + 1)
                if u == 0:
                    at_least(dve, mT_done, n - 1)
                nc.vector.tensor_reduce(nmax[r % 2][:, i, heads[0]:heads[0] + k],
                                        s_ps[(S_UNITS * r + u) % 2][:, 0:k * w].rearrange("p (h w) -> p h w", h=k),
                                        X_AXIS, ALU.max, negate=True).then_inc(max_done, 1)

            def max_lo(n, r):
                dve.wait_ge(m_hi_done, n + 1)
                nc.vector.tensor_tensor(m_lo[r % 2][:, :], x_ps[0:HG, :], m_hi[r % 2][:, :].bitcast(F32),
                                        ALU.subtract).then_inc(m_lo_done, 1)

            def normalise(n, r):
                dve.wait_ge(turn_done, n + 1)
                turned = x_ps[:, :].rearrange("p (i h w) -> p i h w", i=QT, h=HG)
                nc.vector.reciprocal(rden[:, :, :, 0], turned[:, :, :, HD]).then_inc(rden_done, 1)
                dve.wait_ge(rden_done, n + 1)
                half = r % 2
                slot = (r // 2) % 2
                if half == 0:
                    at_least(dve, o_stored[slot], 16 * (n // 4))
                out = o_sb[slot][:, :, half * HG * HD:(half + 1) * HG * HD].rearrange("p i (h d) -> p i h d", h=HG)
                nc.vector.tensor_tensor(out, turned[:, :, :, 0:HD], rden[:, :, :, :].to_broadcast([P, QT, HG, HD]),
                                        ALU.mult).then_inc(o_done, 1)

            for u in range(S_UNITS):
                reduce(0, 0, u)
            max_lo(0, 0)

            def step(n, r):
                more = not is_last(n)
                rn = (r + 1) % 4
                for u in range(S_UNITS):
                    if more:
                        reduce(n + 1, rn, u)
                    if u == 5 and not is_first(n):
                        normalise(n - 1, (r - 1) % 4)
                if more:
                    max_lo(n + 1, rn)
            group_loop(dve, step)
            normalise(NG - 1, 3)


def out_block(nc, o_dram, x1, w_out, x2):
    with ExitStack() as ctx:
        m = Memory(nc, ctx, "out")
        w_hi = m.sb("w_hi", [P, C, D], F32R)
        w_lo = m.sb("w_lo", [P, C, D], F32R)
        ident = m.sb("ident", [P, P])
        x = [m.sb(f"x{i}", [P, D]) for i in range(2)]
        o = [m.sb(f"o{i}", [P, D]) for i in range(2)]
        y = [m.sb(f"y{i}", [P, D]) for i in range(2)]
        oT_hi = [m.sb(f"oT_hi{i}", [P, C * P], F32R) for i in range(2)]
        oT_lo = [m.sb(f"oT_lo{i}", [P, C * P], F32R) for i in range(2)]
        y_ps = [m.ps(f"y_ps{i}") for i in range(2)]
        t_ps = [m.ps(f"t_ps{i}") for i in range(2)]
        loaded = [m.sem(f"loaded{i}") for i in range(2)]
        stored = [m.sem(f"stored{i}") for i in range(2)]
        zeroed, ident_done = m.sem("zeroed"), m.sem("ident_done")
        tr_done, hi_done, lo_done = m.sem("tr_done"), m.sem("hi_done"), m.sem("lo_done")
        y_done, sum_done = m.sem("y_done"), m.sem("sum_done")
        wprep = load_transposed_weight(nc, m, w_out, C, w_hi, w_lo, ident, ident_done, t_ps)
        block = ctx.enter_context(nc.Block())

        @block.sync
        def _(sp):
            def load(t, par):
                at_least(sp, sum_done, t - 1)
                sp.dma_start(o[par][:, :], rows(o_dram, t)).then_inc(loaded[par], 16)
                sp.dma_start(x[par][:, :], rows(x1, t)).then_inc(loaded[par], 16)
            wprep["sync"](sp)
            load(0, 0)
            load(1, 1)

            def step(t, par):
                sp.wait_ge(sum_done, t + 1)
                sp.dma_start(rows(x2, t), y[par][:, :]).then_inc(stored[par], 16)
                if not (isinstance(t, int) and t + 2 >= TILES):
                    load(t + 2, par)
            tile_loop(sp, step)
            for par in range(2):
                sp.wait_ge(stored[par], 16 * (TILES // 2))

        @block.gpsimd
        def _(pool):
            make_identity(nc, pool, ident, zeroed, ident_done)

        @block.tensor
        def _(pe):
            wprep["tensor"](pe)
            sem, count = wprep["done"]
            pe.wait_ge(sem, count)

            def transpose(t, par):
                pe.wait_ge(loaded[par], 32 * (t // 2 + 1))
                at_least(pe, lo_done, t - 1)
                for c in range(C):
                    last = nc.tensor.transpose(t_ps[par][:, c * P:(c + 1) * P], o[par][:, c * P:(c + 1) * P], ident[:, :])
                last.then_inc(tr_done, 1)
            transpose(0, 0)

            def step(t, par):
                if not (isinstance(t, int) and t + 1 >= TILES):
                    transpose(t + 1, 1 - par)
                pe.wait_ge(lo_done, t + 1)
                at_least(pe, sum_done, t - 1)
                split_matmuls(nc, y_ps[par][:, :], oT_hi[par], oT_lo[par], lambda c: w_hi[:, c, :],
                              lambda c: w_lo[:, c, :]).then_inc(y_done, 1)
            tile_loop(pe, step)

        @block.scalar
        def _(act):
            wprep["scalar"](act)

            def step(t, par):
                act.wait_ge(tr_done, t + 1)
                at_least(act, y_done, t - 1)
                nc.scalar.activation(oT_hi[par][:, :], t_ps[par][:, :], ACT.Copy).then_inc(hi_done, 1)
            tile_loop(act, step)

        @block.vector
        def _(dve):
            wprep["vector"](dve)

            def lo(t, par):
                dve.wait_ge(hi_done, t + 1)
                nc.vector.tensor_tensor(oT_lo[par][:, :], t_ps[par][:, :], oT_hi[par][:, :].bitcast(F32),
                                        ALU.subtract).then_inc(lo_done, 1)
            lo(0, 0)

            def step(t, par):
                if not (isinstance(t, int) and t + 1 >= TILES):
                    lo(t + 1, 1 - par)
                dve.wait_ge(y_done, t + 1)
                at_least(dve, stored[par], 16 * (t // 2))
                nc.vector.tensor_tensor(y[par][:, :], y_ps[par][:, :], x[par][:, :], ALU.add).then_inc(sum_done, 1)
            tile_loop(dve, step)


def macaron(nc, x, w_qkv, q_w, q_b, k_w, k_b, w_out, w_gate, b_gate, w_e, b_e, bias_const, out):
    def scratch(name, shape):
        return nc.dram_tensor(name, shape, F32, kind="Internal").ap()

    x1, x2 = scratch("x1", [TOKENS, D]), scratch("x2", [TOKENS, D])
    q_dram, k_dram = scratch("q_parts", [NG * P, SEQ]), scratch("k_parts", [NG * P, SEQ])
    v_dram, o_dram = scratch("v_vals", [TOKENS, H * VW]), scratch("o_vals", [TOKENS, D])
    bias_dram = scratch("bias_rows", [2, BIAS_ROWS + MAX_ROWS, H, SEQ])
    flat = x.rearrange("b s d -> (b s) d")
    ffn_block(nc, "ffn1", flat, x1, w_gate, b_gate, w_e, b_e)
    qkv_block(nc, x1, w_qkv, (q_w, q_b, k_w, k_b), bias_const, q_dram, k_dram, v_dram, bias_dram)
    attention_block(nc, q_dram, k_dram, v_dram, bias_dram, o_dram)
    out_block(nc, o_dram, x1, w_out, x2)
    ffn_block(nc, "ffn2", x2, out.rearrange("b s d -> (b s) d"), w_gate, b_gate, w_e, b_e)


def bias_rows():
    import numpy as np
    step = np.arange(1, H + 1, dtype=np.float32) * (8.0 / H)
    slope = (1.0 / np.power(2.0, step)).astype(np.float32)
    hi = (slope.view(np.uint32) & np.uint32(0xFFFFF000)).view(np.float32)
    lo = slope - hi
    pos = np.arange(SEQ, dtype=np.float32)
    r = np.zeros((2, BIAS_ROWS + MAX_ROWS, H, SEQ), np.float32)
    r[0, 0], r[0, 2] = hi[:, None], lo[:, None]
    r[0, 1] = r[0, 3] = pos[None, :]
    r[1, 0] = r[1, 2] = pos[None, :]
    r[1, 1], r[1, 3] = -hi[:, None], -lo[:, None]
    r[1, 4:] = 1.0
    return r


_INS = ['L0_attn_hidden_states', 'L0_attn_Wqkv', 'L0_attn_q_ln_w', 'L0_attn_q_ln_b', 'L0_attn_k_ln_w',
        'L0_attn_k_ln_b', 'L0_attn_Wout', 'L0_ffn_W_gate', 'L0_ffn_b_gate', 'L0_ffn_W_e', 'L0_ffn_b_e']


def kernel(**inputs):
    import numpy as _np
    import concourse.bacc as _bacc
    from concourse import mybir as _mybir
    from concourse.bass_utils import run_bass_kernel_spmd as _run

    nc = _bacc.Bacc("TRN2", target_bir_lowering=False, num_devices=1)
    arrays, args = {}, []
    for name in _INS:
        a = _np.ascontiguousarray(inputs[name])
        arrays[f"in_{name}"] = a
        args.append(nc.dram_tensor(f"in_{name}", a.shape, _mybir.dt.from_np(a.dtype), kind="ExternalInput").ap())
    a = bias_rows()
    arrays["in_bias_rows"] = a
    args.append(nc.dram_tensor("in_bias_rows", a.shape, _mybir.dt.from_np(a.dtype), kind="ExternalInput").ap())
    args.append(nc.dram_tensor("out_0", (B, SEQ, D), F32, kind="ExternalOutput").ap())
    macaron(nc, *args)
    r = _run(nc, [arrays], core_ids=[0])
    return r.results[0]["out_0"]
```

```python
import concourse.bass as bass
from concourse import mybir
from contextlib import ExitStack

F32 = mybir.dt.float32
F32R = mybir.dt.float32r
BF16 = mybir.dt.bfloat16
I32 = mybir.dt.int32
U32 = mybir.dt.uint32
ALU = mybir.AluOpType
ACT = mybir.ActivationFunctionType
X_AXIS = mybir.AxisListType.X

P = 128
D = 512
B, SEQ = 4, 512
TOKENS = B * SEQ
TILES = TOKENS // P
QT = SEQ // P
C = D // P
E = 8
H = 32
HD = D // H
HG = 4
NG = B * H // HG
VW = 32
CLIP = 8.0
EPS = 1e-5
NEG = -1e30
STACK = 4 * HD
BIAS_ROWS = 4
MAX_ROWS = 2


def at_least(engine, sem, value):
    if isinstance(value, int) and value <= 0:
        return
    engine.wait_ge(sem, value)


class Chain:

    def __init__(self, engine, sem, base=0, passed=None):
        self.engine, self.sem, self.base, self.n, self.passed = engine, sem, base, 0, passed

    def __call__(self, instruction, apart=False):
        self.n += 1
        instruction.then_inc(self.sem, 1)
        self.engine.wait_ge(self.sem, self.base + self.n)
        if apart and not isinstance(self.base, int):
            self.engine.sem_inc(self.passed, 1)


def tile_loop(engine, step, first=2, last=TILES - 2):
    for t in range(first):
        step(t, t % 2)
    with engine.Fori(first // 2, last // 2) as i:
        for par in range(2):
            step(2 * i + par, par)
    for t in range(last, TILES):
        step(t, t % 2)


def rsqrt_steps(nc, chain, var, y, tmp):
    chain(nc.vector.tensor_scalar(tmp[1], var, EPS, None, ALU.add))
    chain(nc.vector.tensor_scalar(y.bitcast(I32), tmp[1].bitcast(I32), -0.5, 1597463007.0, ALU.mult, ALU.add))
    for _ in range(3):
        chain(nc.vector.tensor_tensor(tmp[0], y, y, ALU.mult))
        chain(nc.vector.scalar_tensor_tensor(tmp[0], tmp[0], -0.5, tmp[1], ALU.mult, ALU.mult))
        chain(nc.vector.scalar_tensor_tensor(y, tmp[0], 1.5, y, ALU.add, ALU.mult))


RSQRT_LINKS = 11


def layernorm_steps(nc, chain, x, out, ln):
    chain(nc.vector.bn_stats(ln["stats"], x), apart=True)
    chain(nc.vector.bn_aggr(ln["mv"], ln["stats"]))
    rsqrt_steps(nc, chain, ln["mv"][:, 1:2], ln["rstd"], (ln["t0"], ln["t1"]))
    return nc.vector.tensor_scalar(out, x, ln["mv"][:, 0:1], ln["rstd"], ALU.subtract, ALU.mult)


LN_LINKS = 2 + RSQRT_LINKS


class Memory:

    sems = []

    def __init__(self, nc, ctx, prefix):
        self.nc, self.ctx, self.prefix = nc, ctx, prefix

    def sb(self, name, shape, dt=F32):
        return self.ctx.enter_context(self.nc.sbuf_tensor(f"{self.prefix}_{name}", shape, dt))

    def ps(self, name, width=512):
        return self.ctx.enter_context(self.nc.psum_tensor(f"{self.prefix}_{name}", [P, width], F32))

    def sem(self, name):
        sem = self.nc.alloc_semaphore(name=f"{self.prefix}_{name}")
        Memory.sems.append(sem)
        return sem

    def ln(self):
        return {"stats": self.sb("ln_stats", [P, 6])[:, :], "mv": self.sb("ln_mv", [P, 2])[:, :],
                "rstd": self.sb("ln_rstd", [P, 1])[:, :], "t0": self.sb("ln_t0", [P, 1])[:, :],
                "t1": self.sb("ln_t1", [P, 1])[:, :]}


def clear_semaphores(nc):
    nc.clear_and_free_semaphores(Memory.sems)
    nc.all_engine_barrier()
    Memory.sems = []


def rows(dram, t, n=P):
    return dram[bass.ds(t * n, n), :]


def split_matmuls(nc, out, x_hi, x_lo, w_hi, w_lo):
    for c in range(C):
        s = slice(c * P, (c + 1) * P)
        nc.tensor.matmul(out, x_hi[:, s], w_hi(c), start=(c == 0), stop=False)
        nc.tensor.matmul(out, x_hi[:, s], w_lo(c), start=False, stop=False)
        last = nc.tensor.matmul(out, x_lo[:, s], w_hi(c), start=False, stop=(c == C - 1))
    return last


def load_transposed_weight(nc, m, w, n_tiles, w_hi, w_lo, ident, ident_done, t_ps):
    stage = [m.sb(f"wst{i}", [P, D]) for i in range(2)]
    loaded = [m.sem(f"wst_loaded{i}") for i in range(2)]
    tr, hi, lo = m.sem("wst_tr"), m.sem("wst_hi"), m.sem("wst_lo")

    def cols(w_t, t):
        return w_t[:, :, bass.ds(t * P, P)]

    def pairs(engine, step):
        for t in range(2):
            step(t, t)
        if n_tiles > 2:
            with engine.Fori(1, n_tiles // 2) as i:
                for par in range(2):
                    step(2 * i + par, par)

    def sync(sp):
        def step(t, par):
            at_least(sp, tr, t - 1)
            sp.dma_start(stage[par][:, :], rows(w, t)).then_inc(loaded[par], 16)
        pairs(sp, step)

    def tensor(pe):
        pe.wait_ge(ident_done, 1)

        def step(t, par):
            pe.wait_ge(loaded[par], 16 * (t // 2 + 1))
            at_least(pe, lo, t - 1)
            for c in range(C):
                last = nc.tensor.transpose(t_ps[par][:, c * P:(c + 1) * P], stage[par][:, c * P:(c + 1) * P], ident[:, :])
            last.then_inc(tr, 1)
        pairs(pe, step)

    def bank(par):
        return t_ps[par][:, :].rearrange("p (c n) -> p c n", c=C)

    def scalar(act):
        def step(t, par):
            act.wait_ge(tr, t + 1)
            nc.scalar.activation(cols(w_hi, t), bank(par), ACT.Copy).then_inc(hi, 1)
        pairs(act, step)

    def vector(dve):
        def step(t, par):
            dve.wait_ge(hi, t + 1)
            nc.vector.tensor_tensor(cols(w_lo, t), bank(par), cols(w_hi, t).bitcast(F32), ALU.subtract).then_inc(lo, 1)
        pairs(dve, step)

    return {"sync": sync, "tensor": tensor, "scalar": scalar, "vector": vector, "done": (lo, n_tiles)}


def make_identity(nc, pool, ident, zeroed, done):
    nc.gpsimd.memset(ident[:, :], 0.0).then_inc(zeroed, 1)
    pool.wait_ge(zeroed, 1)
    nc.gpsimd.affine_select(out=ident[:, :], in_=ident[:, :], compare_op=ALU.not_equal, fill=1.0, base=0,
                            pattern=[[-1, P]], channel_multiplier=1).then_inc(done, 1)


def qkv_block(nc, x1, w_qkv, ln_params, bias_const, q_dram, k_dram, v_dram, bias_dram):
    with ExitStack() as ctx:
        m = Memory(nc, ctx, "qkv")
        w_hi = m.sb("w_hi", [P, C, 3 * D], F32R)
        w_lo = m.sb("w_lo", [P, C, 3 * D], F32R)
        ident = m.sb("ident", [P, P])
        lnp = [m.sb(f"lnp{i}", [P, D]) for i in range(4)]
        x = [m.sb(f"x{i}", [P, D]) for i in range(2)]
        xn = [m.sb(f"xn{i}", [P, D]) for i in range(2)]
        xT_hi = [m.sb(f"xT_hi{i}", [P, C * P], F32R) for i in range(2)]
        xT_lo = [m.sb(f"xT_lo{i}", [P, C * P], F32R) for i in range(2)]
        clipped = [[m.sb(f"clip{s}{i}", [P, D]) for i in range(2)] for s in "qk"]
        normed = [[m.sb(f"norm{s}{i}", [P, D]) for i in range(2)] for s in "qk"]
        parts = [[m.sb(f"parts{s}{i}", [P, H, 2, HD], F32R) for i in range(2)] for s in "qk"]
        turned = [[m.sb(f"turned{s}{i}", [P, 8, P], F32R) for i in range(2)] for s in "qk"]
        vals = [m.sb(f"vals{i}", [P, H, VW]) for i in range(2)]
        ln = m.ln()
        qk_stats = m.sb("qk_stats", [P, 2, 6])
        qk_mv = m.sb("qk_mv", [P, 2, 2])
        qk_rstd, qk_t0, qk_t1, qk_var = (m.sb(n, [P, 2]) for n in ("qk_rstd", "qk_t0", "qk_t1", "qk_var"))
        o_ps = [m.ps(f"o_ps{i}") for i in range(3)]
        t_ps = [m.ps(f"t_ps{i}") for i in range(2)]
        s_ps = [m.ps(f"s_ps{i}") for i in range(2)]

        x_loaded = [m.sem(f"x_loaded{i}") for i in range(2)]
        lnp_loaded, bias_copied = m.sem("lnp_loaded"), m.sem("bias_copied")
        zeroed, ident_done, vals_set = m.sem("zeroed"), m.sem("ident_done"), m.sem("vals_set")
        scaled = m.sem("scaled")
        xn_done, tr_done = m.sem("xn_done"), m.sem("tr_done")
        hi_done, lo_done = m.sem("hi_done"), m.sem("lo_done")
        proj_done = [m.sem(f"proj_done{s}") for s in "qkv"]
        clip_done = [m.sem(f"clip_done{s}") for s in "qkv"]
        unit_done = m.sem("unit_done")
        affine_chain, affine_done = m.sem("affine_chain"), m.sem("affine_done")
        part_hi, part_lo = m.sem("part_hi"), m.sem("part_lo")
        turn_done, turn_out = m.sem("turn_done"), m.sem("turn_out")
        qk_stored = [m.sem(f"qk_stored{i}") for i in range(2)]
        v_stored = [m.sem(f"v_stored{i}") for i in range(2)]
        ln_chain, qk_chain, passed = m.sem("ln_chain"), m.sem("qk_chain"), m.sem("passed")

        wprep = load_transposed_weight(nc, m, w_qkv, 3 * D // P, w_hi, w_lo, ident, ident_done, t_ps)
        block = ctx.enter_context(nc.Block())

        def front(t):
            return not (isinstance(t, int) and t + 1 >= TILES)

        @block.sync
        def _(sp):
            for par in range(2):
                sp.dma_start(x[par][:, :], rows(x1, par)).then_inc(x_loaded[par], 16)
            for i, p in enumerate(ln_params):
                sp.dma_start(lnp[i][:, :], p.rearrange("(a e) -> a e", a=1).to_broadcast([P, D])).then_inc(lnp_loaded, 16)
            sp.dma_start(bias_dram, bias_const).then_inc(bias_copied, 16)
            wprep["sync"](sp)

            def store(t, par):
                b, j = t // QT, t % QT
                sp.wait_ge(clip_done[2], t + 1)
                sp.dma_start(rows(v_dram, t), vals[par][:, :, :].rearrange("p h w -> p (h w)")).then_inc(v_stored[par], 16)
                for s, dram in enumerate((q_dram, k_dram)):
                    sp.wait_ge(turn_out, 4 * t + 2 * s + 2)
                    out = dram[bass.ds(b * (8 * P), 8 * P), bass.ds(j * P, P)].rearrange("(g p) n -> p g n", p=P)
                    sp.dma_start(out, turned[s][par][:, :, :].bitcast(F32)).then_inc(qk_stored[par], 16)

            def step(t, par):
                if not (isinstance(t, int) and t + 2 >= TILES):
                    sp.wait_ge(xn_done, t + 1)
                    sp.dma_start(x[par][:, :], rows(x1, t + 2)).then_inc(x_loaded[par], 16)
                store(t, par)
            tile_loop(sp, step)
            sp.wait_ge(bias_copied, 16)
            for par in range(2):
                sp.wait_ge(v_stored[par], 16 * (TILES // 2))
                sp.wait_ge(qk_stored[par], 32 * (TILES // 2))

        @block.gpsimd
        def _(pool):
            make_identity(nc, pool, ident, zeroed, ident_done)
            for par in range(2):
                nc.gpsimd.memset(vals[par][:, :, HD:VW], 0.0).then_inc(zeroed, 1)
            pool.wait_ge(zeroed, 3)
            for par in range(2):
                nc.gpsimd.memset(vals[par][:, :, HD:HD + 1], 1.0).then_inc(vals_set, 1)
            pool.wait_ge(scaled, 2)

            def step(t, par):
                chain = Chain(pool, affine_chain, 2 * t)
                for s in range(2):
                    pool.wait_ge(unit_done, 2 * t + s + 1)
                    chain(nc.gpsimd.tensor_tensor(normed[s][par][:, :], normed[s][par][:, :], lnp[2 * s][:, :], ALU.mult))
                    nc.gpsimd.tensor_tensor(normed[s][par][:, :], normed[s][par][:, :], lnp[2 * s + 1][:, :],
                                            ALU.add).then_inc(affine_done, 1)
            tile_loop(pool, step)

        @block.tensor
        def _(pe):
            wprep["tensor"](pe)
            sem, count = wprep["done"]
            pe.wait_ge(sem, count)

            def transpose(t, par):
                pe.wait_ge(xn_done, t + 1)
                at_least(pe, lo_done, t - 1)
                for c in range(C):
                    last = nc.tensor.transpose(t_ps[par][:, c * P:(c + 1) * P], xn[par][:, c * P:(c + 1) * P], ident[:, :])
                last.then_inc(tr_done, 1)

            def project(t, par, s):
                at_least(pe, clip_done[s], t)
                cols = slice(s * D, (s + 1) * D)
                split_matmuls(nc, o_ps[s][:, :], xT_hi[par], xT_lo[par], lambda c: w_hi[:, c, cols],
                              lambda c: w_lo[:, c, cols]).then_inc(proj_done[s], 1)

            def turn(t, par, s):
                pe.wait_ge(part_lo, 2 * t + s + 1)
                flat = parts[s][par][:, :, :, :].rearrange("p h k d -> p (h k d)").bitcast(F32)
                for half in range(2):
                    at_least(pe, turn_out, 4 * t + 2 * s + half - 1)
                    for g in range(4):
                        col = (4 * half + g) * P
                        last = nc.tensor.transpose(s_ps[half][:, g * P:(g + 1) * P], flat[:, col:col + P], ident[:, :])
                    last.then_inc(turn_done, 1)

            transpose(0, 0)

            def step(t, par):
                pe.wait_ge(lo_done, t + 1)
                project(t, par, 0)
                if front(t):
                    transpose(t + 1, 1 - par)
                project(t, par, 1)
                if not (isinstance(t, int) and t == 0):
                    turn(t - 1, 1 - par, 0)
                project(t, par, 2)
                if not (isinstance(t, int) and t == 0):
                    turn(t - 1, 1 - par, 1)
            tile_loop(pe, step)
            turn(TILES - 1, 1, 0)
            turn(TILES - 1, 1, 1)

        @block.scalar
        def _(act):
            wprep["scalar"](act)

            def hi(t, par):
                act.wait_ge(tr_done, t + 1)
                at_least(act, proj_done[2], t - 1)
                nc.scalar.activation(xT_hi[par][:, :], t_ps[par][:, :], ACT.Copy).then_inc(hi_done, 1)

            def split_hi(t, par, s):
                act.wait_ge(affine_done, 2 * t + s + 1)
                at_least(act, turn_done, 4 * (t - 2) + 2 * s + 2)
                nc.scalar.activation(parts[s][par][:, :, 0, :], normed[s][par][:, :].rearrange("p (h d) -> p h d", d=HD),
                                     ACT.Copy).then_inc(part_hi, 1)

            def turned_out(t, par, s, half):
                act.wait_ge(turn_done, 4 * t + 2 * s + half + 1)
                if half == 0 and s == 0:
                    at_least(act, qk_stored[par], 32 * (t // 2))
                nc.scalar.activation(turned[s][par][:, 4 * half:4 * half + 4, :],
                                     s_ps[half][:, :].rearrange("p (g n) -> p g n", g=4), ACT.Copy).then_inc(turn_out, 1)

            hi(0, 0)

            def step(t, par):
                if front(t):
                    hi(t + 1, 1 - par)
                if not (isinstance(t, int) and t == 0):
                    for s in range(2):
                        for half in range(2):
                            turned_out(t - 1, 1 - par, s, half)
                for s in range(2):
                    split_hi(t, par, s)
            tile_loop(act, step)
            for s in range(2):
                for half in range(2):
                    turned_out(TILES - 1, 1, s, half)

        @block.vector
        def _(dve):
            dve.wait_ge(lnp_loaded, 64)
            for i in range(2):
                nc.vector.tensor_scalar(lnp[i][:, :], lnp[i][:, :], HD ** -0.5, None, ALU.mult).then_inc(scaled, 1)
            wprep["vector"](dve)

            def norm(t, par):
                dve.wait_ge(x_loaded[par], 16 * (t // 2 + 1))
                at_least(dve, tr_done, t - 1)
                chain = Chain(dve, ln_chain, LN_LINKS * t, passed)
                layernorm_steps(nc, chain, x[par][:, :], xn[par][:, :], ln).then_inc(xn_done, 1)

            def lo(t, par):
                dve.wait_ge(hi_done, t + 1)
                nc.vector.tensor_tensor(xT_lo[par][:, :], t_ps[par][:, :], xT_hi[par][:, :].bitcast(F32),
                                        ALU.subtract).then_inc(lo_done, 1)

            def clip(t, par, s):
                dve.wait_ge(proj_done[s], t + 1)
                if s == 2:
                    at_least(dve, v_stored[par], 16 * (t // 2))
                    nc.vector.tensor_scalar(vals[par][:, :, 0:HD], o_ps[2][:, :].rearrange("p (h d) -> p h d", d=HD),
                                            CLIP, -CLIP, ALU.min, ALU.max).then_inc(clip_done[2], 1)
                else:
                    at_least(dve, unit_done, 2 * (t - 1))
                    nc.vector.tensor_scalar(clipped[s][par][:, :], o_ps[s][:, :], CLIP, -CLIP, ALU.min,
                                            ALU.max).then_inc(clip_done[s], 1)

            def unit(t, par):
                chain = Chain(dve, qk_chain, QK_LINKS * t, passed)
                for s in range(2):
                    dve.wait_ge(clip_done[s], t + 1)
                    chain(nc.vector.bn_stats(qk_stats[:, s, :], clipped[s][par][:, :]), apart=True)
                for s in range(2):
                    chain(nc.vector.bn_aggr(qk_mv[:, s, :], qk_stats[:, s, :]), apart=True)
                chain(nc.vector.tensor_copy(qk_var[:, :], qk_mv[:, :, 1]))
                rsqrt_steps(nc, chain, qk_var[:, :], qk_rstd[:, :], (qk_t0[:, :], qk_t1[:, :]))
                assert chain.n == QK_LINKS
                at_least(dve, part_lo, 2 * (t - 1))
                for s in range(2):
                    nc.vector.tensor_scalar(normed[s][par][:, :], clipped[s][par][:, :], qk_mv[:, s, 0:1],
                                            qk_rstd[:, s:s + 1], ALU.subtract, ALU.mult).then_inc(unit_done, 1)

            def split_lo(t, par, s):
                dve.wait_ge(part_hi, 2 * t + s + 1)
                nc.vector.tensor_tensor(parts[s][par][:, :, 1, :], normed[s][par][:, :].rearrange("p (h d) -> p h d", d=HD),
                                        parts[s][par][:, :, 0, :].bitcast(F32), ALU.subtract).then_inc(part_lo, 1)

            norm(0, 0)
            lo(0, 0)
            norm(1, 1)
            dve.wait_ge(vals_set, 2)

            def step(t, par):
                if front(t):
                    lo(t + 1, 1 - par)
                clip(t, par, 0)
                clip(t, par, 1)
                unit(t, par)
                clip(t, par, 2)
                if not (isinstance(t, int) and t + 2 >= TILES):
                    norm(t + 2, par)
                for s in range(2):
                    split_lo(t, par, s)
            tile_loop(dve, step)


QK_LINKS = 5 + RSQRT_LINKS


def stack_unit(u):
    if u == 0:
        return 0, (0, 1, 2, 3), P
    if u < 3:
        return 1, (2 * u - 2, 2 * u - 1), 2 * P
    i = 2 if u < 7 else 3
    return i, ((u - 3) % 4,), (i + 1) * P


S_UNITS = 11
T_UNITS = 5
PCOLS = HG * 10 * P


def prob_cols(h, j):
    return {0: h * 1024, 1: h * 1024 + 512, 3: h * 1024 + 896, 2: HG * 1024 + h * 256}[j]


def attention_block(nc, q_dram, k_dram, v_dram, bias_dram, o_dram):
    with ExitStack() as ctx:
        m = Memory(nc, ctx, "att")
        RING = 4
        q_st = [m.sb(f"q_st{i}", [P, HG, SEQ], F32R) for i in range(RING)]
        k_st = [m.sb(f"k_st{i}", [P, HG, SEQ], F32R) for i in range(RING)]
        v_sb = [m.sb(f"v_sb{i}", [P, QT, HG * VW]) for i in range(RING)]
        prob = [m.sb(f"prob{i}", [P, PCOLS]) for i in range(2)]
        nmax = [m.sb(f"nmax{i}", [P, QT, HG]) for i in range(2)]
        m_hi = [m.sb(f"m_hi{i}", [HG, SEQ], F32R) for i in range(2)]
        m_lo = [m.sb(f"m_lo{i}", [HG, SEQ], F32R) for i in range(2)]
        oT = [m.sb(f"oT{i}", [P, SEQ]) for i in range(2)]
        rden = m.sb("rden", [P, QT, HG, 1])
        o_sb = [m.sb(f"o_sb{i}", [P, QT, 2 * HG * HD]) for i in range(2)]
        ident = m.sb("ident", [P, P])
        ident_bf = m.sb("ident_bf", [P, P], BF16)
        mask = m.sb("mask", [P, HG, P], BF16)
        mask_t = m.sb("mask_t", [P, 2, P], BF16)
        s_ps = [m.ps(f"s_ps{i}") for i in range(2)]
        st_ps = [m.ps(f"st_ps{i}", 1024) for i in range(2)]
        pv_ps = m.ps("pv_ps")
        x_ps = m.ps("x_ps")

        stack_loaded = [m.sem(f"stack_loaded{i}") for i in range(RING)]
        zeroed, const_done = m.sem("zeroed"), m.sem("const_done")
        s_done, max_done = m.sem("s_done"), m.sem("max_done")
        mT_done, m_hi_done, m_lo_done = m.sem("mT_done"), m.sem("m_hi_done"), m.sem("m_lo_done")
        m_loaded = [m.sem(f"m_loaded{i}") for i in range(2)]
        st_done, exp_done = m.sem("st_done"), m.sem("exp_done")
        pv_done, oT_done, turn_done = m.sem("pv_done"), m.sem("oT_done"), m.sem("turn_done")
        rden_done, o_done = m.sem("rden_done"), m.sem("o_done")
        o_stored = [m.sem(f"o_stored{i}") for i in range(2)]
        LOADS = 8
        SCORE_ROWS = STACK + BIAS_ROWS
        FULL_ROWS = SCORE_ROWS + MAX_ROWS
        block = ctx.enter_context(nc.Block())

        def group_loop(engine, step):
            step(0, 0)
            with engine.Fori(0, (NG - 4) // 4) as i:
                for k in range(1, 5):
                    step(4 * i + k, k % 4)
            for n in range(NG - 3, NG):
                step(n, n % 4)

        def is_last(n, ahead=1):
            return isinstance(n, int) and n + ahead >= NG

        def is_first(n):
            return isinstance(n, int) and n == 0

        @block.sync
        def _(sp):
            def load(n, r):
                at_least(sp, st_done, T_UNITS * (n - 3))
                at_least(sp, pv_done, n - 3)
                src_q = q_dram[bass.ds(n * P, P), :].rearrange("(h r) n -> r h n", h=HG)
                src_k = k_dram[bass.ds(n * P, P), :].rearrange("(h r) n -> r h n", h=HG)
                q, k, done = q_st[r], k_st[r], stack_loaded[r]
                g8 = n % 8

                def put(dst, src):
                    sp.dma_start(dst.bitcast(F32), src).then_inc(done, 16)
                put(q[0:2 * HD, :, :], src_q)
                put(q[2 * HD:4 * HD, :, :], src_q)
                put(k[0:2 * HD, :, :], src_k)
                put(k[2 * HD:3 * HD, :, :], src_k[HD:2 * HD])
                put(k[3 * HD:4 * HD, :, :], src_k[0:HD])
                put(q[STACK:STACK + BIAS_ROWS, :, :], bias_dram[0, 0:BIAS_ROWS, bass.ds(g8 * HG, HG), :])
                put(k[STACK:FULL_ROWS, :, :], bias_dram[1, :, bass.ds(g8 * HG, HG), :])
                b = n // 8
                src_v = v_dram[bass.ds(b * SEQ, SEQ), bass.ds(g8 * (HG * VW), HG * VW)].rearrange("(j p) w -> p j w", p=P)
                sp.dma_start(v_sb[r][:, :, :], src_v).then_inc(done, 16)

            def max_rows(n, r):
                sp.wait_ge(m_lo_done, n + 1)
                at = q_st[r]
                for i, src in enumerate((m_hi, m_lo)):
                    row = SCORE_ROWS + i
                    sp.dma_start(at[row:row + 1, :, :].bitcast(F32), src[r % 2][:, :].bitcast(F32)).then_inc(m_loaded[r % 2], 16)

            def store(n, r):
                sp.wait_ge(o_done, n + 1)
                out = o_dram[bass.ds((n // 8) * SEQ, SEQ), bass.ds(((n % 8) // 2) * P, P)].rearrange("(i p) w -> p i w", p=P)
                sp.dma_start(out, o_sb[(r // 2) % 2][:, :, :]).then_inc(o_stored[(r // 2) % 2], 16)

            for n in range(3):
                load(n, n)
            max_rows(0, 0)

            def step(n, r):
                if not is_last(n, 3):
                    load(n + 3, (r + 3) % 4)
                if not is_last(n):
                    max_rows(n + 1, (r + 1) % 4)
                if not is_first(n) and r % 2 == 0:
                    store(n - 1, (r - 1) % 4)
            group_loop(sp, step)
            store(NG - 1, 3)
            for i in range(2):
                sp.wait_ge(o_stored[i], 16 * (NG // 4))

        @block.gpsimd
        def _(pool):
            nc.gpsimd.memset(ident[:, :], 0.0).then_inc(zeroed, 1)
            nc.gpsimd.memset(ident_bf[:, :], 0.0).then_inc(zeroed, 1)
            nc.gpsimd.memset(mask[:, :, :], 0.0).then_inc(zeroed, 1)
            nc.gpsimd.memset(mask_t[:, :, :], 0.0).then_inc(zeroed, 1)
            pool.wait_ge(zeroed, 4)
            for a in (ident, ident_bf):
                nc.gpsimd.affine_select(out=a[:, :], in_=a[:, :], compare_op=ALU.not_equal, fill=1.0, base=0,
                                        pattern=[[-1, P]], channel_multiplier=1).then_inc(const_done, 1)
            nc.gpsimd.affine_select(out=mask[:, :, :], in_=mask[:, :, :], compare_op=ALU.is_ge, fill=NEG, base=0,
                                    pattern=[[0, HG], [-1, P]], channel_multiplier=1).then_inc(const_done, 1)
            nc.gpsimd.affine_select(out=mask_t[:, :, :], in_=mask_t[:, :, :], compare_op=ALU.is_ge, fill=NEG, base=0,
                                    pattern=[[0, 2], [1, P]], channel_multiplier=-1).then_inc(const_done, 1)

        @block.tensor
        def _(pe):
            pe.wait_ge(const_done, 4)

            def scores(n, r, u):
                i, heads, w = stack_unit(u)
                bank = s_ps[(S_UNITS * r + u) % 2]
                if u == 0:
                    pe.wait_ge(stack_loaded[r], 16 * LOADS * (n // 4 + 1))
                at_least(pe, max_done, S_UNITS * n + u - 1)
                k = len(heads)
                diag = bank[:, 0:k * w].rearrange("p (h w) -> p h w", h=k)[:, :, i * P:(i + 1) * P]
                nc.tensor.matmul(diag, ident_bf[:, :], mask[:, 0:k, :], start=True, stop=False, skip_group_check=True)
                for a, h in enumerate(heads):
                    last = nc.tensor.matmul(bank[:, a * w:(a + 1) * w], q_st[r][0:SCORE_ROWS, h, i * P:(i + 1) * P],
                                            k_st[r][0:SCORE_ROWS, h, 0:w], start=False, stop=(a == k - 1),
                                            skip_group_check=True)
                last.then_inc(s_done, 1)

            def turn_max(n, r):
                pe.wait_ge(max_done, S_UNITS * (n + 1))
                at_least(pe, o_done, n - 1)
                if isinstance(n, int) and n == 1:
                    pe.wait_ge(m_lo_done, 1)
                for i in range(QT):
                    last = nc.tensor.transpose(x_ps[0:HG, i * P:(i + 1) * P], nmax[r % 2][:, i, :], ident[:, :])
                last.then_inc(mT_done, 1)

            def scores_by_key(n, r, u):
                bank = st_ps[(T_UNITS * r + u) % 2]
                if u == 0:
                    pe.wait_ge(m_loaded[r % 2], 32 * (n // 2 + 1))
                at_least(pe, exp_done, T_UNITS * n + u - 1)
                todo = [(u, 0, 0), (u, 1, 512), (u, 3, 896)] if u < 4 else [(h, 2, 256 * h) for h in range(HG)]
                if u < 4:
                    diags = [bank[:, 0:P], bank[:, 512:1024].rearrange("p (a w) -> p a w", a=4)[:, 0:4:3, :]]
                else:
                    diags = [bank[:, 512 * a:512 * (a + 1)].rearrange("p (h w) -> p h w", h=2)[:, :, 0:P] for a in range(2)]
                for d in diags:
                    rhs = mask_t[:, 0, :] if len(d.shape) == 2 else mask_t[:, :, :]
                    nc.tensor.matmul(d, ident_bf[:, :], rhs, start=True, stop=False, skip_group_check=True)
                for h, j, col in todo:
                    w = SEQ - j * P
                    last = nc.tensor.matmul(bank[:, col:col + w], k_st[r][0:FULL_ROWS, h, j * P:(j + 1) * P],
                                            q_st[r][0:FULL_ROWS, h, j * P:SEQ], start=False, stop=True,
                                            skip_group_check=True)
                last.then_inc(st_done, 1)

            def values(n, r):
                pe.wait_ge(exp_done, T_UNITS * (n + 1))
                at_least(pe, oT_done, n)
                for j in range(QT):
                    for h in range(HG):
                        w = SEQ - j * P
                        col = prob_cols(h, j)
                        last = nc.tensor.matmul(pv_ps[VW * h:VW * (h + 1), j * P:SEQ], v_sb[r][:, j, VW * h:VW * (h + 1)],
                                                prob[r % 2][:, col:col + w], start=(j == 0), stop=(j == QT - 1))
                last.then_inc(pv_done, 1)

            def turn_out(n, r):
                pe.wait_ge(oT_done, n + 1)
                if isinstance(n, int) and n + 1 >= NG:
                    pe.wait_ge(o_done, n)
                else:
                    pe.wait_ge(m_lo_done, n + 2)
                for i in range(QT):
                    last = nc.tensor.transpose(x_ps[:, i * P:(i + 1) * P], oT[r % 2][:, i * P:(i + 1) * P], ident[:, :])
                last.then_inc(turn_done, 1)

            for u in range(S_UNITS):
                scores(0, 0, u)
            turn_max(0, 0)

            def step(n, r):
                rn, rp = (r + 1) % 4, (r - 1) % 4
                more = not is_last(n)
                for item in ("S0 S1 S2 PV S3 T0 S4 T1 S5 OT T2 S6 T3 S7 T4 S8 S9 S10 MT").split():
                    kind, u = item[0], item[1:]
                    if kind == "S" and more:
                        scores(n + 1, rn, int(u))
                    elif kind == "T":
                        scores_by_key(n, r, int(u))
                    elif kind == "P" and not is_first(n):
                        values(n - 1, rp)
                    elif kind == "O" and not is_first(n):
                        turn_out(n - 1, rp)
                    elif kind == "M" and more:
                        turn_max(n + 1, rn)
            group_loop(pe, step)
            values(NG - 1, 3)
            turn_out(NG - 1, 3)

        @block.scalar
        def _(act):
            def max_hi(n, r):
                act.wait_ge(mT_done, n + 1)
                at_least(act, m_loaded[r % 2], 32 * (n // 2))
                nc.scalar.activation(m_hi[r % 2][:, :], x_ps[0:HG, :], ACT.Copy).then_inc(m_hi_done, 1)

            def exps(n, r, u):
                act.wait_ge(st_done, T_UNITS * n + u + 1)
                if u == 0:
                    at_least(act, pv_done, n - 1)
                nc.scalar.activation(prob[r % 2][:, 1024 * u:1024 * (u + 1)], st_ps[(T_UNITS * r + u) % 2][:, :],
                                     ACT.Exp).then_inc(exp_done, 1)

            def out_copy(n, r):
                act.wait_ge(pv_done, n + 1)
                at_least(act, turn_done, n)
                nc.scalar.activation(oT[r % 2][:, :], pv_ps[:, :], ACT.Copy).then_inc(oT_done, 1)

            max_hi(0, 0)

            def step(n, r):
                if not is_first(n):
                    out_copy(n - 1, (r - 1) % 4)
                for u in range(T_UNITS):
                    exps(n, r, u)
                if not is_last(n):
                    max_hi(n + 1, (r + 1) % 4)
            group_loop(act, step)
            out_copy(NG - 1, 3)

        @block.vector
        def _(dve):
            def reduce(n, r, u):
                i, heads, w = stack_unit(u)
                k = len(heads)
                dve.wait_ge(s_done, S_UNITS * n + u + 1)
                if u == 0:
                    at_least(dve, mT_done, n - 1)
                nc.vector.tensor_reduce(nmax[r % 2][:, i, heads[0]:heads[0] + k],
                                        s_ps[(S_UNITS * r + u) % 2][:, 0:k * w].rearrange("p (h w) -> p h w", h=k),
                                        X_AXIS, ALU.max, negate=True).then_inc(max_done, 1)

            def max_lo(n, r):
                dve.wait_ge(m_hi_done, n + 1)
                nc.vector.tensor_tensor(m_lo[r % 2][:, :], x_ps[0:HG, :], m_hi[r % 2][:, :].bitcast(F32),
                                        ALU.subtract).then_inc(m_lo_done, 1)

            def normalise(n, r):
                dve.wait_ge(turn_done, n + 1)
                turned = x_ps[:, :].rearrange("p (i h w) -> p i h w", i=QT, h=HG)
                nc.vector.reciprocal(rden[:, :, :, 0], turned[:, :, :, HD]).then_inc(rden_done, 1)
                dve.wait_ge(rden_done, n + 1)
                half = r % 2
                slot = (r // 2) % 2
                if half == 0:
                    at_least(dve, o_stored[slot], 16 * (n // 4))
                out = o_sb[slot][:, :, half * HG * HD:(half + 1) * HG * HD].rearrange("p i (h d) -> p i h d", h=HG)
                nc.vector.tensor_tensor(out, turned[:, :, :, 0:HD], rden[:, :, :, :].to_broadcast([P, QT, HG, HD]),
                                        ALU.mult).then_inc(o_done, 1)

            for u in range(S_UNITS):
                reduce(0, 0, u)
            max_lo(0, 0)

            def step(n, r):
                more = not is_last(n)
                rn = (r + 1) % 4
                for u in range(S_UNITS):
                    if more:
                        reduce(n + 1, rn, u)
                    if u == 5 and not is_first(n):
                        normalise(n - 1, (r - 1) % 4)
                if more:
                    max_lo(n + 1, rn)
            group_loop(dve, step)
            normalise(NG - 1, 3)



SLOT_TILES = 2 * TOKENS // P + E - 1
TAB = SLOT_TILES + 1


class Experts:

    def __init__(self, nc, ctx, prefix):
        m = Memory(nc, ctx, prefix)
        self.w_hi = m.sb("w_hi", [P, E * C, D], F32R)
        self.w_lo = m.sb("w_lo", [P, E * C, D], F32R)
        self.token_of = m.sb("token_of", [P, TAB], I32)
        self.row_of = m.sb("row_of", [P, TAB], I32)
        self.expert_of = m.sb("expert_of", [1, TAB], I32)


def ring_loop(engine, step, total, ring, first):
    for t in range(first):
        step(t, t % ring)
    turns = (total - first - 1) // ring
    with engine.Fori(0, turns) as i:
        for k in range(ring):
            step(first + ring * i + k, (first + k) % ring)
    for t in range(first + turns * ring, total):
        step(t, t % ring)


def known(t, limit):
    return isinstance(t, int) and t >= limit


def route_block(nc, prefix, ex, x_in, xn_dram, acc, w_gate, b_gate, w_e, o_dram=None, w_out=None):
    proj = o_dram is not None
    with ExitStack() as ctx:
        m = Memory(nc, ctx, prefix)
        w_stage = [m.sb(f"w_stage{i}", [P, 2, D]) for i in range(2)]
        g_raw = m.sb("g_raw", [P, C, E])
        g_hi = m.sb("g_hi", [P, C, E], F32R)
        g_lo = m.sb("g_lo", [P, C, E], F32R)
        bg_bc = m.sb("bg_bc", [P, E])
        ident = m.sb("ident", [P, P])
        x = [m.sb(f"x{i}", [P, D]) for i in range(2)]
        xn = [m.sb(f"xn{i}", [P, D]) for i in range(2)]
        xT_hi = m.sb("xT_hi", [P, C * P], F32R)
        xT_lo = m.sb("xT_lo", [P, C * P], F32R)
        ln = m.ln()
        t_ps = [m.ps(f"t_ps{i}") for i in range(2)]
        g_ps = m.ps("g_ps")
        rank_ps, total_ps, id_ps = m.ps("rank_ps"), m.ps("total_ps"), m.ps("id_ps")
        if proj:
            wo_hi = m.sb("wo_hi", [P, C, D], F32R)
            wo_lo = m.sb("wo_lo", [P, C, D], F32R)
            o = [m.sb(f"o{i}", [P, D]) for i in range(2)]
            oT_hi = m.sb("oT_hi", [P, C * P], F32R)
            oT_lo = m.sb("oT_lo", [P, C * P], F32R)
            y_ps = m.ps("y_ps")
        TE = TILES * E
        n_expert = m.sb("n_expert", [P, TILES, E])
        n_full = m.sb("n_full", [P, E, TILES])
        n_col = m.sb("n_col", [P, P], BF16)
        n_tile = m.sb("n_tile", [P, TAB], BF16)
        n_token_tile = m.sb("n_token_tile", [P, 2 * TILES], BF16)
        n_part = m.sb("n_part", [P, 1])
        n_slot_tile = m.sb("n_slot_tile", [1, TAB, E])
        ones8 = m.sb("ones8", [P, E])
        ones_bf = m.sb("ones_bf", [P, P], BF16)
        before = m.sb("before", [P, P], BF16)
        logits = m.sb("logits", [P, TILES, E])
        eq = m.sb("eq", [P, TILES, E])
        val = m.sb("val", [P, TILES, E])
        rest = m.sb("rest", [P, TILES, E])
        best = m.sb("best", [P, TILES, 1])
        low = m.sb("low", [P, TILES, 1])
        pick = [m.sb(f"pick{i}", [P, TILES, E]) for i in range(2)]
        picked = m.sb("picked", [P, TE], BF16)
        over = m.sb("over", [P, E, TILES])
        n_tiles = m.sb("n_tiles", [P, E])
        ends = m.sb("ends", [P, E])
        begins = m.sb("begins", [P, E])
        slot_e = m.sb("slot_e", [P, TILES, E])
        slot_m = m.sb("slot_m", [P, TILES, E])
        slot = m.sb("slot", [P, 2, TILES])
        slot_i = m.sb("slot_i", [P, 2 * TILES], I32)
        slot_hi_i = m.sb("slot_hi_i", [P, 2 * TILES], I32)
        slot_lo_i = m.sb("slot_lo_i", [P, 2 * TILES], I32)
        slot_hi = m.sb("slot_hi", [P, 2 * TILES, 1], BF16)
        slot_lo = m.sb("slot_lo", [P, 2 * TILES])
        at_col = m.sb("at_col", [P, 2 * TILES, P], BF16)
        at_tile = m.sb("at_tile", [P, 2 * TILES, 3, TAB], BF16)
        found = m.sb("found", [P, 3, TAB])
        empty = m.sb("empty", [P, TAB])
        past = m.sb("past", [1, TAB, E])
        exp_f = m.sb("exp_f", [1, TAB, 1])

        w_loaded = [m.sem(f"w_loaded{i}") for i in range(2)]
        w_hi_done, w_lo_done = m.sem("w_hi_done"), m.sem("w_lo_done")
        g_loaded, bias_loaded, g_hi_done, g_lo_done = (m.sem(n) for n in ("g_loaded", "bias_loaded", "g_hi_done", "g_lo_done"))
        zeroed, ident_done, const_done = m.sem("zeroed"), m.sem("ident_done"), m.sem("const_done")
        x_loaded = [m.sem(f"x_loaded{i}") for i in range(2)]
        x_stored = [m.sem(f"x_stored{i}") for i in range(2)]
        xn_stored = [m.sem(f"xn_stored{i}") for i in range(2)]
        acc_set = m.sem("acc_set")
        xn_done, tr_done, hi_done, lo_done = (m.sem(n) for n in ("xn_done", "tr_done", "hi_done", "lo_done"))
        gate_done, logits_done = m.sem("gate_done"), m.sem("logits_done")
        o_tr, o_hi, o_lo, y_done, sum_done = (m.sem(n) for n in ("o_tr", "o_hi", "o_lo", "y_done", "sum_done"))
        ln_chain, chain_sem, passed = m.sem("ln_chain"), m.sem("chain"), m.sem("passed")
        picked_done, rank_done, onehot_done, ids_done = (m.sem(n) for n in ("picked_done", "rank_done", "onehot_done", "ids_done"))
        wprep = load_transposed_weight(nc, m, w_out, C, wo_hi, wo_lo, ident, ident_done, t_ps) if proj else None
        block = ctx.enter_context(nc.Block())
        FIRST = 4

        def stages(t, lead, main, mid, tail):
            if not known(t, TILES - 1):
                lead(t + 1)
            main(t)
            if not isinstance(t, int) or t >= 1:
                mid(t - 1)
            if not isinstance(t, int) or t >= 2:
                tail(t - 2)

        def nothing(*_):
            pass

        @block.sync
        def _(sp):
            def load(t, par):
                at_least(sp, xn_done, t - 1)
                if proj:
                    at_least(sp, x_stored[par], 16 * (t // 2))
                    sp.dma_start(o[par][:, :], rows(o_dram, t)).then_inc(x_loaded[par], 16)
                sp.dma_start(x[par][:, :], rows(x_in, t)).then_inc(x_loaded[par], 16)

            load(0, 0)
            load(1, 1)
            sp.dma_start(g_raw[:, :, :], w_gate.rearrange("(c p) e -> p c e", p=P)).then_inc(g_loaded, 16)
            sp.dma_start(bg_bc[:, :], b_gate.rearrange("(a e) -> a e", a=1).to_broadcast([P, E])).then_inc(bias_loaded, 16)
            sp.dma_start(acc[TOKENS:TOKENS + P, :], x_in[0:P, :]).then_inc(acc_set, 16)
            if proj:
                wprep["sync"](sp)

            def weights(n):
                if n >= 2:
                    sp.wait_ge(w_lo_done, n - 1)
                sp.dma_start(w_stage[n % 2][:, :, :], w_e[n // 2, (n % 2) * 2 * P:(n % 2 + 1) * 2 * P, :]
                             .rearrange("(c p) h -> p c h", p=P)).then_inc(w_loaded[n % 2], 16)

            def step(t, par):
                if proj:
                    sp.wait_ge(sum_done, t + 1)
                    sp.dma_start(rows(acc, t), x[par][:, :]).then_inc(x_stored[par], 16)
                sp.wait_ge(xn_done, t + 1)
                sp.dma_start(rows(xn_dram, t), xn[par][:, :]).then_inc(xn_stored[par], 16)
                if not known(t, TILES - 2):
                    load(t + 2, par)

            for t in range(TILES):
                weights(t)
                step(t, t % 2)
            if not proj:
                sp.dma_start(acc[0:TOKENS, :], x_in[:, :]).then_inc(acc_set, 16)
            sp.wait_ge(acc_set, 16 if proj else 32)
            sp.wait_ge(bias_loaded, 16)
            for par in range(2):
                sp.wait_ge(xn_stored[par], 16 * (TILES // 2))
                if proj:
                    sp.wait_ge(x_stored[par], 16 * (TILES // 2))

        @block.gpsimd
        def _(pool):
            make_identity(nc, pool, ident, zeroed, ident_done)
            small = dict(base=0, allow_small_or_imprecise_dtypes=True)
            nc.gpsimd.iota(n_expert[:, :, :], [[0, TILES], [1, E]], channel_multiplier=0, **small).then_inc(const_done, 1)
            nc.gpsimd.iota(n_full[:, :, :], [[0, E], [P, TILES]], channel_multiplier=0, **small).then_inc(const_done, 1)
            nc.gpsimd.iota(n_col[:, :], [[1, P]], channel_multiplier=0, **small).then_inc(const_done, 1)
            nc.gpsimd.iota(n_tile[:, :], [[1, TAB]], channel_multiplier=0, **small).then_inc(const_done, 1)
            nc.gpsimd.iota(n_token_tile[:, :], [[0, 2], [1, TILES]], channel_multiplier=0, **small).then_inc(const_done, 1)
            nc.gpsimd.iota(n_part[:, :], [[0, 1]], channel_multiplier=1, **small).then_inc(const_done, 1)
            nc.gpsimd.iota(n_slot_tile[:, :, :], [[1, TAB], [0, E]], channel_multiplier=0, **small).then_inc(const_done, 1)
            nc.gpsimd.memset(ones8[:, :], 1.0).then_inc(const_done, 1)
            nc.gpsimd.memset(ones_bf[:, :], 1.0).then_inc(const_done, 1)
            pool.wait_ge(const_done, 9)
            nc.gpsimd.affine_select(out=before[:, :], in_=ones_bf[:, :], compare_op=ALU.is_gt, fill=0.0, base=0,
                                    pattern=[[1, P]], channel_multiplier=-1).then_inc(const_done, 1)

        @block.tensor
        def _(pe):
            if proj:
                wprep["tensor"](pe)
                sem, count = wprep["done"]
                pe.wait_ge(sem, count)
            pe.wait_ge(ident_done, 1)
            pe.wait_ge(g_lo_done, 1)

            def o_transpose(t, par):
                pe.wait_ge(x_loaded[par], 32 * (t // 2 + 1))
                at_least(pe, o_lo, t)
                for c in range(C):
                    last = nc.tensor.transpose(t_ps[0][:, c * P:(c + 1) * P], o[par][:, c * P:(c + 1) * P], ident[:, :])
                last.then_inc(o_tr, 1)

            def out_proj(t):
                pe.wait_ge(o_lo, t + 1)
                at_least(pe, sum_done, t)
                split_matmuls(nc, y_ps[:, :], oT_hi, oT_lo, lambda c: wo_hi[:, c, :], lambda c: wo_lo[:, c, :]).then_inc(y_done, 1)

            def transpose(t, par):
                pe.wait_ge(xn_done, t + 1)
                at_least(pe, lo_done, t)
                for c in range(C):
                    last = nc.tensor.transpose(t_ps[1][:, c * P:(c + 1) * P], xn[par][:, c * P:(c + 1) * P], ident[:, :])
                last.then_inc(tr_done, 1)

            def gate(t):
                pe.wait_ge(lo_done, t + 1)
                at_least(pe, logits_done, t)
                split_matmuls(nc, g_ps[:, 0:E], xT_hi, xT_lo, lambda c: g_hi[:, c, :],
                              lambda c: g_lo[:, c, :]).then_inc(gate_done, 1)

            if proj:
                o_transpose(0, 0)

            def step(t, par):
                if proj:
                    out_proj(t)
                    if not known(t, TILES - 1):
                        o_transpose(t + 1, 1 - par)
                if not isinstance(t, int) or t >= 1:
                    transpose(t - 1, 1 - par)
                    gate(t - 1)
            ring_loop(pe, step, TILES, 2, FIRST)
            transpose(TILES - 1, 1)
            gate(TILES - 1)

            pe.wait_ge(const_done, 10)
            pe.wait_ge(picked_done, 1)
            nc.tensor.matmul(rank_ps[:, 0:TE], before[:, :], picked[:, :], start=True, stop=False, skip_group_check=True)
            for s in range(1, TILES):
                last = nc.tensor.matmul(rank_ps[:, s * E:TE], ones_bf[:, :], picked[:, 0:TE - s * E], start=False,
                                        stop=(s == TILES - 1), skip_group_check=True)
            for s in range(TILES):
                last = nc.tensor.matmul(total_ps[:, 0:E], ones_bf[:, :], picked[:, s * E:(s + 1) * E],
                                        start=(s == 0), stop=(s == TILES - 1))
            last.then_inc(rank_done, 1)
            for n in range(2 * TILES):
                pe.wait_ge(onehot_done, n + 1)
                last = nc.tensor.matmul(id_ps[:, 0:3 * TAB], at_col[:, n, :], at_tile[:, n, :, :].rearrange("p a s -> p (a s)"),
                                        start=(n == 0), stop=(n == 2 * TILES - 1))
            last.then_inc(ids_done, 1)

        @block.scalar
        def _(act):
            if proj:
                wprep["scalar"](act)
            act.wait_ge(g_loaded, 16)
            nc.scalar.activation(g_hi[:, :, :], g_raw[:, :, :], ACT.Copy).then_inc(g_hi_done, 1)

            def o_split(t, par):
                act.wait_ge(o_tr, t + 1)
                at_least(act, y_done, t)
                nc.scalar.activation(oT_hi[:, :], t_ps[0][:, :], ACT.Copy).then_inc(o_hi, 1)

            def hi(t):
                act.wait_ge(tr_done, t + 1)
                at_least(act, gate_done, t)
                nc.scalar.activation(xT_hi[:, :], t_ps[1][:, :], ACT.Copy).then_inc(hi_done, 1)

            def weights(n):
                act.wait_ge(w_loaded[n % 2], 16 * (n // 2 + 1))
                nc.scalar.activation(ex.w_hi[:, 2 * n:2 * n + 2, :], w_stage[n % 2][:, :, :], ACT.Copy).then_inc(w_hi_done, 1)

            if proj:
                o_split(0, 0)
            for t in range(TILES):
                if proj and t + 1 < TILES:
                    o_split(t + 1, (t + 1) % 2)
                weights(t)
                if t >= 1:
                    hi(t - 1)
            hi(TILES - 1)

        @block.vector
        def _(dve):
            if proj:
                wprep["vector"](dve)

            def o_rest(t):
                dve.wait_ge(o_hi, t + 1)
                nc.vector.tensor_tensor(oT_lo[:, :], t_ps[0][:, :], oT_hi[:, :].bitcast(F32), ALU.subtract).then_inc(o_lo, 1)

            def add_x(t, par):
                dve.wait_ge(y_done, t + 1)
                nc.vector.tensor_tensor(x[par][:, :], y_ps[:, :], x[par][:, :], ALU.add).then_inc(sum_done, 1)
                dve.wait_ge(sum_done, t + 1)

            def norm(t, par):
                at_least(dve, tr_done, t - 1)
                at_least(dve, xn_stored[par], 16 * (t // 2))
                dve.wait_ge(x_loaded[par], (32 if proj else 16) * (t // 2 + 1))
                chain = Chain(dve, ln_chain, LN_LINKS * t, passed)
                layernorm_steps(nc, chain, x[par][:, :], xn[par][:, :], ln).then_inc(xn_done, 1)

            def lo(t):
                dve.wait_ge(hi_done, t + 1)
                nc.vector.tensor_tensor(xT_lo[:, :], t_ps[1][:, :], xT_hi[:, :].bitcast(F32), ALU.subtract).then_inc(lo_done, 1)

            def keep_logits(t):
                dve.wait_ge(gate_done, t + 1)
                nc.vector.tensor_tensor(logits[:, t, :], g_ps[:, 0:E], bg_bc[:, :], ALU.add).then_inc(logits_done, 1)

            def weights(n):
                dve.wait_ge(w_hi_done, n + 1)
                nc.vector.tensor_tensor(ex.w_lo[:, 2 * n:2 * n + 2, :], w_stage[n % 2][:, :, :],
                                        ex.w_hi[:, 2 * n:2 * n + 2, :].bitcast(F32), ALU.subtract).then_inc(w_lo_done, 1)

            dve.wait_ge(g_hi_done, 1)
            nc.vector.tensor_tensor(g_lo[:, :, :], g_raw[:, :, :], g_hi[:, :, :].bitcast(F32), ALU.subtract).then_inc(g_lo_done, 1)
            dve.wait_ge(bias_loaded, 16)
            if proj:
                o_rest(0)
            for t in range(TILES):
                if proj:
                    add_x(t, t % 2)
                norm(t, t % 2)
                if proj and t + 1 < TILES:
                    o_rest(t + 1)
                weights(t)
                if t >= 1:
                    lo(t - 1)
                    keep_logits(t - 1)
            lo(TILES - 1)
            keep_logits(TILES - 1)

            chain = Chain(dve, chain_sem)
            dve.wait_ge(const_done, 10)
            dve.wait_ge(logits_done, TILES)
            three = [P, TILES, E]
            for k, source in enumerate((logits, rest)):
                chain(nc.vector.tensor_reduce(best[:, :, 0], source[:, :, :], X_AXIS, ALU.max))
                chain(nc.vector.tensor_tensor(eq[:, :, :], source[:, :, :], best[:, :, :].to_broadcast(three), ALU.is_equal))
                chain(nc.vector.scalar_tensor_tensor(val[:, :, :], eq[:, :, :], -100.0, n_expert[:, :, :], ALU.mult, ALU.add))
                chain(nc.vector.tensor_reduce(low[:, :, 0], val[:, :, :], X_AXIS, ALU.min))
                chain(nc.vector.tensor_tensor(pick[k][:, :, :], val[:, :, :], low[:, :, :].to_broadcast(three), ALU.is_equal))
                if k == 0:
                    chain(nc.vector.scalar_tensor_tensor(rest[:, :, :], pick[0][:, :, :], NEG, logits[:, :, :], ALU.mult, ALU.add))
            flat = "p t e -> p (t e)"
            nc.vector.tensor_tensor(picked[:, :], pick[0][:, :, :].rearrange(flat), pick[1][:, :, :].rearrange(flat),
                                    ALU.add).then_inc(picked_done, 1)
            dve.wait_ge(rank_done, 1)
            chain(nc.vector.tensor_tensor(over[:, :, :], total_ps[:, 0:E].rearrange("p (e a) -> p e a", a=1).to_broadcast([P, E, TILES]),
                                          n_full[:, :, :], ALU.is_gt))
            chain(nc.vector.tensor_reduce(n_tiles[:, :], over[:, :, :], X_AXIS, ALU.add))
            chain(nc.vector.tensor_tensor_scan(ends[:, :], ones8[:, :], n_tiles[:, :], 0.0, ALU.mult, ALU.add))
            chain(nc.vector.tensor_tensor(begins[:, :], ends[:, :], n_tiles[:, :], ALU.subtract))
            begin_all = begins[:, :].rearrange("p (a e) -> p a e", a=1).to_broadcast(three)
            chain(nc.vector.scalar_tensor_tensor(slot_e[:, :, :], begin_all, float(P),
                                                 rank_ps[:, 0:TE].rearrange("p (t e) -> p t e", e=E), ALU.mult, ALU.add))
            for k in range(2):
                chain(nc.vector.tensor_tensor(slot_m[:, :, :], pick[k][:, :, :], slot_e[:, :, :], ALU.mult))
                chain(nc.vector.tensor_reduce(slot[:, k, :], slot_m[:, :, :], X_AXIS, ALU.add))
            chain(nc.vector.tensor_copy(slot_i[:, :], slot[:, :, :].rearrange("p k t -> p (k t)")))
            chain(nc.vector.tensor_scalar(slot_hi_i[:, :], slot_i[:, :], 7, None, ALU.arith_shift_right))
            chain(nc.vector.tensor_scalar(slot_lo_i[:, :], slot_i[:, :], P - 1, None, ALU.bitwise_and))
            chain(nc.vector.tensor_copy(slot_hi[:, :, 0], slot_hi_i[:, :]))
            chain(nc.vector.tensor_copy(slot_lo[:, :], slot_lo_i[:, :]))
            every = [P, 2 * TILES, TAB]
            chain(nc.vector.tensor_tensor(at_tile[:, :, 0, :], slot_hi[:, :, :].to_broadcast(every),
                                          n_tile[:, :].rearrange("p (a s) -> p a s", a=1).to_broadcast(every), ALU.is_equal))
            chain(nc.vector.tensor_scalar(at_tile[:, :, 1, :], at_tile[:, :, 0, :], n_part[:, :], None, ALU.mult))
            chain(nc.vector.tensor_tensor(at_tile[:, :, 2, :], at_tile[:, :, 0, :],
                                          n_token_tile[:, :].rearrange("p (n a) -> p n a", a=1).to_broadcast(every), ALU.mult))
            for n in range(2 * TILES):
                nc.vector.tensor_scalar(at_col[:, n, :], n_col[:, :], slot_lo[:, n:n + 1], None,
                                        ALU.is_equal).then_inc(onehot_done, 1)
            chain(nc.vector.tensor_tensor(past[:, :, :], ends[0:1, :].rearrange("p (a e) -> p a e", a=1).to_broadcast([1, TAB, E]),
                                          n_slot_tile[:, :, :], ALU.is_le))
            chain(nc.vector.tensor_reduce(exp_f[:, :, 0], past[:, :, :], X_AXIS, ALU.add))
            chain(nc.vector.tensor_scalar(ex.expert_of[:, :], exp_f[:, :, 0], float(E - 1), None, ALU.min))
            dve.wait_ge(ids_done, 1)
            chain(nc.vector.tensor_copy(found[:, :, :], id_ps[:, 0:3 * TAB].rearrange("p (a s) -> p a s", a=3)))
            chain(nc.vector.scalar_tensor_tensor(found[:, 1, :], found[:, 2, :], float(P), found[:, 1, :], ALU.mult, ALU.add))
            chain(nc.vector.tensor_copy(ex.token_of[:, :], found[:, 1, :]))
            chain(nc.vector.tensor_scalar(empty[:, :], found[:, 0, :], -1.0, 1.0, ALU.mult, ALU.add))
            chain(nc.vector.tensor_scalar(found[:, 2, :], empty[:, :], n_part[:, :], None, ALU.mult))
            chain(nc.vector.scalar_tensor_tensor(found[:, 1, :], empty[:, :], float(TOKENS), found[:, 1, :], ALU.mult, ALU.add))
            chain(nc.vector.tensor_tensor(ex.row_of[:, :], found[:, 1, :], found[:, 2, :], ALU.add))


def expert_block(nc, prefix, ex, xn_dram, acc, b_e, out=None):
    with ExitStack() as ctx:
        m = Memory(nc, ctx, prefix)
        RING = 4
        ident = m.sb("ident", [P, P])
        bias = m.sb("bias", [P, E * D])
        xg = [m.sb(f"xg{i}", [P, D]) for i in range(RING)]
        xT_hi = [m.sb(f"xT_hi{i}", [P, C * P], F32R) for i in range(2)]
        xT_lo = [m.sb(f"xT_lo{i}", [P, C * P], F32R) for i in range(2)]
        z = [m.sb(f"z{i}", [P, D]) for i in range(2)]
        y = [m.sb(f"y{i}", [P, D]) for i in range(RING)]
        t_ps = [m.ps(f"t_ps{i}") for i in range(2)]
        z_ps = [m.ps(f"z_ps{i}") for i in range(2)]
        zeroed, ident_done = m.sem("zeroed"), m.sem("ident_done")
        gathered = [m.sem(f"gathered{i}") for i in range(RING)]
        added = m.sem("added")
        tr_done, hi_done, lo_done, z_done, zb_done, y_done = (
            m.sem(n) for n in ("tr_done", "hi_done", "lo_done", "z_done", "zb_done", "y_done"))
        copied, bias_loaded = m.sem("copied"), m.sem("bias_loaded")
        block = ctx.enter_context(nc.Block())
        N = SLOT_TILES
        FIRST = 4

        @block.gpsimd
        def _(pool):
            def gather(s):
                if s >= RING:
                    pool.wait_ge(tr_done, s - RING + 1)
                nc.gpsimd.indirect_dma_start(out=xg[s % RING][:, :], out_offset=None, in_=xn_dram[:, :],
                                             in_offset=bass.IndirectOffsetOnAxis(ap=ex.token_of[:, s:s + 1], axis=0)
                                             ).then_inc(gathered[s % RING], 16)
            gather(0)
            make_identity(nc, pool, ident, zeroed, ident_done)
            gather(1)
            gather(2)
            for s in range(N):
                if s + 3 < N:
                    gather(s + 3)
                pool.wait_ge(y_done, s + 1)
                if s >= 1:
                    pool.wait_ge(added, 16 * s)
                nc.gpsimd.indirect_dma_start(out=acc[:, :], out_offset=bass.IndirectOffsetOnAxis(ap=ex.row_of[:, s:s + 1], axis=0),
                                             in_=y[s % RING][:, :], in_offset=None, compute_op=ALU.add).then_inc(added, 16)
            pool.wait_ge(added, 16 * N)

        @block.sync
        def _(sp):
            sp.dma_start(bias[:, :], b_e.rearrange("(a e) h -> a (e h)", a=1).to_broadcast([P, E * D])).then_inc(bias_loaded, 16)
            sp.wait_ge(bias_loaded, 16)
            if out is not None:
                sp.wait_ge(added, 16 * N)
                sp.dma_start(out, acc[0:TOKENS, :]).then_inc(copied, 16)
                sp.wait_ge(copied, 16)

        @block.tensor
        def _(pe):
            pe.wait_ge(ident_done, 1)

            def transpose(s, r):
                pe.wait_ge(gathered[r], 16 * (s // RING + 1))
                at_least(pe, lo_done, s - 1)
                for c in range(C):
                    last = nc.tensor.transpose(t_ps[r % 2][:, c * P:(c + 1) * P], xg[r][:, c * P:(c + 1) * P], ident[:, :])
                last.then_inc(tr_done, 1)
            transpose(0, 0)

            def step(s, r):
                if not known(s, N - 1):
                    transpose(s + 1, (r + 1) % RING)
                expert = pe.value_load(ex.expert_of[0:1, bass.ds(s, 1)], min_val=0, max_val=E - 1)
                pe.wait_ge(lo_done, s + 1)
                at_least(pe, zb_done, s - 1)
                split_matmuls(nc, z_ps[r % 2][:, :], xT_hi[r % 2], xT_lo[r % 2],
                              lambda c: ex.w_hi[:, bass.ds(expert * C + c, 1), :].rearrange("p a n -> p (a n)"),
                              lambda c: ex.w_lo[:, bass.ds(expert * C + c, 1), :].rearrange("p a n -> p (a n)")).then_inc(z_done, 1)
            ring_loop(pe, step, N, RING, FIRST)

        @block.scalar
        def _(act):
            def hi(s, r):
                act.wait_ge(tr_done, s + 1)
                at_least(act, z_done, s - 1)
                nc.scalar.activation(xT_hi[r % 2][:, :], t_ps[r % 2][:, :], ACT.Copy).then_inc(hi_done, 1)
            hi(0, 0)

            def step(s, r):
                if not known(s, N - 1):
                    hi(s + 1, (r + 1) % RING)
                act.wait_ge(zb_done, s + 1)
                at_least(act, added, 16 * (s - RING + 1))
                nc.scalar.activation(y[r][:, :], z[r % 2][:, :], ACT.Relu, scale=0.25).then_inc(y_done, 1)
            ring_loop(act, step, N, RING, FIRST)

        @block.vector
        def _(dve):
            def lo(s, r):
                dve.wait_ge(hi_done, s + 1)
                nc.vector.tensor_tensor(xT_lo[r % 2][:, :], t_ps[r % 2][:, :], xT_hi[r % 2][:, :].bitcast(F32),
                                        ALU.subtract).then_inc(lo_done, 1)
            lo(0, 0)
            dve.wait_ge(bias_loaded, 16)

            def step(s, r):
                if not known(s, N - 1):
                    lo(s + 1, (r + 1) % RING)
                expert = dve.value_load(ex.expert_of[0:1, bass.ds(s, 1)], min_val=0, max_val=E - 1)
                dve.wait_ge(z_done, s + 1)
                at_least(dve, y_done, s - 1)
                nc.vector.tensor_tensor(z[r % 2][:, :], z_ps[r % 2][:, :], bias[:, bass.ds(expert * D, D)],
                                        ALU.add).then_inc(zb_done, 1)
            ring_loop(dve, step, N, RING, FIRST)


def macaron(nc, x, w_qkv, q_w, q_b, k_w, k_b, w_out, w_gate, b_gate, w_e, b_e, bias_const, out):
    def scratch(name, shape):
        return nc.dram_tensor(name, shape, F32, kind="Internal").ap()

    acc1, acc2 = scratch("acc1", [TOKENS + P, D]), scratch("acc2", [TOKENS + P, D])
    xn = scratch("xn", [TOKENS, D])
    q_dram, k_dram = scratch("q_parts", [NG * P, SEQ]), scratch("k_parts", [NG * P, SEQ])
    v_dram, o_dram = scratch("v_vals", [TOKENS, H * VW]), scratch("o_vals", [TOKENS, D])
    bias_dram = scratch("bias_rows", [2, BIAS_ROWS + MAX_ROWS, H, SEQ])
    flat = x.rearrange("b s d -> (b s) d")
    Memory.sems = []
    with ExitStack() as ctx:
        ex = Experts(nc, ctx, "ex1")
        route_block(nc, "route1", ex, flat, xn, acc1, w_gate, b_gate, w_e)
        expert_block(nc, "exp1", ex, xn, acc1, b_e)
    clear_semaphores(nc)
    qkv_block(nc, acc1, w_qkv, (q_w, q_b, k_w, k_b), bias_const, q_dram, k_dram, v_dram, bias_dram)
    attention_block(nc, q_dram, k_dram, v_dram, bias_dram, o_dram)
    with ExitStack() as ctx:
        ex = Experts(nc, ctx, "ex2")
        route_block(nc, "route2", ex, acc1, xn, acc2, w_gate, b_gate, w_e, o_dram, w_out)
        expert_block(nc, "exp2", ex, xn, acc2, b_e, out.rearrange("b s d -> (b s) d"))


def bias_rows():
    import numpy as np
    step = np.arange(1, H + 1, dtype=np.float32) * (8.0 / H)
    slope = (1.0 / np.power(2.0, step)).astype(np.float32)
    hi = (slope.view(np.uint32) & np.uint32(0xFFFFF000)).view(np.float32)
    lo = slope - hi
    pos = np.arange(SEQ, dtype=np.float32)
    r = np.zeros((2, BIAS_ROWS + MAX_ROWS, H, SEQ), np.float32)
    r[0, 0], r[0, 2] = hi[:, None], lo[:, None]
    r[0, 1] = r[0, 3] = pos[None, :]
    r[1, 0] = r[1, 2] = pos[None, :]
    r[1, 1], r[1, 3] = -hi[:, None], -lo[:, None]
    r[1, 4:] = 1.0
    return r


_INS = ['L0_attn_hidden_states', 'L0_attn_Wqkv', 'L0_attn_q_ln_w', 'L0_attn_q_ln_b', 'L0_attn_k_ln_w',
        'L0_attn_k_ln_b', 'L0_attn_Wout', 'L0_ffn_W_gate', 'L0_ffn_b_gate', 'L0_ffn_W_e', 'L0_ffn_b_e']


def kernel(**inputs):
    import numpy as _np
    import concourse.bacc as _bacc
    from concourse import mybir as _mybir
    from concourse.bass_utils import run_bass_kernel_spmd as _run

    nc = _bacc.Bacc("TRN2", target_bir_lowering=False, num_devices=1)
    arrays, args = {}, []
    for name in _INS:
        a = _np.ascontiguousarray(inputs[name])
        arrays[f"in_{name}"] = a
        args.append(nc.dram_tensor(f"in_{name}", a.shape, _mybir.dt.from_np(a.dtype), kind="ExternalInput").ap())
    a = bias_rows()
    arrays["in_bias_rows"] = a
    args.append(nc.dram_tensor("in_bias_rows", a.shape, _mybir.dt.from_np(a.dtype), kind="ExternalInput").ap())
    args.append(nc.dram_tensor("out_0", (B, SEQ, D), F32, kind="ExternalOutput").ap())
    macaron(nc, *args)
    r = _run(nc, [arrays], core_ids=[0])
    return r.results[0]["out_0"]
```

```python
import concourse.bass as bass
from concourse import mybir
from contextlib import ExitStack

F32 = mybir.dt.float32
F32R = mybir.dt.float32r
BF16 = mybir.dt.bfloat16
I32 = mybir.dt.int32
U32 = mybir.dt.uint32
ALU = mybir.AluOpType
ACT = mybir.ActivationFunctionType
X_AXIS = mybir.AxisListType.X

P = 128
D = 512
B, SEQ = 4, 512
TOKENS = B * SEQ
TILES = TOKENS // P
QT = SEQ // P
C = D // P
E = 8
H = 32
HD = D // H
HG = 4
NG = B * H // HG
VW = 32
CLIP = 8.0
EPS = 1e-5
NEG = -1e30
STACK = 4 * HD
BIAS_ROWS = 4
MAX_ROWS = 2


def at_least(engine, sem, value):
    if isinstance(value, int) and value <= 0:
        return
    engine.wait_ge(sem, value)


class Chain:

    def __init__(self, engine, sem, base=0, passed=None):
        self.engine, self.sem, self.base, self.n, self.passed = engine, sem, base, 0, passed

    def __call__(self, instruction, apart=False):
        self.n += 1
        instruction.then_inc(self.sem, 1)
        self.engine.wait_ge(self.sem, self.base + self.n)
        if apart and not isinstance(self.base, int):
            self.engine.sem_inc(self.passed, 1)


def tile_loop(engine, step, first=2, last=TILES - 2):
    for t in range(first):
        step(t, t % 2)
    with engine.Fori(first // 2, last // 2) as i:
        for par in range(2):
            step(2 * i + par, par)
    for t in range(last, TILES):
        step(t, t % 2)


def rsqrt_steps(nc, chain, var, y, tmp):
    chain(nc.vector.tensor_scalar(tmp[1], var, EPS, None, ALU.add))
    chain(nc.vector.tensor_scalar(y.bitcast(I32), tmp[1].bitcast(I32), -0.5, 1597463007.0, ALU.mult, ALU.add))
    for _ in range(3):
        chain(nc.vector.tensor_tensor(tmp[0], y, y, ALU.mult))
        chain(nc.vector.scalar_tensor_tensor(tmp[0], tmp[0], -0.5, tmp[1], ALU.mult, ALU.mult))
        chain(nc.vector.scalar_tensor_tensor(y, tmp[0], 1.5, y, ALU.add, ALU.mult))


RSQRT_LINKS = 11


def layernorm_steps(nc, chain, x, out, ln):
    chain(nc.vector.bn_stats(ln["stats"], x), apart=True)
    chain(nc.vector.bn_aggr(ln["mv"], ln["stats"]))
    rsqrt_steps(nc, chain, ln["mv"][:, 1:2], ln["rstd"], (ln["t0"], ln["t1"]))
    return nc.vector.tensor_scalar(out, x, ln["mv"][:, 0:1], ln["rstd"], ALU.subtract, ALU.mult)


LN_LINKS = 2 + RSQRT_LINKS


class Memory:

    sems = []

    def __init__(self, nc, ctx, prefix):
        self.nc, self.ctx, self.prefix = nc, ctx, prefix

    def sb(self, name, shape, dt=F32):
        return self.ctx.enter_context(self.nc.sbuf_tensor(f"{self.prefix}_{name}", shape, dt))

    def ps(self, name, width=512):
        return self.ctx.enter_context(self.nc.psum_tensor(f"{self.prefix}_{name}", [P, width], F32))

    def sem(self, name):
        sem = self.nc.alloc_semaphore(name=f"{self.prefix}_{name}")
        Memory.sems.append(sem)
        return sem

    def ln(self):
        return {"stats": self.sb("ln_stats", [P, 6])[:, :], "mv": self.sb("ln_mv", [P, 2])[:, :],
                "rstd": self.sb("ln_rstd", [P, 1])[:, :], "t0": self.sb("ln_t0", [P, 1])[:, :],
                "t1": self.sb("ln_t1", [P, 1])[:, :]}


def clear_semaphores(nc):
    nc.clear_and_free_semaphores(Memory.sems)
    nc.all_engine_barrier()
    Memory.sems = []


def rows(dram, t, n=P):
    return dram[bass.ds(t * n, n), :]


def split_matmuls(nc, out, x_hi, x_lo, w_hi, w_lo):
    for c in range(C):
        s = slice(c * P, (c + 1) * P)
        nc.tensor.matmul(out, x_hi[:, s], w_hi(c), start=(c == 0), stop=False)
        nc.tensor.matmul(out, x_hi[:, s], w_lo(c), start=False, stop=False)
        last = nc.tensor.matmul(out, x_lo[:, s], w_hi(c), start=False, stop=(c == C - 1))
    return last


def load_transposed_weight(nc, m, w, n_tiles, w_hi, w_lo, ident, ident_done, banks, stage=None):
    R = len(banks)
    stage = stage or [m.sb(f"wst{i}", [P, D])[:, :] for i in range(R)]
    loaded = [m.sem(f"wst_loaded{i}") for i in range(R)]
    tr, hi, lo = m.sem("wst_tr"), m.sem("wst_hi"), m.sem("wst_lo")

    def cols(w_t, t):
        return w_t[:, :, bass.ds(t * P, P)]

    def ring(engine, step):
        for t in range(R):
            step(t, t)
        if n_tiles > R:
            with engine.Fori(1, n_tiles // R) as i:
                for k in range(R):
                    step(R * i + k, k)

    def sync(sp):
        def step(t, k):
            at_least(sp, tr, t - R + 1)
            sp.dma_start(stage[k], rows(w, t)).then_inc(loaded[k], 16)
        ring(sp, step)

    def tensor(pe):
        pe.wait_ge(ident_done, 1)

        def step(t, k):
            pe.wait_ge(loaded[k], 16 * (t // R + 1))
            at_least(pe, lo, t - R + 1)
            for c in range(C):
                last = nc.tensor.transpose(banks[k][:, c * P:(c + 1) * P], stage[k][:, c * P:(c + 1) * P], ident[:, :])
            last.then_inc(tr, 1)
        ring(pe, step)

    def bank(k):
        return banks[k][:, :].rearrange("p (c n) -> p c n", c=C)

    def scalar(act):
        def step(t, k):
            act.wait_ge(tr, t + 1)
            nc.scalar.activation(cols(w_hi, t), bank(k), ACT.Copy).then_inc(hi, 1)
        ring(act, step)

    def vector(dve):
        def step(t, k):
            dve.wait_ge(hi, t + 1)
            nc.vector.tensor_tensor(cols(w_lo, t), bank(k), cols(w_hi, t).bitcast(F32), ALU.subtract).then_inc(lo, 1)
        ring(dve, step)

    return {"sync": sync, "tensor": tensor, "scalar": scalar, "vector": vector, "done": (lo, n_tiles)}


def make_identity(nc, pool, ident, zeroed, done):
    nc.gpsimd.memset(ident[:, :], 0.0).then_inc(zeroed, 1)
    pool.wait_ge(zeroed, 1)
    nc.gpsimd.affine_select(out=ident[:, :], in_=ident[:, :], compare_op=ALU.not_equal, fill=1.0, base=0,
                            pattern=[[-1, P]], channel_multiplier=1).then_inc(done, 1)


def qkv_block(nc, x1, w_qkv, ln_params, bias_const, q_dram, k_dram, v_dram, bias_dram):
    with ExitStack() as ctx:
        m = Memory(nc, ctx, "qkv")
        w_hi = m.sb("w_hi", [P, C, 3 * D], F32R)
        w_lo = m.sb("w_lo", [P, C, 3 * D], F32R)
        ident = m.sb("ident", [P, P])
        lnp = [m.sb(f"lnp{i}", [P, D]) for i in range(4)]
        x = [m.sb(f"x{i}", [P, D]) for i in range(2)]
        xn = [m.sb(f"xn{i}", [P, D]) for i in range(2)]
        xT_hi = [m.sb(f"xT_hi{i}", [P, C * P], F32R) for i in range(2)]
        xT_lo = [m.sb(f"xT_lo{i}", [P, C * P], F32R) for i in range(2)]
        clipped = [[m.sb(f"clip{s}{i}", [P, D]) for i in range(2)] for s in "qk"]
        normed = [[m.sb(f"norm{s}{i}", [P, D]) for i in range(2)] for s in "qk"]
        parts = [[m.sb(f"parts{s}{i}", [P, H, 2, HD], F32R) for i in range(2)] for s in "qk"]
        turned_sb = [[m.sb(f"turned{s}{i}", [P, 8, P], F32R) for i in range(2)] for s in "qk"]
        vals = [m.sb(f"vals{i}", [P, H, VW]) for i in range(2)]
        ln = m.ln()
        stats3 = m.sb("stats3", [P, 3, 6])
        mv3 = m.sb("mv3", [P, 3, 2])
        rstd3, tmp3a, tmp3b = (m.sb(n, [P, 3]) for n in ("rstd3", "tmp3a", "tmp3b"))
        o_ps = [m.ps(f"o_ps{i}") for i in range(3)]
        t_ps = [m.ps(f"t_ps{i}") for i in range(2)]
        s_ps = [m.ps(f"s_ps{i}") for i in range(2)]

        x_loaded = [m.sem(f"x_loaded{i}") for i in range(2)]
        lnp_loaded, bias_copied = m.sem("lnp_loaded"), m.sem("bias_copied")
        zeroed, ident_done, vals_set = m.sem("zeroed"), m.sem("ident_done"), m.sem("vals_set")
        scaled = m.sem("scaled")
        xn_done, tr_done = m.sem("xn_done"), m.sem("tr_done")
        hi_done, lo_done = m.sem("hi_done"), m.sem("lo_done")
        proj_done = [m.sem(f"proj_done{s}") for s in "qkv"]
        clip_done = [m.sem(f"clip_done{s}") for s in "qkv"]
        unit_done = m.sem("unit_done")
        affine_chain, affine_done = m.sem("affine_chain"), m.sem("affine_done")
        part_hi, part_lo = m.sem("part_hi"), m.sem("part_lo")
        turn_done, turn_out = m.sem("turn_done"), m.sem("turn_out")
        qk_stored = [m.sem(f"qk_stored{i}") for i in range(2)]
        v_stored = [m.sem(f"v_stored{i}") for i in range(2)]
        ln_chain, qk_chain, passed = m.sem("ln_chain"), m.sem("qk_chain"), m.sem("passed")

        wprep = load_transposed_weight(nc, m, w_qkv, 3 * D // P, w_hi, w_lo, ident, ident_done, t_ps + s_ps)
        block = ctx.enter_context(nc.Block())

        def front(t):
            return not (isinstance(t, int) and t + 1 >= TILES)

        def after(t, n):
            return not (isinstance(t, int) and t < n)

        @block.sync
        def _(sp):
            for par in range(2):
                sp.dma_start(x[par][:, :], rows(x1, par)).then_inc(x_loaded[par], 16)
            wprep["sync"](sp)
            for i, p in enumerate(ln_params):
                sp.dma_start(lnp[i][:, :], p.rearrange("(a e) -> a e", a=1).to_broadcast([P, D])).then_inc(lnp_loaded, 16)
            sp.dma_start(bias_dram, bias_const).then_inc(bias_copied, 16)

            def load_x(t, par):
                sp.wait_ge(xn_done, t - 1)
                sp.dma_start(x[par][:, :], rows(x1, t)).then_inc(x_loaded[par], 16)

            def store_v(t, par):
                sp.wait_ge(clip_done[2], t + 1)
                sp.dma_start(rows(v_dram, t), vals[par][:, :, :].rearrange("p h w -> p (h w)")).then_inc(v_stored[par], 16)

            def store_qk(t, par):
                b, j = t // QT, t % QT
                for s, dram in enumerate((q_dram, k_dram)):
                    sp.wait_ge(turn_out, 4 * t + 2 * s + 2)
                    out = dram[bass.ds(b * (8 * P), 8 * P), bass.ds(j * P, P)].rearrange("(g p) n -> p g n", p=P)
                    sp.dma_start(out, turned_sb[s][par][:, :, :].bitcast(F32)).then_inc(qk_stored[par], 16)

            def step(t, par):
                if not (isinstance(t, int) and t + 3 >= TILES):
                    load_x(t + 3, 1 - par)
                store_v(t, par)
                if after(t, 2):
                    store_qk(t - 2, par)
            load_x(2, 0)
            tile_loop(sp, step, last=TILES - 4)
            store_qk(TILES - 2, 0)
            store_qk(TILES - 1, 1)
            sp.wait_ge(bias_copied, 16)
            for par in range(2):
                sp.wait_ge(v_stored[par], 16 * (TILES // 2))
                sp.wait_ge(qk_stored[par], 32 * (TILES // 2))

        @block.gpsimd
        def _(pool):
            make_identity(nc, pool, ident, zeroed, ident_done)
            for par in range(2):
                nc.gpsimd.memset(vals[par][:, :, HD:VW], 0.0).then_inc(zeroed, 1)
            pool.wait_ge(zeroed, 3)
            for par in range(2):
                nc.gpsimd.memset(vals[par][:, :, HD:HD + 1], 1.0).then_inc(vals_set, 1)
            pool.wait_ge(scaled, 2)

            def split_lo(t, par, s):
                pool.wait_ge(part_hi, 2 * t + s + 1)
                nc.gpsimd.tensor_tensor(parts[s][par][:, :, 1, :], normed[s][par][:, :].rearrange("p (h d) -> p h d", d=HD),
                                        parts[s][par][:, :, 0, :].bitcast(F32), ALU.subtract).then_inc(part_lo, 1)

            def step(t, par):
                chain = Chain(pool, affine_chain, 2 * t)
                for s in range(2):
                    pool.wait_ge(unit_done, 2 * t + s + 1)
                    chain(nc.gpsimd.tensor_tensor(normed[s][par][:, :], normed[s][par][:, :], lnp[2 * s][:, :], ALU.mult))
                    nc.gpsimd.tensor_tensor(normed[s][par][:, :], normed[s][par][:, :], lnp[2 * s + 1][:, :],
                                            ALU.add).then_inc(affine_done, 1)
                for s in range(2):
                    split_lo(t, par, s)
            tile_loop(pool, step)

        @block.tensor
        def _(pe):
            wprep["tensor"](pe)
            sem, count = wprep["done"]
            pe.wait_ge(sem, count)

            def transpose(t, par):
                pe.wait_ge(xn_done, t + 1)
                at_least(pe, lo_done, t - 1)
                for c in range(C):
                    last = nc.tensor.transpose(t_ps[par][:, c * P:(c + 1) * P], xn[par][:, c * P:(c + 1) * P], ident[:, :])
                last.then_inc(tr_done, 1)

            def project(t, par, s):
                at_least(pe, clip_done[s], t)
                cols = slice(s * D, (s + 1) * D)
                split_matmuls(nc, o_ps[s][:, :], xT_hi[par], xT_lo[par], lambda c: w_hi[:, c, cols],
                              lambda c: w_lo[:, c, cols]).then_inc(proj_done[s], 1)

            def turn(t, par, s):
                pe.wait_ge(part_lo, 2 * t + s + 1)
                flat = parts[s][par][:, :, :, :].rearrange("p h k d -> p (h k d)").bitcast(F32)
                for half in range(2):
                    at_least(pe, turn_out, 4 * t + 2 * s + half - 1)
                    for g in range(4):
                        col = (4 * half + g) * P
                        last = nc.tensor.transpose(s_ps[half][:, g * P:(g + 1) * P], flat[:, col:col + P], ident[:, :])
                    last.then_inc(turn_done, 1)

            transpose(0, 0)

            def step(t, par):
                pe.wait_ge(lo_done, t + 1)
                project(t, par, 0)
                if after(t, 2):
                    turn(t - 2, par, 1)
                if front(t):
                    transpose(t + 1, 1 - par)
                project(t, par, 1)
                project(t, par, 2)
                if after(t, 1):
                    turn(t - 1, 1 - par, 0)
            tile_loop(pe, step)
            turn(TILES - 2, 0, 1)
            turn(TILES - 1, 1, 0)
            turn(TILES - 1, 1, 1)

        @block.scalar
        def _(act):
            wprep["scalar"](act)

            def hi(t, par):
                act.wait_ge(tr_done, t + 1)
                at_least(act, proj_done[2], t - 1)
                nc.scalar.activation(xT_hi[par][:, :], t_ps[par][:, :], ACT.Copy).then_inc(hi_done, 1)

            def split_hi(t, par, s):
                act.wait_ge(affine_done, 2 * t + s + 1)
                at_least(act, turn_done, 4 * (t - 2) + 2 * s + 2)
                nc.scalar.activation(parts[s][par][:, :, 0, :], normed[s][par][:, :].rearrange("p (h d) -> p h d", d=HD),
                                     ACT.Copy).then_inc(part_hi, 1)

            def turned_out(t, par, s, half):
                act.wait_ge(turn_done, 4 * t + 2 * s + half + 1)
                if half == 0:
                    at_least(act, qk_stored[par], 32 * (t // 2))
                nc.scalar.activation(turned_sb[s][par][:, 4 * half:4 * half + 4, :],
                                     s_ps[half][:, :].rearrange("p (g n) -> p g n", g=4), ACT.Copy).then_inc(turn_out, 1)

            hi(0, 0)

            def turned(t, par, s):
                for half in range(2):
                    turned_out(t, par, s, half)

            def step(t, par):
                if after(t, 2):
                    turned(t - 2, par, 1)
                if after(t, 1):
                    split_hi(t - 1, 1 - par, 0)
                if front(t):
                    hi(t + 1, 1 - par)
                if after(t, 1):
                    split_hi(t - 1, 1 - par, 1)
                    turned(t - 1, 1 - par, 0)
            tile_loop(act, step, first=4)
            turned(TILES - 2, 0, 1)
            split_hi(TILES - 1, 1, 0)
            split_hi(TILES - 1, 1, 1)
            turned(TILES - 1, 1, 0)
            turned(TILES - 1, 1, 1)

        @block.vector
        def _(dve):
            def norm(t, par):
                dve.wait_ge(x_loaded[par], 16 * (t // 2 + 1))
                at_least(dve, tr_done, t - 1)
                chain = Chain(dve, ln_chain, LN_LINKS * t, passed)
                layernorm_steps(nc, chain, x[par][:, :], xn[par][:, :], ln).then_inc(xn_done, 1)

            def lo(t, par):
                dve.wait_ge(hi_done, t + 1)
                nc.vector.tensor_tensor(xT_lo[par][:, :], t_ps[par][:, :], xT_hi[par][:, :].bitcast(F32),
                                        ALU.subtract).then_inc(lo_done, 1)

            def clip(t, par, s):
                dve.wait_ge(proj_done[s], t + 1)
                if s == 2:
                    at_least(dve, v_stored[par], 16 * (t // 2))
                    nc.vector.tensor_scalar(vals[par][:, :, 0:HD], o_ps[2][:, :].rearrange("p (h d) -> p h d", d=HD),
                                            CLIP, -CLIP, ALU.min, ALU.max).then_inc(clip_done[2], 1)
                else:
                    at_least(dve, unit_done, 2 * (t - 1))
                    nc.vector.tensor_scalar(clipped[s][par][:, :], o_ps[s][:, :], CLIP, -CLIP, ALU.min,
                                            ALU.max).then_inc(clip_done[s], 1)

            def unit(t, par):
                ahead = not (isinstance(t, int) and t + 2 >= TILES)
                base = QK_LINKS * t - (2 * max(0, t + 2 - TILES) if isinstance(t, int) else 0)
                chain = Chain(dve, qk_chain, base, passed)
                if ahead:
                    dve.wait_ge(x_loaded[par], 16 * (t // 2 + 2))
                    chain(nc.vector.bn_stats(stats3[:, 2, :], x[par][:, :]))
                if front(t):
                    lo(t + 1, 1 - par)
                for s in range(2):
                    clip(t, par, s)
                for s in range(2):
                    dve.wait_ge(clip_done[s], t + 1)
                    chain(nc.vector.bn_stats(stats3[:, s, :], clipped[s][par][:, :]), apart=True)
                for s in range(3 if ahead else 2):
                    chain(nc.vector.bn_aggr(mv3[:, s, :], stats3[:, s, :]), apart=(s < (2 if ahead else 1)))
                rsqrt_steps(nc, chain, mv3[:, :, 1], rstd3[:, :], (tmp3a[:, :], tmp3b[:, :]))
                if ahead:
                    dve.wait_ge(tr_done, t + 1)
                    nc.vector.tensor_scalar(xn[par][:, :], x[par][:, :], mv3[:, 2, 0:1], rstd3[:, 2:3],
                                            ALU.subtract, ALU.mult).then_inc(xn_done, 1)
                at_least(dve, part_lo, 2 * (t - 1))
                for s in range(2):
                    nc.vector.tensor_scalar(normed[s][par][:, :], clipped[s][par][:, :], mv3[:, s, 0:1],
                                            rstd3[:, s:s + 1], ALU.subtract, ALU.mult).then_inc(unit_done, 1)

            norm(0, 0)
            norm(1, 1)
            wprep["vector"](dve)
            lo(0, 0)
            dve.wait_ge(lnp_loaded, 64)
            for i in range(2):
                nc.vector.tensor_scalar(lnp[i][:, :], lnp[i][:, :], HD ** -0.5, None, ALU.mult).then_inc(scaled, 1)
            dve.wait_ge(vals_set, 2)

            def step(t, par):
                unit(t, par)
                clip(t, par, 2)
            tile_loop(dve, step)


QK_LINKS = 6 + RSQRT_LINKS


def stack_unit(u):
    if u == 0:
        return 0, (0, 1, 2, 3), P
    if u < 3:
        return 1, (2 * u - 2, 2 * u - 1), 2 * P
    i = 2 if u < 7 else 3
    return i, ((u - 3) % 4,), (i + 1) * P


S_UNITS = 11
T_UNITS = 5
PCOLS = HG * 10 * P


def prob_cols(h, j):
    return {0: h * 1024, 1: h * 1024 + 512, 3: h * 1024 + 896, 2: HG * 1024 + h * 256}[j]


def attention_block(nc, q_dram, k_dram, v_dram, bias_dram, o_dram):
    with ExitStack() as ctx:
        m = Memory(nc, ctx, "att")
        RING = 4
        q_st = [m.sb(f"q_st{i}", [P, HG, SEQ], F32R) for i in range(RING)]
        k_st = [m.sb(f"k_st{i}", [P, HG, SEQ], F32R) for i in range(RING)]
        v_sb = [m.sb(f"v_sb{i}", [P, QT, HG * VW]) for i in range(RING)]
        prob = [m.sb(f"prob{i}", [P, PCOLS]) for i in range(2)]
        nmax = [m.sb(f"nmax{i}", [P, QT, HG]) for i in range(2)]
        m_hi = [m.sb(f"m_hi{i}", [HG, SEQ], F32R) for i in range(2)]
        m_lo = [m.sb(f"m_lo{i}", [HG, SEQ], F32R) for i in range(2)]
        oT = [m.sb(f"oT{i}", [P, SEQ]) for i in range(2)]
        rden = m.sb("rden", [P, QT, HG, 1])
        o_sb = [m.sb(f"o_sb{i}", [P, QT, 2 * HG * HD]) for i in range(2)]
        ident = m.sb("ident", [P, P])
        ident_bf = m.sb("ident_bf", [P, P], BF16)
        mask = m.sb("mask", [P, HG, P], BF16)
        mask_t = m.sb("mask_t", [P, 2, P], BF16)
        s_ps = [m.ps(f"s_ps{i}") for i in range(2)]
        st_ps = [m.ps(f"st_ps{i}", 1024) for i in range(2)]
        pv_ps = m.ps("pv_ps")
        x_ps = m.ps("x_ps")

        stack_loaded = [m.sem(f"stack_loaded{i}") for i in range(RING)]
        zeroed, const_done = m.sem("zeroed"), m.sem("const_done")
        s_done, max_done = m.sem("s_done"), m.sem("max_done")
        mT_done, m_hi_done, m_lo_done = m.sem("mT_done"), m.sem("m_hi_done"), m.sem("m_lo_done")
        m_loaded = [m.sem(f"m_loaded{i}") for i in range(2)]
        st_done, exp_done = m.sem("st_done"), m.sem("exp_done")
        pv_done, oT_done, turn_done = m.sem("pv_done"), m.sem("oT_done"), m.sem("turn_done")
        rden_done, o_done = m.sem("rden_done"), m.sem("o_done")
        o_stored = [m.sem(f"o_stored{i}") for i in range(2)]
        LOADS = 8
        SCORE_ROWS = STACK + BIAS_ROWS
        FULL_ROWS = SCORE_ROWS + MAX_ROWS
        block = ctx.enter_context(nc.Block())

        def group_loop(engine, step):
            step(0, 0)
            with engine.Fori(0, (NG - 4) // 4) as i:
                for k in range(1, 5):
                    step(4 * i + k, k % 4)
            for n in range(NG - 3, NG):
                step(n, n % 4)

        def is_last(n, ahead=1):
            return isinstance(n, int) and n + ahead >= NG

        def is_first(n):
            return isinstance(n, int) and n == 0

        @block.sync
        def _(sp):
            def load(n, r):
                at_least(sp, st_done, T_UNITS * (n - 3))
                at_least(sp, pv_done, n - 3)
                src_q = q_dram[bass.ds(n * P, P), :].rearrange("(h r) n -> r h n", h=HG)
                src_k = k_dram[bass.ds(n * P, P), :].rearrange("(h r) n -> r h n", h=HG)
                q, k, done = q_st[r], k_st[r], stack_loaded[r]
                g8 = n % 8

                def put(dst, src):
                    sp.dma_start(dst.bitcast(F32), src).then_inc(done, 16)
                put(q[0:2 * HD, :, :], src_q)
                put(q[2 * HD:4 * HD, :, :], src_q)
                put(k[0:2 * HD, :, :], src_k)
                put(k[2 * HD:3 * HD, :, :], src_k[HD:2 * HD])
                put(k[3 * HD:4 * HD, :, :], src_k[0:HD])
                put(q[STACK:STACK + BIAS_ROWS, :, :], bias_dram[0, 0:BIAS_ROWS, bass.ds(g8 * HG, HG), :])
                put(k[STACK:FULL_ROWS, :, :], bias_dram[1, :, bass.ds(g8 * HG, HG), :])
                b = n // 8
                src_v = v_dram[bass.ds(b * SEQ, SEQ), bass.ds(g8 * (HG * VW), HG * VW)].rearrange("(j p) w -> p j w", p=P)
                sp.dma_start(v_sb[r][:, :, :], src_v).then_inc(done, 16)

            def max_rows(n, r):
                sp.wait_ge(m_lo_done, n + 1)
                at = q_st[r]
                for i, src in enumerate((m_hi, m_lo)):
                    row = SCORE_ROWS + i
                    sp.dma_start(at[row:row + 1, :, :].bitcast(F32), src[r % 2][:, :].bitcast(F32)).then_inc(m_loaded[r % 2], 16)

            def store(n, r):
                sp.wait_ge(o_done, n + 1)
                out = o_dram[bass.ds((n // 8) * SEQ, SEQ), bass.ds(((n % 8) // 2) * P, P)].rearrange("(i p) w -> p i w", p=P)
                sp.dma_start(out, o_sb[(r // 2) % 2][:, :, :]).then_inc(o_stored[(r // 2) % 2], 16)

            for n in range(3):
                load(n, n)
            max_rows(0, 0)

            def step(n, r):
                if not is_last(n, 3):
                    load(n + 3, (r + 3) % 4)
                if not is_last(n):
                    max_rows(n + 1, (r + 1) % 4)
                if not is_first(n) and r % 2 == 0:
                    store(n - 1, (r - 1) % 4)
            group_loop(sp, step)
            store(NG - 1, 3)
            for i in range(2):
                sp.wait_ge(o_stored[i], 16 * (NG // 4))

        @block.gpsimd
        def _(pool):
            nc.gpsimd.memset(ident[:, :], 0.0).then_inc(zeroed, 1)
            nc.gpsimd.memset(ident_bf[:, :], 0.0).then_inc(zeroed, 1)
            nc.gpsimd.memset(mask[:, :, :], 0.0).then_inc(zeroed, 1)
            nc.gpsimd.memset(mask_t[:, :, :], 0.0).then_inc(zeroed, 1)
            pool.wait_ge(zeroed, 4)
            for a in (ident, ident_bf):
                nc.gpsimd.affine_select(out=a[:, :], in_=a[:, :], compare_op=ALU.not_equal, fill=1.0, base=0,
                                        pattern=[[-1, P]], channel_multiplier=1).then_inc(const_done, 1)
            nc.gpsimd.affine_select(out=mask[:, :, :], in_=mask[:, :, :], compare_op=ALU.is_ge, fill=NEG, base=0,
                                    pattern=[[0, HG], [-1, P]], channel_multiplier=1).then_inc(const_done, 1)
            nc.gpsimd.affine_select(out=mask_t[:, :, :], in_=mask_t[:, :, :], compare_op=ALU.is_ge, fill=NEG, base=0,
                                    pattern=[[0, 2], [1, P]], channel_multiplier=-1).then_inc(const_done, 1)

        @block.tensor
        def _(pe):
            pe.wait_ge(const_done, 4)

            def scores(n, r, u):
                i, heads, w = stack_unit(u)
                bank = s_ps[(S_UNITS * r + u) % 2]
                if u == 0:
                    pe.wait_ge(stack_loaded[r], 16 * LOADS * (n // 4 + 1))
                at_least(pe, max_done, S_UNITS * n + u - 1)
                k = len(heads)
                diag = bank[:, 0:k * w].rearrange("p (h w) -> p h w", h=k)[:, :, i * P:(i + 1) * P]
                nc.tensor.matmul(diag, ident_bf[:, :], mask[:, 0:k, :], start=True, stop=False, skip_group_check=True)
                for a, h in enumerate(heads):
                    last = nc.tensor.matmul(bank[:, a * w:(a + 1) * w], q_st[r][0:SCORE_ROWS, h, i * P:(i + 1) * P],
                                            k_st[r][0:SCORE_ROWS, h, 0:w], start=False, stop=(a == k - 1),
                                            skip_group_check=True)
                last.then_inc(s_done, 1)

            def turn_max(n, r):
                pe.wait_ge(max_done, S_UNITS * (n + 1))
                at_least(pe, o_done, n - 1)
                if isinstance(n, int) and n == 1:
                    pe.wait_ge(m_lo_done, 1)
                for i in range(QT):
                    last = nc.tensor.transpose(x_ps[0:HG, i * P:(i + 1) * P], nmax[r % 2][:, i, :], ident[:, :])
                last.then_inc(mT_done, 1)

            def scores_by_key(n, r, u):
                bank = st_ps[(T_UNITS * r + u) % 2]
                if u == 0:
                    pe.wait_ge(m_loaded[r % 2], 32 * (n // 2 + 1))
                at_least(pe, exp_done, T_UNITS * n + u - 1)
                todo = [(u, 0, 0), (u, 1, 512), (u, 3, 896)] if u < 4 else [(h, 2, 256 * h) for h in range(HG)]
                if u < 4:
                    diags = [bank[:, 0:P], bank[:, 512:1024].rearrange("p (a w) -> p a w", a=4)[:, 0:4:3, :]]
                else:
                    diags = [bank[:, 512 * a:512 * (a + 1)].rearrange("p (h w) -> p h w", h=2)[:, :, 0:P] for a in range(2)]
                for d in diags:
                    rhs = mask_t[:, 0, :] if len(d.shape) == 2 else mask_t[:, :, :]
                    nc.tensor.matmul(d, ident_bf[:, :], rhs, start=True, stop=False, skip_group_check=True)
                for h, j, col in todo:
                    w = SEQ - j * P
                    last = nc.tensor.matmul(bank[:, col:col + w], k_st[r][0:FULL_ROWS, h, j * P:(j + 1) * P],
                                            q_st[r][0:FULL_ROWS, h, j * P:SEQ], start=False, stop=True,
                                            skip_group_check=True)
                last.then_inc(st_done, 1)

            def values(n, r, j):
                if j == 0:
                    pe.wait_ge(exp_done, T_UNITS * (n + 1))
                    at_least(pe, oT_done, n)
                for h in range(HG):
                    w = SEQ - j * P
                    col = prob_cols(h, j)
                    last = nc.tensor.matmul(pv_ps[VW * h:VW * (h + 1), j * P:SEQ], v_sb[r][:, j, VW * h:VW * (h + 1)],
                                            prob[r % 2][:, col:col + w], start=(j == 0), stop=(j == QT - 1))
                if j == QT - 1:
                    last.then_inc(pv_done, 1)

            def turn_out(n, r):
                pe.wait_ge(oT_done, n + 1)
                if isinstance(n, int) and n + 1 >= NG:
                    pe.wait_ge(o_done, n)
                else:
                    pe.wait_ge(m_lo_done, n + 2)
                for i in range(QT):
                    last = nc.tensor.transpose(x_ps[:, i * P:(i + 1) * P], oT[r % 2][:, i * P:(i + 1) * P], ident[:, :])
                last.then_inc(turn_done, 1)

            for u in range(S_UNITS):
                scores(0, 0, u)
            turn_max(0, 0)

            def step(n, r):
                rn, rp = (r + 1) % 4, (r - 1) % 4
                more = not is_last(n)
                for item in "S0 S1 P0 S2 P1 S3 P2 S4 P3 S5 T0 O T1 S6 T2 S7 S8 T3 S9 S10 T4 M".split():
                    kind, u = item[0], item[1:]
                    if kind == "S" and more:
                        scores(n + 1, rn, int(u))
                    elif kind == "T":
                        scores_by_key(n, r, int(u))
                    elif kind == "P" and not is_first(n):
                        values(n - 1, rp, int(u))
                    elif kind == "O" and not is_first(n):
                        turn_out(n - 1, rp)
                    elif kind == "M" and more:
                        turn_max(n + 1, rn)
            group_loop(pe, step)
            for j in range(QT):
                values(NG - 1, 3, j)
            turn_out(NG - 1, 3)

        @block.scalar
        def _(act):
            def max_hi(n, r):
                act.wait_ge(mT_done, n + 1)
                at_least(act, m_loaded[r % 2], 32 * (n // 2))
                nc.scalar.activation(m_hi[r % 2][:, :], x_ps[0:HG, :], ACT.Copy).then_inc(m_hi_done, 1)

            def exps(n, r, u):
                act.wait_ge(st_done, T_UNITS * n + u + 1)
                if u == 0:
                    at_least(act, pv_done, n - 1)
                nc.scalar.activation(prob[r % 2][:, 1024 * u:1024 * (u + 1)], st_ps[(T_UNITS * r + u) % 2][:, :],
                                     ACT.Exp).then_inc(exp_done, 1)

            def out_copy(n, r):
                act.wait_ge(pv_done, n + 1)
                at_least(act, turn_done, n)
                nc.scalar.activation(oT[r % 2][:, :], pv_ps[:, :], ACT.Copy).then_inc(oT_done, 1)

            max_hi(0, 0)

            def step(n, r):
                if not is_first(n):
                    out_copy(n - 1, (r - 1) % 4)
                for u in range(T_UNITS):
                    exps(n, r, u)
                if not is_last(n):
                    max_hi(n + 1, (r + 1) % 4)
            group_loop(act, step)
            out_copy(NG - 1, 3)

        @block.vector
        def _(dve):
            def reduce(n, r, u):
                i, heads, w = stack_unit(u)
                k = len(heads)
                dve.wait_ge(s_done, S_UNITS * n + u + 1)
                if u == 0:
                    at_least(dve, mT_done, n - 1)
                nc.vector.tensor_reduce(nmax[r % 2][:, i, heads[0]:heads[0] + k],
                                        s_ps[(S_UNITS * r + u) % 2][:, 0:k * w].rearrange("p (h w) -> p h w", h=k),
                                        X_AXIS, ALU.max, negate=True).then_inc(max_done, 1)

            def max_lo(n, r):
                dve.wait_ge(m_hi_done, n + 1)
                nc.vector.tensor_tensor(m_lo[r % 2][:, :], x_ps[0:HG, :], m_hi[r % 2][:, :].bitcast(F32),
                                        ALU.subtract).then_inc(m_lo_done, 1)

            def normalise(n, r):
                dve.wait_ge(turn_done, n + 1)
                turned = x_ps[:, :].rearrange("p (i h w) -> p i h w", i=QT, h=HG)
                nc.vector.reciprocal(rden[:, :, :, 0], turned[:, :, :, HD]).then_inc(rden_done, 1)
                dve.wait_ge(rden_done, n + 1)
                half = r % 2
                slot = (r // 2) % 2
                if half == 0:
                    at_least(dve, o_stored[slot], 16 * (n // 4))
                out = o_sb[slot][:, :, half * HG * HD:(half + 1) * HG * HD].rearrange("p i (h d) -> p i h d", h=HG)
                nc.vector.tensor_tensor(out, turned[:, :, :, 0:HD], rden[:, :, :, :].to_broadcast([P, QT, HG, HD]),
                                        ALU.mult).then_inc(o_done, 1)

            for u in range(S_UNITS):
                reduce(0, 0, u)

            def step(n, r):
                more = not is_last(n)
                rn = (r + 1) % 4
                for u in range(S_UNITS):
                    if more:
                        reduce(n + 1, rn, u)
                    if u == 0:
                        max_lo(n, r)
                    if u == 5 and not is_first(n):
                        normalise(n - 1, (r - 1) % 4)
            group_loop(dve, step)
            normalise(NG - 1, 3)



SLOT_TILES = 2 * TOKENS // P + E - 1
TAB = SLOT_TILES + 1


class Experts:

    def __init__(self, nc, ctx, prefix):
        m = Memory(nc, ctx, prefix)
        self.w_hi = m.sb("w_hi", [P, E * C, D], F32R)
        self.w_lo = m.sb("w_lo", [P, E * C, D], F32R)
        self.token_of = m.sb("token_of", [P, TAB], I32)
        self.row_of = m.sb("row_of", [P, TAB], I32)
        self.expert_of = m.sb("expert_of", [1, TAB], I32)


def ring_loop(engine, step, total, ring, first):
    for t in range(first):
        step(t, t % ring)
    turns = (total - first - 1) // ring
    with engine.Fori(0, turns) as i:
        for k in range(ring):
            step(first + ring * i + k, (first + k) % ring)
    for t in range(first + turns * ring, total):
        step(t, t % ring)


def known(t, limit):
    return isinstance(t, int) and t >= limit


def route_block(nc, prefix, ex, x_in, xn_dram, acc, w_gate, b_gate, w_e, o_dram=None, w_out=None):
    proj = o_dram is not None
    with ExitStack() as ctx:
        m = Memory(nc, ctx, prefix)
        w_stage = [m.sb(f"w_stage{i}", [P, 2, D]) for i in range(2)]
        g_raw = m.sb("g_raw", [P, C, E])
        bg_bc = m.sb("bg_bc", [P, E])
        ident = m.sb("ident", [P, P])
        g_both = m.sb("g_both", [P, C, 2 * E], F32R)
        x = [m.sb(f"x{i}", [P, 2, D]) for i in range(2)]
        xn = [m.sb(f"xn{i}", [P, 2, D]) for i in range(2)]
        xT_hi = [m.sb(f"xT_hi{i}", [P, C * P], F32R) for i in range(2)]
        xT_lo = [m.sb(f"xT_lo{i}", [P, C * P], F32R) for i in range(2)]
        stats, mv = m.sb("stats", [P, 2, 6]), m.sb("mv", [P, 2, 2])
        rstd, tmp_a, tmp_b = (m.sb(n, [P, 2]) for n in ("rstd", "tmp_a", "tmp_b"))
        t_ps = [m.ps(f"t_ps{i}") for i in range(2)]
        g_ps = m.ps("g_ps")
        route_ps = m.ps("route_ps")
        if proj:
            wo_hi = m.sb("wo_hi", [P, C, D], F32R)
            wo_lo = m.sb("wo_lo", [P, C, D], F32R)
            o = [m.sb(f"o{i}", [P, D]) for i in range(2)]
            oT_hi = [m.sb(f"oT_hi{i}", [P, C * P], F32R) for i in range(2)]
            oT_lo = [m.sb(f"oT_lo{i}", [P, C * P], F32R) for i in range(2)]
            o_ps = [m.ps(f"o_ps{i}") for i in range(2)]
            y_ps = [m.ps(f"y_ps{i}") for i in range(2)]
        TE = TILES * E
        rank_ps, total_ps = route_ps[:, 0:TE], route_ps[:, TE:TE + E]
        id_ps = route_ps[:, TE + 2 * E:TE + 2 * E + 3 * TAB]
        COL_RING = 4
        n_expert = m.sb("n_expert", [P, TILES, E])
        n_full = m.sb("n_full", [P, E, TILES])
        n_col = m.sb("n_col", [P, P], BF16)
        n_tile = m.sb("n_tile", [P, TAB], BF16)
        n_token_tile = m.sb("n_token_tile", [P, 2 * TILES], BF16)
        n_part = m.sb("n_part", [P, 1])
        ones8 = m.sb("ones8", [P, E])
        ones_bf = m.sb("ones_bf", [P, P], BF16)
        before = m.sb("before", [P, P], BF16)
        logits = m.sb("logits", [P, TILES, E])
        eq = m.sb("eq", [P, TILES, E])
        val = m.sb("val", [P, TILES, E])
        rest = m.sb("rest", [P, TILES, E])
        best = m.sb("best", [P, TILES, 1])
        low = m.sb("low", [P, TILES, 1])
        pick = [m.sb(f"pick{i}", [P, TILES, E]) for i in range(2)]
        picked = m.sb("picked", [P, TE], BF16)
        over = m.sb("over", [P, E, TILES])
        n_tiles = m.sb("n_tiles", [P, E])
        ends = m.sb("ends", [P, E])
        begins = m.sb("begins", [P, E])
        slot_e, slot_m = val, rest
        slot = m.sb("slot", [P, 2, TILES])
        slot_i = m.sb("slot_i", [P, 2 * TILES], I32)
        slot_hi_i = m.sb("slot_hi_i", [P, 2 * TILES], I32)
        slot_lo_i = m.sb("slot_lo_i", [P, 2 * TILES], I32)
        slot_hi = m.sb("slot_hi", [P, 2 * TILES, 1], BF16)
        slot_lo = m.sb("slot_lo", [P, 2 * TILES])
        at_col = m.sb("at_col", [P, COL_RING, P], BF16)
        at_tile = m.sb("at_tile", [P, 2 * TILES, 3, TAB], BF16)
        found = m.sb("found", [P, 3, TAB])
        empty = m.sb("empty", [P, TAB])
        past = m.sb("past", [1, TAB, E])
        exp_f = m.sb("exp_f", [1, TAB, 1])

        w_loaded = [m.sem(f"w_loaded{i}") for i in range(2)]
        w_hi_done, w_lo_done = m.sem("w_hi_done"), m.sem("w_lo_done")
        g_loaded, bias_loaded, g_hi_done, g_lo_done = (m.sem(n) for n in ("g_loaded", "bias_loaded", "g_hi_done", "g_lo_done"))
        zeroed, ident_done, const_done = m.sem("zeroed"), m.sem("ident_done"), m.sem("const_done")
        x_loaded = [m.sem(f"x_loaded{i}") for i in range(2)]
        x_stored = [m.sem(f"x_stored{i}") for i in range(2)]
        xn_stored = [m.sem(f"xn_stored{i}") for i in range(2)]
        o_loaded = [m.sem(f"o_loaded{i}") for i in range(2)]
        xn_done, tr_done, hi_done, lo_done = (m.sem(n) for n in ("xn_done", "tr_done", "hi_done", "lo_done"))
        gate_done = m.sem("gate_done")
        o_tr, o_hi, o_lo, y_done, sum_done = (m.sem(n) for n in ("o_tr", "o_hi", "o_lo", "y_done", "sum_done"))
        ln_chain, chain_sem = m.sem("ln_chain"), m.sem("chain")
        picked_done, rank_done, onehot_done, ids_done = (m.sem(n) for n in ("picked_done", "rank_done", "onehot_done", "ids_done"))
        wprep = load_transposed_weight(nc, m, w_out, C, wo_hi, wo_lo, ident, ident_done, t_ps + o_ps,
                                       [xn[i // 2][:, i % 2, :] for i in range(C)]) if proj else None
        block = ctx.enter_context(nc.Block())
        PAIRS = TILES // 2

        def pair_rows(dram, u):
            return dram[2 * P * u:2 * P * (u + 1), :].rearrange("(k p) d -> p k d", p=P)

        @block.sync
        def _(sp):
            def load_x(u):
                p = u % 2
                if u >= 2:
                    sp.wait_ge(xn_done, 2 * u - 2)
                    sp.wait_ge(x_stored[p], 16 * (u // 2))
                sp.dma_start(x[p][:, :, :], pair_rows(x_in, u)).then_inc(x_loaded[p], 16)

            def load_o(t):
                if t >= 2:
                    sp.wait_ge(o_tr, t - 1)
                sp.dma_start(o[t % 2][:, :], rows(o_dram, t)).then_inc(o_loaded[t % 2], 16)

            def store_x(u):
                sp.wait_ge(sum_done if proj else x_loaded[u % 2], 2 * u + 2 if proj else 16 * (u // 2 + 1))
                sp.dma_start(pair_rows(acc, u), x[u % 2][:, :, :]).then_inc(x_stored[u % 2], 16)

            def store_xn(u):
                sp.wait_ge(xn_done, 2 * u + 2)
                sp.dma_start(pair_rows(xn_dram, u), xn[u % 2][:, :, :]).then_inc(xn_stored[u % 2], 16)

            def load_weights(n):
                if n >= 2:
                    sp.wait_ge(w_lo_done, n - 1)
                sp.dma_start(w_stage[n % 2][:, :, :], w_e[n // 2, (n % 2) * 2 * P:(n % 2 + 1) * 2 * P, :]
                             .rearrange("(c p) h -> p c h", p=P)).then_inc(w_loaded[n % 2], 16)

            if proj:
                wprep["sync"](sp)
                load_o(0)
                load_o(1)
            load_x(0)
            sp.dma_start(g_raw[:, :, :], w_gate.rearrange("(c p) e -> p c e", p=P)).then_inc(g_loaded, 16)
            sp.dma_start(bg_bc[:, :], b_gate.rearrange("(a e) -> a e", a=1).to_broadcast([P, E])).then_inc(bias_loaded, 16)
            if proj:
                load_o(2)
                load_o(3)
            for u in range(PAIRS):
                load_weights(2 * u)
                if u + 1 < PAIRS:
                    load_x(u + 1)
                if u >= 1:
                    store_xn(u - 1)
                load_weights(2 * u + 1)
                if proj and 2 * u + 4 < TILES:
                    load_o(2 * u + 4)
                    load_o(2 * u + 5)
                store_x(u)
            store_xn(PAIRS - 1)
            sp.wait_ge(bias_loaded, 16)
            for par in range(2):
                sp.wait_ge(xn_stored[par], 16 * (PAIRS // 2))
                sp.wait_ge(x_stored[par], 16 * (PAIRS // 2))

        @block.gpsimd
        def _(pool):
            make_identity(nc, pool, ident, zeroed, ident_done)
            small = dict(base=0, allow_small_or_imprecise_dtypes=True)
            nc.gpsimd.iota(n_expert[:, :, :], [[0, TILES], [1, E]], channel_multiplier=0, **small).then_inc(const_done, 1)
            nc.gpsimd.iota(n_full[:, :, :], [[0, E], [P, TILES]], channel_multiplier=0, **small).then_inc(const_done, 1)
            nc.gpsimd.iota(n_col[:, :], [[1, P]], channel_multiplier=0, **small).then_inc(const_done, 1)
            nc.gpsimd.iota(n_tile[:, :], [[1, TAB]], channel_multiplier=0, **small).then_inc(const_done, 1)
            nc.gpsimd.iota(n_token_tile[:, :], [[0, 2], [1, TILES]], channel_multiplier=0, **small).then_inc(const_done, 1)
            nc.gpsimd.iota(n_part[:, :], [[0, 1]], channel_multiplier=1, **small).then_inc(const_done, 1)
            nc.gpsimd.memset(ones8[:, :], 1.0).then_inc(const_done, 1)
            nc.gpsimd.memset(ones_bf[:, :], 1.0).then_inc(const_done, 1)
            pool.wait_ge(const_done, 8)
            nc.gpsimd.affine_select(out=before[:, :], in_=ones_bf[:, :], compare_op=ALU.is_gt, fill=0.0, base=0,
                                    pattern=[[1, P]], channel_multiplier=-1).then_inc(const_done, 1)
            for n in range(TILES):
                pool.wait_ge(w_hi_done, n + 1)
                nc.gpsimd.tensor_tensor(ex.w_lo[:, 2 * n:2 * n + 2, :], w_stage[n % 2][:, :, :],
                                        ex.w_hi[:, 2 * n:2 * n + 2, :].bitcast(F32), ALU.subtract).then_inc(w_lo_done, 1)

        @block.tensor
        def _(pe):
            if proj:
                wprep["tensor"](pe)
                sem, count = wprep["done"]
                pe.wait_ge(sem, count)
            pe.wait_ge(ident_done, 1)
            pe.wait_ge(g_lo_done, 1)

            def transpose4(bank, source):
                for c in range(C):
                    last = nc.tensor.transpose(bank[:, c * P:(c + 1) * P], source[:, c * P:(c + 1) * P], ident[:, :])
                return last

            def o_transpose(t):
                pe.wait_ge(o_loaded[t % 2], 16 * (t // 2 + 1))
                at_least(pe, o_lo, t - 1)
                transpose4(o_ps[t % 2], o[t % 2][:, :]).then_inc(o_tr, 1)

            def out_proj(t):
                pe.wait_ge(o_lo, t + 1)
                at_least(pe, sum_done, t - 1)
                split_matmuls(nc, y_ps[t % 2][:, :], oT_hi[t % 2], oT_lo[t % 2], lambda c: wo_hi[:, c, :],
                              lambda c: wo_lo[:, c, :]).then_inc(y_done, 1)

            def transpose(t):
                pe.wait_ge(xn_done, t + 1)
                at_least(pe, lo_done, t - 1)
                transpose4(t_ps[t % 2], xn[t // 2 % 2][:, t % 2, :]).then_inc(tr_done, 1)

            def gate(t):
                pe.wait_ge(lo_done, t + 1)
                col = 2 * E * t
                for c in range(C):
                    k = slice(c * P, (c + 1) * P)
                    nc.tensor.matmul(g_ps[:, col:col + 2 * E], xT_hi[t % 2][:, k], g_both[:, c, :], start=(c == 0),
                                     stop=False, skip_group_check=True)
                    last = nc.tensor.matmul(g_ps[:, col:col + E], xT_lo[t % 2][:, k], g_both[:, c, 0:E], start=False,
                                            stop=(c == C - 1), skip_group_check=True)
                last.then_inc(gate_done, 1)

            if proj:
                o_transpose(0)
                o_transpose(1)
            for u in range(PAIRS + 1):
                if proj and u < PAIRS:
                    out_proj(2 * u)
                    if u + 1 < PAIRS:
                        o_transpose(2 * u + 2)
                if u >= 1:
                    transpose(2 * u - 2)
                    transpose(2 * u - 1)
                if proj and u < PAIRS:
                    out_proj(2 * u + 1)
                    if u + 1 < PAIRS:
                        o_transpose(2 * u + 3)
                if u >= 1:
                    gate(2 * u - 2)
                    gate(2 * u - 1)

            pe.wait_ge(const_done, 9)
            pe.wait_ge(picked_done, 1)
            nc.tensor.matmul(rank_ps, before[:, :], picked[:, :], start=True, stop=False, skip_group_check=True)
            for s in range(1, TILES):
                last = nc.tensor.matmul(rank_ps[:, s * E:TE], ones_bf[:, :], picked[:, 0:TE - s * E], start=False,
                                        stop=(s == TILES - 1), skip_group_check=True)
            for s in range(TILES):
                last = nc.tensor.matmul(total_ps, ones_bf[:, :], picked[:, s * E:(s + 1) * E],
                                        start=(s == 0), stop=(s == TILES - 1))
            last.then_inc(rank_done, 1)
            for n in range(2 * TILES):
                pe.wait_ge(onehot_done, n + 1)
                nc.tensor.matmul(id_ps, at_col[:, n % COL_RING, :], at_tile[:, n, :, :].rearrange("p a s -> p (a s)"),
                                 start=(n == 0), stop=(n == 2 * TILES - 1)).then_inc(ids_done, 1)

        @block.scalar
        def _(act):
            if proj:
                wprep["scalar"](act)
            act.wait_ge(g_loaded, 16)
            nc.scalar.activation(g_both[:, :, 0:E], g_raw[:, :, :], ACT.Copy).then_inc(g_hi_done, 1)

            def o_split(t):
                act.wait_ge(o_tr, t + 1)
                at_least(act, y_done, t - 1)
                nc.scalar.activation(oT_hi[t % 2][:, :], o_ps[t % 2][:, :], ACT.Copy).then_inc(o_hi, 1)

            def hi(t):
                act.wait_ge(tr_done, t + 1)
                at_least(act, gate_done, t - 1)
                nc.scalar.activation(xT_hi[t % 2][:, :], t_ps[t % 2][:, :], ACT.Copy).then_inc(hi_done, 1)

            def weights(n):
                act.wait_ge(w_loaded[n % 2], 16 * (n // 2 + 1))
                nc.scalar.activation(ex.w_hi[:, 2 * n:2 * n + 2, :], w_stage[n % 2][:, :, :], ACT.Copy).then_inc(w_hi_done, 1)

            if proj:
                o_split(0)
                o_split(1)
            for u in range(PAIRS + 1):
                if proj and u + 1 < PAIRS:
                    o_split(2 * u + 2)
                if u >= 1:
                    hi(2 * u - 2)
                    hi(2 * u - 1)
                if u < PAIRS:
                    weights(2 * u)
                if proj and u + 1 < PAIRS:
                    o_split(2 * u + 3)
                if u < PAIRS:
                    weights(2 * u + 1)

        @block.vector
        def _(dve):
            if proj:
                wprep["vector"](dve)

            def o_rest(t):
                dve.wait_ge(o_hi, t + 1)
                nc.vector.tensor_tensor(oT_lo[t % 2][:, :], o_ps[t % 2][:, :], oT_hi[t % 2][:, :].bitcast(F32),
                                        ALU.subtract).then_inc(o_lo, 1)

            def add_x(t):
                row = x[t // 2 % 2][:, t % 2, :]
                dve.wait_ge(y_done, t + 1)
                nc.vector.tensor_tensor(row, y_ps[t % 2][:, :], row, ALU.add).then_inc(sum_done, 1)

            def lo(t):
                dve.wait_ge(hi_done, t + 1)
                nc.vector.tensor_tensor(xT_lo[t % 2][:, :], t_ps[t % 2][:, :], xT_hi[t % 2][:, :].bitcast(F32),
                                        ALU.subtract).then_inc(lo_done, 1)

            dve.wait_ge(g_hi_done, 1)
            nc.vector.tensor_tensor(g_both[:, :, E:2 * E], g_raw[:, :, :], g_both[:, :, 0:E].bitcast(F32),
                                    ALU.subtract).then_inc(g_lo_done, 1)
            if proj:
                o_rest(0)
                o_rest(1)
            norm = Chain(dve, ln_chain)

            def tile_stats(t):
                if proj:
                    dve.wait_ge(sum_done, t + 1)
                norm(nc.vector.bn_stats(stats[:, t % 2, :], x[t // 2 % 2][:, t % 2, :]))

            for u in range(PAIRS + 1):
                p = u % 2
                if u < PAIRS:
                    dve.wait_ge(x_loaded[p], 16 * (u // 2 + 1))
                if proj and u < PAIRS:
                    add_x(2 * u)
                    if u + 1 < PAIRS:
                        o_rest(2 * u + 2)
                if u >= 1:
                    lo(2 * u - 2)
                    lo(2 * u - 1)
                if u == PAIRS:
                    break
                tile_stats(2 * u)
                if proj:
                    add_x(2 * u + 1)
                    if u + 1 < PAIRS:
                        o_rest(2 * u + 3)
                tile_stats(2 * u + 1)
                for k in range(2):
                    norm(nc.vector.bn_aggr(mv[:, k, :], stats[:, k, :]))
                rsqrt_steps(nc, norm, mv[:, :, 1], rstd[:, :], (tmp_a[:, :], tmp_b[:, :]))
                if u >= 2:
                    dve.wait_ge(tr_done, 2 * u - 2)
                    dve.wait_ge(xn_stored[p], 16 * (u // 2))
                for k in range(2):
                    nc.vector.tensor_scalar(xn[p][:, k, :], x[p][:, k, :], mv[:, k, 0:1], rstd[:, k:k + 1],
                                            ALU.subtract, ALU.mult).then_inc(xn_done, 1)

            chain = Chain(dve, chain_sem)
            dve.wait_ge(const_done, 9)
            dve.wait_ge(bias_loaded, 16)
            dve.wait_ge(gate_done, TILES)
            three = [P, TILES, E]
            halves = g_ps[:, 0:2 * TE].rearrange("p (t k e) -> p t e k", k=2, e=E)
            chain(nc.vector.tensor_reduce(logits[:, :, :], halves, X_AXIS, ALU.add))
            chain(nc.vector.tensor_tensor(logits[:, :, :], logits[:, :, :],
                                          bg_bc[:, :].rearrange("p (a e) -> p a e", a=1).to_broadcast(three), ALU.add))
            for k, source in enumerate((logits, rest)):
                chain(nc.vector.tensor_reduce(best[:, :, 0], source[:, :, :], X_AXIS, ALU.max))
                chain(nc.vector.tensor_tensor(eq[:, :, :], source[:, :, :], best[:, :, :].to_broadcast(three), ALU.is_equal))
                chain(nc.vector.scalar_tensor_tensor(val[:, :, :], eq[:, :, :], -100.0, n_expert[:, :, :], ALU.mult, ALU.add))
                chain(nc.vector.tensor_reduce(low[:, :, 0], val[:, :, :], X_AXIS, ALU.min))
                chain(nc.vector.tensor_tensor(pick[k][:, :, :], val[:, :, :], low[:, :, :].to_broadcast(three), ALU.is_equal))
                if k == 0:
                    chain(nc.vector.scalar_tensor_tensor(rest[:, :, :], pick[0][:, :, :], NEG, logits[:, :, :], ALU.mult, ALU.add))
            flat = "p t e -> p (t e)"
            nc.vector.tensor_tensor(picked[:, :], pick[0][:, :, :].rearrange(flat), pick[1][:, :, :].rearrange(flat),
                                    ALU.add).then_inc(picked_done, 1)
            dve.wait_ge(rank_done, 1)
            chain(nc.vector.tensor_tensor(over[:, :, :], total_ps.rearrange("p (e a) -> p e a", a=1).to_broadcast([P, E, TILES]),
                                          n_full[:, :, :], ALU.is_gt))
            chain(nc.vector.tensor_reduce(n_tiles[:, :], over[:, :, :], X_AXIS, ALU.add))
            chain(nc.vector.tensor_tensor_scan(ends[:, :], ones8[:, :], n_tiles[:, :], 0.0, ALU.mult, ALU.add))
            chain(nc.vector.tensor_tensor(begins[:, :], ends[:, :], n_tiles[:, :], ALU.subtract))
            begin_all = begins[:, :].rearrange("p (a e) -> p a e", a=1).to_broadcast(three)
            chain(nc.vector.scalar_tensor_tensor(slot_e[:, :, :], begin_all, float(P),
                                                 rank_ps.rearrange("p (t e) -> p t e", e=E), ALU.mult, ALU.add))
            for k in range(2):
                chain(nc.vector.tensor_tensor(slot_m[:, :, :], pick[k][:, :, :], slot_e[:, :, :], ALU.mult))
                chain(nc.vector.tensor_reduce(slot[:, k, :], slot_m[:, :, :], X_AXIS, ALU.add))
            chain(nc.vector.tensor_copy(slot_i[:, :], slot[:, :, :].rearrange("p k t -> p (k t)")))
            chain(nc.vector.tensor_scalar(slot_hi_i[:, :], slot_i[:, :], 7, None, ALU.arith_shift_right))
            chain(nc.vector.tensor_scalar(slot_lo_i[:, :], slot_i[:, :], P - 1, None, ALU.bitwise_and))
            chain(nc.vector.tensor_copy(slot_hi[:, :, 0], slot_hi_i[:, :]))
            chain(nc.vector.tensor_copy(slot_lo[:, :], slot_lo_i[:, :]))
            every = [P, 2 * TILES, TAB]
            chain(nc.vector.tensor_tensor(at_tile[:, :, 0, :], slot_hi[:, :, :].to_broadcast(every),
                                          n_tile[:, :].rearrange("p (a s) -> p a s", a=1).to_broadcast(every), ALU.is_equal))
            chain(nc.vector.tensor_scalar(at_tile[:, :, 1, :], at_tile[:, :, 0, :], n_part[:, :], None, ALU.mult))
            chain(nc.vector.tensor_tensor(at_tile[:, :, 2, :], at_tile[:, :, 0, :],
                                          n_token_tile[:, :].rearrange("p (n a) -> p n a", a=1).to_broadcast(every), ALU.mult))
            for n in range(2 * TILES):
                if n >= COL_RING:
                    dve.wait_ge(ids_done, n - COL_RING + 1)
                nc.vector.tensor_scalar(at_col[:, n % COL_RING, :], n_col[:, :], slot_lo[:, n:n + 1], None,
                                        ALU.is_equal).then_inc(onehot_done, 1)
            chain(nc.vector.tensor_tensor(past[:, :, :], ends[0:1, :].rearrange("p (a e) -> p a e", a=1).to_broadcast([1, TAB, E]),
                                          n_tile[0:1, :].rearrange("p (s a) -> p s a", a=1).to_broadcast([1, TAB, E]), ALU.is_le))
            chain(nc.vector.tensor_reduce(exp_f[:, :, 0], past[:, :, :], X_AXIS, ALU.add))
            chain(nc.vector.tensor_scalar(ex.expert_of[:, :], exp_f[:, :, 0], float(E - 1), None, ALU.min))
            dve.wait_ge(ids_done, 2 * TILES)
            chain(nc.vector.tensor_copy(found[:, :, :], id_ps.rearrange("p (a s) -> p a s", a=3)))
            chain(nc.vector.scalar_tensor_tensor(found[:, 1, :], found[:, 2, :], float(P), found[:, 1, :], ALU.mult, ALU.add))
            chain(nc.vector.tensor_copy(ex.token_of[:, :], found[:, 1, :]))
            chain(nc.vector.tensor_scalar(empty[:, :], found[:, 0, :], -1.0, 1.0, ALU.mult, ALU.add))
            chain(nc.vector.tensor_scalar(found[:, 2, :], empty[:, :], n_part[:, :], None, ALU.mult))
            chain(nc.vector.scalar_tensor_tensor(found[:, 1, :], empty[:, :], float(TOKENS), found[:, 1, :], ALU.mult, ALU.add))
            chain(nc.vector.tensor_tensor(ex.row_of[:, :], found[:, 1, :], found[:, 2, :], ALU.add))


def expert_block(nc, prefix, ex, xn_dram, acc, b_e):
    with ExitStack() as ctx:
        m = Memory(nc, ctx, prefix)
        RING = 4
        ident = m.sb("ident", [P, P])
        bias = m.sb("bias", [P, E * D])
        xg = [m.sb(f"xg{i}", [P, D]) for i in range(RING)]
        xT_hi = [m.sb(f"xT_hi{i}", [P, C * P], F32R) for i in range(2)]
        xT_lo = [m.sb(f"xT_lo{i}", [P, C * P], F32R) for i in range(2)]
        z = [m.sb(f"z{i}", [P, D]) for i in range(2)]
        y = [m.sb(f"y{i}", [P, D]) for i in range(RING)]
        t_ps = [m.ps(f"t_ps{i}") for i in range(2)]
        z_ps = [m.ps(f"z_ps{i}") for i in range(2)]
        zeroed, ident_done = m.sem("zeroed"), m.sem("ident_done")
        gathered = [m.sem(f"gathered{i}") for i in range(RING)]
        added = m.sem("added")
        tr_done, hi_done, lo_done, z_done, zb_done, y_done = (
            m.sem(n) for n in ("tr_done", "hi_done", "lo_done", "z_done", "zb_done", "y_done"))
        bias_loaded = m.sem("bias_loaded")
        block = ctx.enter_context(nc.Block())
        N = SLOT_TILES
        FIRST = 4

        @block.gpsimd
        def _(pool):
            def gather(s):
                if s >= RING:
                    pool.wait_ge(tr_done, s - RING + 1)
                nc.gpsimd.indirect_dma_start(out=xg[s % RING][:, :], out_offset=None, in_=xn_dram[:, :],
                                             in_offset=bass.IndirectOffsetOnAxis(ap=ex.token_of[:, s:s + 1], axis=0)
                                             ).then_inc(gathered[s % RING], 16)
            gather(0)
            make_identity(nc, pool, ident, zeroed, ident_done)
            gather(1)
            gather(2)
            for s in range(N):
                if s + 3 < N:
                    gather(s + 3)
                pool.wait_ge(y_done, s + 1)
                if s >= 1:
                    pool.wait_ge(added, 16 * s)
                nc.gpsimd.indirect_dma_start(out=acc[:, :], out_offset=bass.IndirectOffsetOnAxis(ap=ex.row_of[:, s:s + 1], axis=0),
                                             in_=y[s % RING][:, :], in_offset=None, compute_op=ALU.add,
                                             bounds_check=TOKENS - 1, oob_is_err=False).then_inc(added, 16)
            pool.wait_ge(added, 16 * N)

        @block.sync
        def _(sp):
            sp.wait_ge(gathered[1], 16)
            sp.dma_start(bias[:, :], b_e.rearrange("(a e) h -> a (e h)", a=1).to_broadcast([P, E * D])).then_inc(bias_loaded, 16)
            sp.wait_ge(bias_loaded, 16)

        @block.tensor
        def _(pe):
            pe.wait_ge(ident_done, 1)

            def transpose(s, r):
                pe.wait_ge(gathered[r], 16 * (s // RING + 1))
                at_least(pe, lo_done, s - 1)
                for c in range(C):
                    last = nc.tensor.transpose(t_ps[r % 2][:, c * P:(c + 1) * P], xg[r][:, c * P:(c + 1) * P], ident[:, :])
                last.then_inc(tr_done, 1)
            transpose(0, 0)

            def step(s, r):
                if not known(s, N - 1):
                    transpose(s + 1, (r + 1) % RING)
                expert = pe.value_load(ex.expert_of[0:1, bass.ds(s, 1)], min_val=0, max_val=E - 1)
                pe.wait_ge(lo_done, s + 1)
                at_least(pe, zb_done, s - 1)
                split_matmuls(nc, z_ps[r % 2][:, :], xT_hi[r % 2], xT_lo[r % 2],
                              lambda c: ex.w_hi[:, bass.ds(expert * C + c, 1), :].rearrange("p a n -> p (a n)"),
                              lambda c: ex.w_lo[:, bass.ds(expert * C + c, 1), :].rearrange("p a n -> p (a n)")).then_inc(z_done, 1)
            ring_loop(pe, step, N, RING, FIRST)

        @block.scalar
        def _(act):
            def hi(s, r):
                act.wait_ge(tr_done, s + 1)
                at_least(act, z_done, s - 1)
                nc.scalar.activation(xT_hi[r % 2][:, :], t_ps[r % 2][:, :], ACT.Copy).then_inc(hi_done, 1)
            hi(0, 0)

            def step(s, r):
                if not known(s, N - 1):
                    hi(s + 1, (r + 1) % RING)
                act.wait_ge(zb_done, s + 1)
                at_least(act, added, 16 * (s - RING + 1))
                nc.scalar.activation(y[r][:, :], z[r % 2][:, :], ACT.Relu, scale=0.25).then_inc(y_done, 1)
            ring_loop(act, step, N, RING, FIRST)

        @block.vector
        def _(dve):
            def lo(s, r):
                dve.wait_ge(hi_done, s + 1)
                nc.vector.tensor_tensor(xT_lo[r % 2][:, :], t_ps[r % 2][:, :], xT_hi[r % 2][:, :].bitcast(F32),
                                        ALU.subtract).then_inc(lo_done, 1)
            lo(0, 0)
            dve.wait_ge(bias_loaded, 16)

            def step(s, r):
                if not known(s, N - 1):
                    lo(s + 1, (r + 1) % RING)
                expert = dve.value_load(ex.expert_of[0:1, bass.ds(s, 1)], min_val=0, max_val=E - 1)
                dve.wait_ge(z_done, s + 1)
                at_least(dve, y_done, s - 1)
                nc.vector.tensor_tensor(z[r % 2][:, :], z_ps[r % 2][:, :], bias[:, bass.ds(expert * D, D)],
                                        ALU.add).then_inc(zb_done, 1)
            ring_loop(dve, step, N, RING, FIRST)


def macaron(nc, x, w_qkv, q_w, q_b, k_w, k_b, w_out, w_gate, b_gate, w_e, b_e, bias_const, out):
    def scratch(name, shape):
        return nc.dram_tensor(name, shape, F32, kind="Internal").ap()

    acc1 = scratch("acc1", [TOKENS, D])
    acc2 = out.rearrange("b s d -> (b s) d")
    xn = scratch("xn", [TOKENS, D])
    q_dram, k_dram = scratch("q_parts", [NG * P, SEQ]), scratch("k_parts", [NG * P, SEQ])
    v_dram, o_dram = scratch("v_vals", [TOKENS, H * VW]), scratch("o_vals", [TOKENS, D])
    bias_dram = scratch("bias_rows", [2, BIAS_ROWS + MAX_ROWS, H, SEQ])
    flat = x.rearrange("b s d -> (b s) d")
    Memory.sems = []
    with ExitStack() as ctx:
        ex = Experts(nc, ctx, "ex1")
        route_block(nc, "route1", ex, flat, xn, acc1, w_gate, b_gate, w_e)
        expert_block(nc, "exp1", ex, xn, acc1, b_e)
    clear_semaphores(nc)
    qkv_block(nc, acc1, w_qkv, (q_w, q_b, k_w, k_b), bias_const, q_dram, k_dram, v_dram, bias_dram)
    attention_block(nc, q_dram, k_dram, v_dram, bias_dram, o_dram)
    with ExitStack() as ctx:
        ex = Experts(nc, ctx, "ex2")
        route_block(nc, "route2", ex, acc1, xn, acc2, w_gate, b_gate, w_e, o_dram, w_out)
        expert_block(nc, "exp2", ex, xn, acc2, b_e)


def bias_rows():
    import numpy as np
    step = np.arange(1, H + 1, dtype=np.float32) * (8.0 / H)
    slope = (1.0 / np.power(2.0, step)).astype(np.float32)
    hi = (slope.view(np.uint32) & np.uint32(0xFFFFF000)).view(np.float32)
    lo = slope - hi
    pos = np.arange(SEQ, dtype=np.float32)
    r = np.zeros((2, BIAS_ROWS + MAX_ROWS, H, SEQ), np.float32)
    r[0, 0], r[0, 2] = hi[:, None], lo[:, None]
    r[0, 1] = r[0, 3] = pos[None, :]
    r[1, 0] = r[1, 2] = pos[None, :]
    r[1, 1], r[1, 3] = -hi[:, None], -lo[:, None]
    r[1, 4:] = 1.0
    return r


_INS = ['L0_attn_hidden_states', 'L0_attn_Wqkv', 'L0_attn_q_ln_w', 'L0_attn_q_ln_b', 'L0_attn_k_ln_w',
        'L0_attn_k_ln_b', 'L0_attn_Wout', 'L0_ffn_W_gate', 'L0_ffn_b_gate', 'L0_ffn_W_e', 'L0_ffn_b_e']


def kernel(**inputs):
    import numpy as _np
    import concourse.bacc as _bacc
    from concourse import mybir as _mybir
    from concourse.bass_utils import run_bass_kernel_spmd as _run

    nc = _bacc.Bacc("TRN2", target_bir_lowering=False, num_devices=1)
    arrays, args = {}, []
    for name in _INS:
        a = _np.ascontiguousarray(inputs[name])
        arrays[f"in_{name}"] = a
        args.append(nc.dram_tensor(f"in_{name}", a.shape, _mybir.dt.from_np(a.dtype), kind="ExternalInput").ap())
    a = bias_rows()
    arrays["in_bias_rows"] = a
    args.append(nc.dram_tensor("in_bias_rows", a.shape, _mybir.dt.from_np(a.dtype), kind="ExternalInput").ap())
    args.append(nc.dram_tensor("out_0", (B, SEQ, D), F32, kind="ExternalOutput").ap())
    macaron(nc, *args)
    r = _run(nc, [arrays], core_ids=[0])
    return r.results[0]["out_0"]
```
